# Optimizing a Trainium2 kernel written in Bass

```python
import numpy as np
import jax
import jax.numpy as jnp

def _softmax(x, axis=-1):
    return jax.nn.softmax(x, axis=axis)

def _gelu(x):
    return jax.nn.gelu(x, approximate=True)

def _silu(x):
    return jax.nn.silu(x)

def _sigmoid(x):
    return jax.nn.sigmoid(x)

def _layernorm(x, axis=-1, eps=1e-05):
    m = jnp.mean(x, axis=axis, keepdims=True)
    v = jnp.var(x, axis=axis, keepdims=True)
    return (x - m) / jnp.sqrt(v + eps)

def _scatter_add(tgt, idx, src, axis=0):
    return tgt.at[idx].add(src)

def _segment_sum(src, seg, n):
    return jax.ops.segment_sum(src, seg, n)
kernel_name = 'mk_decoder_preln_d2_seqx_r4_b572dd'

def setup_inputs(seed: int=0):
    np.random.seed(seed)
    _w = jnp.asarray

    def _rec_inputs():
        import jax
        import jax.numpy as jnp
        _rk = jax.random.key(seed)
        x = -0.0003929 + 0.9999 * jax.random.normal(jax.random.fold_in(_rk, 1), (8, 512, 256), jnp.float32)
        _lenS = 512 - jax.random.randint(jax.random.fold_in(_rk, 7), (8,), 0, max(1, 512 // 4) + 1, jnp.int32)
        _lenS2 = 1601 - jax.random.randint(jax.random.fold_in(_rk, 8), (8,), 0, max(1, 1601 // 4) + 1, jnp.int32)
        _ctx_1024P = jax.random.normal(jax.random.fold_in(_rk, 11), (8, 16, 256), jnp.float32)
        _ctx_1024c = jax.random.dirichlet(jax.random.fold_in(_rk, 511), 0.3 * jnp.ones((16,), jnp.float32), (8, 1601))
        _ctx_1024t = jnp.einsum('bsk,bkd->bsd', _ctx_1024c, _ctx_1024P)
        _ctx_1024t = _ctx_1024t * jax.lax.rsqrt(jnp.mean(jnp.square(_ctx_1024t)) + 1e-12) * 0.953939
        ctx_1024 = 0.00208318 + 0.999174 * (_ctx_1024t + 0.3 * jax.random.normal(jax.random.fold_in(_rk, 611), (8, 1601, 256), jnp.float32))
        _validS = jnp.arange(512)[None, :] < _lenS[:, None]
        _validS2 = jnp.arange(1601)[None, :] < _lenS2[:, None]
        _causal = jnp.tril(jnp.ones((512, 512), dtype=bool))
        mask_BxSxS2_ff0 = jnp.where(jnp.ones((8, 512, 1601), dtype=bool), 0.0, -1000000000.0).astype(jnp.float32)
        return (x, ctx_1024, mask_BxSxS2_ff0)
    x, ctx_1024, mask_BxSxS2_ff0 = _rec_inputs()

    def _L0_attn_setup():
        import jax, jax.numpy as jnp
        import numpy as np
        DIM = 256
        N_HEADS = 16
        HEAD_DIM = DIM // N_HEADS
        D_LATENT = 64
        B, T = (1, 1024)
        key = jax.random.key(seed)
        ks = jax.random.split(key, 6)
        s = 0.02
        return {'x': jax.random.normal(ks[0], (B, T, DIM), dtype=jnp.float32), 'W_DKV': jax.random.normal(ks[1], (DIM, D_LATENT), dtype=jnp.float32) * s, 'W_UK': jax.random.normal(ks[2], (D_LATENT, DIM), dtype=jnp.float32) * s, 'W_UV': jax.random.normal(ks[3], (D_LATENT, DIM), dtype=jnp.float32) * s, 'W_UQ': jax.random.normal(ks[4], (DIM, DIM), dtype=jnp.float32) * s, 'W_O': jax.random.normal(ks[5], (DIM, DIM), dtype=jnp.float32) * s}
    _L0_attn_all = _L0_attn_setup()
    _L0_attn_in = {k: v for k, v in _L0_attn_all.items() if k in ('W_DKV', 'W_UK', 'W_UV', 'W_UQ', 'W_O')}
    del _L0_attn_all

    def _L0_xattn_setup():
        import jax, jax.numpy as jnp
        import numpy as np
        NUM_HEADS = 16
        DIM = 256
        key = jax.random.key(seed)
        ks = jax.random.split(key, 12)
        B, N, T, C = (4, 1024, 77, DIM)
        s = 1.0 / np.sqrt(C)
        return {'hidden_states': jax.random.normal(ks[0], (B, N, C), jnp.float32), 'encoder_hidden_states': jax.random.normal(ks[1], (B, T, C), jnp.float32), 'attention_mask': jnp.zeros((B, N, T), jnp.float32), 'Wq': jax.random.normal(ks[2], (C, C), jnp.float32) * s, 'bq': jnp.zeros((C,), jnp.float32), 'Wk': jax.random.normal(ks[3], (C, C), jnp.float32) * s, 'bk': jnp.zeros((C,), jnp.float32), 'Wv': jax.random.normal(ks[4], (C, C), jnp.float32) * s, 'bv': jnp.zeros((C,), jnp.float32), 'Wo': jax.random.normal(ks[5], (C, C), jnp.float32) * s, 'bo': jnp.zeros((C,), jnp.float32)}
    _L0_xattn_all = _L0_xattn_setup()
    _L0_xattn_in = {k: v for k, v in _L0_xattn_all.items() if k in ('Wq', 'bq', 'Wk', 'bk', 'Wv', 'bv', 'Wo', 'bo')}
    del _L0_xattn_all

    def _L0_ffn_setup():
        import jax, jax.numpy as jnp
        import numpy as np
        DIM = 256

        def _reference_tuple_inner(x, W_r, W_k, W_v, mu_r, mu_k):
            B, T, C = x.shape
            x_prev = jnp.concatenate([jnp.zeros((B, 1, C), x.dtype), x[:, :-1, :]], axis=1)
            xr = mu_r * x + (1.0 - mu_r) * x_prev
            xk = mu_k * x + (1.0 - mu_k) * x_prev
            r = jax.nn.sigmoid(jnp.einsum('btc,dc->btd', xr, W_r))
            k = jnp.einsum('btc,dc->btd', xk, W_k)
            k_act = jnp.square(jax.nn.relu(k))
            out = r * jnp.einsum('btc,dc->btd', k_act, W_v)
            new_state = x[:, -1, :]
            return (out, new_state)
        key = jax.random.key(seed)
        ks = jax.random.split(key, 6)
        B, T, C = (8, 512, DIM)
        x = jax.random.normal(ks[0], (B, T, C), dtype=jnp.float32)
        s = 1.0 / np.sqrt(C)
        W_r = jax.random.uniform(ks[1], (C, C), jnp.float32, -s, s)
        W_k = jax.random.uniform(ks[2], (C, C), jnp.float32, -s, s)
        W_v = jax.random.uniform(ks[3], (C, C), jnp.float32, -s, s)
        mu_r = jax.random.uniform(ks[4], (C,), jnp.float32)
        mu_k = jax.random.uniform(ks[5], (C,), jnp.float32)
        return {'x': x, 'W_r': W_r, 'W_k': W_k, 'W_v': W_v, 'mu_r': mu_r, 'mu_k': mu_k}
    _L0_ffn_all = _L0_ffn_setup()
    _L0_ffn_in = {k: v for k, v in _L0_ffn_all.items() if k in ('W_r', 'W_k', 'W_v', 'mu_r', 'mu_k')}
    del _L0_ffn_all

    def _L1_attn_setup():
        import math
        import jax, jax.numpy as jnp
        import numpy as np
        B, T, C = (2, 512, 256)
        H, N1, N2, N3 = (16, 6, 4, 6)
        HD = C // H

        def _rotary(T_, hd, dtype):
            inv_freq = 1.0 / 10000.0 ** (jnp.arange(0, hd, 2, dtype=jnp.float32) / hd)
            freqs = jnp.outer(jnp.arange(T_, dtype=jnp.float32), inv_freq)
            return (jnp.cos(freqs)[None, :, None, :].astype(dtype), jnp.sin(freqs)[None, :, None, :].astype(dtype))

        def _apply_rot(x, cos, sin):
            x1, x2 = (x[..., :x.shape[-1] // 2], x[..., x.shape[-1] // 2:])
            return jnp.concatenate([x1 * cos + x2 * sin, -x1 * sin + x2 * cos], axis=-1).astype(x.dtype)

        def _causal_bias(L, S, dtype):
            mask = jnp.triu(jnp.ones((L, S), bool), k=1)
            return jnp.where(mask, jnp.asarray(-jnp.inf, dtype), jnp.asarray(0.0, dtype))

        def _sdpa(q, k, v, scale):
            scores = jnp.einsum('bhtd,bhsd->bhts', q, k) * scale + _causal_bias(q.shape[-2], k.shape[-2], q.dtype)
            return jnp.einsum('bhts,bhsd->bhtd', jax.nn.softmax(scores, axis=-1), v)

        def _hyp_attn(q, k, v, curv):
            eps = 1e-06
            tq = jnp.sqrt(1.0 / curv + jnp.sum(q * q, axis=-1, keepdims=True))
            tk = jnp.sqrt(1.0 / curv + jnp.sum(k * k, axis=-1, keepdims=True))
            inner = jnp.einsum('bhtd,bhsd->bhts', q, k) - tq * jnp.swapaxes(tk, -1, -2)
            arg = jnp.maximum(-curv * inner, 1.0 + 1e-07)
            dis = jnp.sqrt(1.0 / curv) * jnp.arccosh(arg)
            scores = 1.0 / (eps + dis) + _causal_bias(q.shape[-2], k.shape[-2], q.dtype)
            return jnp.einsum('bhts,bhsd->bhtd', jax.nn.softmax(scores, axis=-1), v)
        key = jax.random.key(seed)
        k1, k2, k3 = jax.random.split(key, 3)
        return {'x': jax.random.normal(k1, (B, T, C), jnp.float32), 'qkv_w': jax.random.normal(k2, (3 * C, C), jnp.float32) * C ** (-0.5), 'proj_w': jax.random.normal(k3, (C, C), jnp.float32) * C ** (-0.5), 'proj_b': jnp.zeros((C,), jnp.float32), 'curvature': jnp.ones((1, N2, 1, 1), jnp.float32)}
    _L1_attn_all = _L1_attn_setup()
    _L1_attn_in = {k: v for k, v in _L1_attn_all.items() if k in ('qkv_w', 'proj_w', 'proj_b', 'curvature')}
    del _L1_attn_all

    def _L1_xattn_setup():
        import jax, jax.numpy as jnp
        import numpy as np
        HEAD = 16
        EMB = 256
        B, S = (8, 1024)

        def _proj_heads(x, W, b, H, d):
            Bx, Sx, _ = x.shape
            y = x @ W.T + b
            return y.reshape(Bx, Sx, H, d).transpose(0, 2, 1, 3)
        key = jax.random.key(seed)
        ks = jax.random.split(key, 11)
        scale = 1.0 / np.sqrt(EMB).astype(np.float32)
        inp = {'query': jax.random.normal(ks[0], (B, S, EMB), jnp.float32), 'key': jax.random.normal(ks[1], (B, S, EMB), jnp.float32), 'value': jax.random.normal(ks[2], (B, S, EMB), jnp.float32), 'Wq': jax.random.normal(ks[3], (EMB, EMB), jnp.float32) * scale, 'bq': jnp.zeros((EMB,), jnp.float32), 'Wk': jax.random.normal(ks[4], (EMB, EMB), jnp.float32) * scale, 'bk': jnp.zeros((EMB,), jnp.float32), 'Wv': jax.random.normal(ks[5], (EMB, EMB), jnp.float32) * scale, 'bv': jnp.zeros((EMB,), jnp.float32), 'Wo': jax.random.normal(ks[6], (EMB, EMB), jnp.float32) * scale, 'bo': jnp.zeros((EMB,), jnp.float32)}
        return inp
    _L1_xattn_all = _L1_xattn_setup()
    _L1_xattn_in = {k: v for k, v in _L1_xattn_all.items() if k in ('Wq', 'bq', 'Wk', 'bk', 'Wv', 'bv', 'Wo', 'bo')}
    del _L1_xattn_all

    def _L1_ffn_setup():
        import jax, jax.numpy as jnp
        import numpy as np
        H = 256
        NH = 16
        HD = H // NH
        HH = HD // 2
        L = H // 4
        I = int(H * 1.0)
        ER = 7
        TOPK = 2
        BASE = 10000.0
        EPS = 1e-05

        def rmsnorm(x, w):
            norm = jnp.sqrt(jnp.mean(x * x, axis=-1, keepdims=True)) + EPS
            return x / norm * w

        def rope_tables(seq_len):
            inv_freq = 1.0 / BASE ** (jnp.arange(0, HH, 2, dtype=jnp.float32) / HH)
            t = jnp.arange(seq_len, dtype=jnp.float32)
            freqs = jnp.einsum('i,j->ij', t, inv_freq)
            emb = jnp.concatenate([freqs, freqs], axis=-1)
            cos = jnp.cos(emb)[None, :, None, :]
            sin = jnp.sin(emb)[None, :, None, :]
            return (cos, sin)

        def rotate_half(x):
            x1, x2 = jnp.split(x, 2, axis=-1)
            return jnp.concatenate([-x2, x1], axis=-1)

        def silu(x):
            return x * jax.nn.sigmoid(x)

        def mla(xn, W_kvd, W_qd, W_ku, W_qu, W_vu, W_ropeq, W_ropek, W_o):
            B, S, _ = xn.shape
            kv_lat = xn @ W_kvd
            q_lat = xn @ W_qd
            k = (kv_lat @ W_ku).reshape(B, S, NH, HH)
            q = (q_lat @ W_qu).reshape(B, S, NH, HH)
            v = (kv_lat @ W_vu).reshape(B, S, NH, HD)
            q_rope = (q_lat @ W_ropeq).reshape(B, S, NH, HH)
            k_rope = (xn @ W_ropek).reshape(B, S, NH, HH)
            cos, sin = rope_tables(S)
            k_rope = k_rope * cos + rotate_half(k_rope) * sin
            q_rope = q_rope * cos + rotate_half(q_rope) * sin
            kk = jnp.concatenate([k, k_rope], axis=-1)
            qq = jnp.concatenate([q, q_rope], axis=-1)
            scale = 1.0 / jnp.sqrt(jnp.float32(HD))
            scores = jnp.einsum('bqhd,bkhd->bhqk', qq, kk) * scale
            causal = jnp.tril(jnp.ones((S, S), dtype=bool))
            scores = jnp.where(causal[None, None], scores, jnp.finfo(scores.dtype).min)
            probs = jax.nn.softmax(scores, axis=-1)
            y = jnp.einsum('bhqk,bkhd->bqhd', probs, v).reshape(B, S, H)
            return y @ W_o

        def moe(xn, Wg_s, Wu_s, Wd_s, Wg_r, Wu_r, Wd_r, W_router, routing_bias):
            B, S, _ = xn.shape
            xt = xn.reshape(B * S, H)
            shared = silu(xt @ Wg_s) * (xt @ Wu_s) @ Wd_s
            logits = xt @ W_router + routing_bias
            probs = jax.nn.sigmoid(logits)
            scores, idx = jax.lax.top_k(probs, TOPK)
            scores = scores / jnp.sum(scores, axis=-1, keepdims=True)
            wts = jnp.sum(jax.nn.one_hot(idx, ER, dtype=xt.dtype) * scores[..., None], axis=1)
            g = jnp.einsum('th,ehi->tei', xt, Wg_r)
            u = jnp.einsum('th,ehi->tei', xt, Wu_r)
            hmid = silu(g) * u
            combined = jnp.einsum('tei,eih,te->th', hmid, Wd_r, wts)
            return (shared + combined).reshape(B, S, H)
        key = jax.random.key(seed)
        ks = jax.random.split(key, 20)
        s = 0.02
        r = lambda k, shp: jax.random.normal(k, shp, dtype=jnp.float32) * s
        return {'x': jax.random.normal(ks[0], (4, 256, H), dtype=jnp.float32), 'w_ln1': jnp.ones((H,), jnp.float32), 'w_ln2': jnp.ones((H,), jnp.float32), 'W_kvd': r(ks[1], (H, L)), 'W_qd': r(ks[2], (H, L)), 'W_ku': r(ks[3], (L, NH * HH)), 'W_qu': r(ks[4], (L, NH * HH)), 'W_vu': r(ks[5], (L, H)), 'W_ropeq': r(ks[6], (L, H // 2)), 'W_ropek': r(ks[7], (H, H // 2)), 'W_o': r(ks[8], (H, H)), 'Wg_s': r(ks[9], (H, I)), 'Wu_s': r(ks[10], (H, I)), 'Wd_s': r(ks[11], (I, H)), 'Wg_r': r(ks[12], (ER, H, I)), 'Wu_r': r(ks[13], (ER, H, I)), 'Wd_r': r(ks[14], (ER, I, H)), 'W_router': r(ks[15], (H, ER)), 'routing_bias': jnp.zeros((ER,), jnp.float32)}
    _L1_ffn_all = _L1_ffn_setup()
    _L1_ffn_in = {k: v for k, v in _L1_ffn_all.items() if k in ('w_ln1', 'w_ln2', 'W_kvd', 'W_qd', 'W_ku', 'W_qu', 'W_vu', 'W_ropeq', 'W_ropek', 'W_o', 'Wg_s', 'Wu_s', 'Wd_s', 'Wg_r', 'Wu_r', 'Wd_r', 'W_router', 'routing_bias')}
    del _L1_ffn_all
    return {'x': x, 'ctx_1024': ctx_1024, 'mask_BxSxS2_ff0': mask_BxSxS2_ff0, 'L0_attn_W_DKV': _L0_attn_in['W_DKV'], 'L0_attn_W_UK': _L0_attn_in['W_UK'], 'L0_attn_W_UV': _L0_attn_in['W_UV'], 'L0_attn_W_UQ': _L0_attn_in['W_UQ'], 'L0_attn_W_O': _L0_attn_in['W_O'], 'L0_xattn_Wq': _L0_xattn_in['Wq'], 'L0_xattn_bq': _L0_xattn_in['bq'], 'L0_xattn_Wk': _L0_xattn_in['Wk'], 'L0_xattn_bk': _L0_xattn_in['bk'], 'L0_xattn_Wv': _L0_xattn_in['Wv'], 'L0_xattn_bv': _L0_xattn_in['bv'], 'L0_xattn_Wo': _L0_xattn_in['Wo'], 'L0_xattn_bo': _L0_xattn_in['bo'], 'L0_ffn_W_r': _L0_ffn_in['W_r'], 'L0_ffn_W_k': _L0_ffn_in['W_k'], 'L0_ffn_W_v': _L0_ffn_in['W_v'], 'L0_ffn_mu_r': _L0_ffn_in['mu_r'], 'L0_ffn_mu_k': _L0_ffn_in['mu_k'], 'L1_attn_qkv_w': _L1_attn_in['qkv_w'], 'L1_attn_proj_w': _L1_attn_in['proj_w'], 'L1_attn_proj_b': _L1_attn_in['proj_b'], 'L1_attn_curvature': _L1_attn_in['curvature'], 'L1_xattn_Wq': _L1_xattn_in['Wq'], 'L1_xattn_bq': _L1_xattn_in['bq'], 'L1_xattn_Wk': _L1_xattn_in['Wk'], 'L1_xattn_bk': _L1_xattn_in['bk'], 'L1_xattn_Wv': _L1_xattn_in['Wv'], 'L1_xattn_bv': _L1_xattn_in['bv'], 'L1_xattn_Wo': _L1_xattn_in['Wo'], 'L1_xattn_bo': _L1_xattn_in['bo'], 'L1_ffn_w_ln1': _L1_ffn_in['w_ln1'], 'L1_ffn_w_ln2': _L1_ffn_in['w_ln2'], 'L1_ffn_W_kvd': _L1_ffn_in['W_kvd'], 'L1_ffn_W_qd': _L1_ffn_in['W_qd'], 'L1_ffn_W_ku': _L1_ffn_in['W_ku'], 'L1_ffn_W_qu': _L1_ffn_in['W_qu'], 'L1_ffn_W_vu': _L1_ffn_in['W_vu'], 'L1_ffn_W_ropeq': _L1_ffn_in['W_ropeq'], 'L1_ffn_W_ropek': _L1_ffn_in['W_ropek'], 'L1_ffn_W_o': _L1_ffn_in['W_o'], 'L1_ffn_Wg_s': _L1_ffn_in['Wg_s'], 'L1_ffn_Wu_s': _L1_ffn_in['Wu_s'], 'L1_ffn_Wd_s': _L1_ffn_in['Wd_s'], 'L1_ffn_Wg_r': _L1_ffn_in['Wg_r'], 'L1_ffn_Wu_r': _L1_ffn_in['Wu_r'], 'L1_ffn_Wd_r': _L1_ffn_in['Wd_r'], 'L1_ffn_W_router': _L1_ffn_in['W_router'], 'L1_ffn_routing_bias': _L1_ffn_in['routing_bias']}

def reference(x, ctx_1024, mask_BxSxS2_ff0, L0_attn_W_DKV, L0_attn_W_UK, L0_attn_W_UV, L0_attn_W_UQ, L0_attn_W_O, L0_xattn_Wq, L0_xattn_bq, L0_xattn_Wk, L0_xattn_bk, L0_xattn_Wv, L0_xattn_bv, L0_xattn_Wo, L0_xattn_bo, L0_ffn_W_r, L0_ffn_W_k, L0_ffn_W_v, L0_ffn_mu_r, L0_ffn_mu_k, L1_attn_qkv_w, L1_attn_proj_w, L1_attn_proj_b, L1_attn_curvature, L1_xattn_Wq, L1_xattn_bq, L1_xattn_Wk, L1_xattn_bk, L1_xattn_Wv, L1_xattn_bv, L1_xattn_Wo, L1_xattn_bo, L1_ffn_w_ln1, L1_ffn_w_ln2, L1_ffn_W_kvd, L1_ffn_W_qd, L1_ffn_W_ku, L1_ffn_W_qu, L1_ffn_W_vu, L1_ffn_W_ropeq, L1_ffn_W_ropek, L1_ffn_W_o, L1_ffn_Wg_s, L1_ffn_Wu_s, L1_ffn_Wd_s, L1_ffn_Wg_r, L1_ffn_Wu_r, L1_ffn_Wd_r, L1_ffn_W_router, L1_ffn_routing_bias):
    import jax
    import jax.numpy as jnp

    def _L0_attn_ref(x, W_DKV, W_UK, W_UV, W_UQ, W_O):
        import jax, jax.numpy as jnp
        import numpy as np
        DIM = 256
        N_HEADS = 16
        HEAD_DIM = DIM // N_HEADS
        D_LATENT = 64
        B, T = (1, 1024)
        b, t, d = x.shape
        h, hd = (N_HEADS, HEAD_DIM)
        c_kv = x @ W_DKV
        k = (c_kv @ W_UK).reshape(b, t, h, hd)
        v = (c_kv @ W_UV).reshape(b, t, h, hd)
        q = (x @ W_UQ).reshape(b, t, h, hd)
        scale = 1.0 / jnp.sqrt(jnp.asarray(hd, x.dtype))
        scores = jnp.einsum('bqhd,bkhd->bhqk', q, k) * scale
        causal = jnp.tril(jnp.ones((t, t), dtype=bool))
        scores = jnp.where(causal, scores, jnp.asarray(-jnp.inf, scores.dtype))
        probs = jax.nn.softmax(scores, axis=-1)
        ctx = jnp.einsum('bhqk,bkhd->bqhd', probs, v).reshape(b, t, d)
        return ctx @ W_O

    def _L0_xattn_ref(hidden_states, encoder_hidden_states, attention_mask, Wq, bq, Wk, bk, Wv, bv, Wo, bo):
        import jax, jax.numpy as jnp
        import numpy as np
        NUM_HEADS = 16
        DIM = 256
        B, N, C = hidden_states.shape
        T = encoder_hidden_states.shape[1]
        H = NUM_HEADS
        D = C // H
        q = (hidden_states @ Wq.T + bq).reshape(B, N, H, D).transpose(0, 2, 1, 3)
        k = (encoder_hidden_states @ Wk.T + bk).reshape(B, T, H, D).transpose(0, 2, 1, 3)
        v = (encoder_hidden_states @ Wv.T + bv).reshape(B, T, H, D).transpose(0, 2, 1, 3)
        scale = 1.0 / jnp.sqrt(jnp.asarray(D, q.dtype))
        scores = jnp.einsum('bhnd,bhtd->bhnt', q, k) * scale + attention_mask[:, None, :, :]
        attn = jax.nn.softmax(scores, axis=-1)
        out = jnp.einsum('bhnt,bhtd->bhnd', attn, v)
        out = out.transpose(0, 2, 1, 3).reshape(B, N, C)
        return out @ Wo.T + bo

    def _L0_ffn_ref(x, W_r, W_k, W_v, mu_r, mu_k):
        import jax, jax.numpy as jnp
        import numpy as np
        DIM = 256

        def _reference_tuple_inner(x, W_r, W_k, W_v, mu_r, mu_k):
            B, T, C = x.shape
            x_prev = jnp.concatenate([jnp.zeros((B, 1, C), x.dtype), x[:, :-1, :]], axis=1)
            xr = mu_r * x + (1.0 - mu_r) * x_prev
            xk = mu_k * x + (1.0 - mu_k) * x_prev
            r = jax.nn.sigmoid(jnp.einsum('btc,dc->btd', xr, W_r))
            k = jnp.einsum('btc,dc->btd', xk, W_k)
            k_act = jnp.square(jax.nn.relu(k))
            out = r * jnp.einsum('btc,dc->btd', k_act, W_v)
            new_state = x[:, -1, :]
            return (out, new_state)
        return _reference_tuple_inner(x, W_r, W_k, W_v, mu_r, mu_k)[0]

    def _L1_attn_ref(x, qkv_w, proj_w, proj_b, curvature):
        import math
        import jax, jax.numpy as jnp
        import numpy as np
        B, T, C = (2, 512, 256)
        H, N1, N2, N3 = (16, 6, 4, 6)
        HD = C // H

        def _rotary(T_, hd, dtype):
            inv_freq = 1.0 / 10000.0 ** (jnp.arange(0, hd, 2, dtype=jnp.float32) / hd)
            freqs = jnp.outer(jnp.arange(T_, dtype=jnp.float32), inv_freq)
            return (jnp.cos(freqs)[None, :, None, :].astype(dtype), jnp.sin(freqs)[None, :, None, :].astype(dtype))

        def _apply_rot(x, cos, sin):
            x1, x2 = (x[..., :x.shape[-1] // 2], x[..., x.shape[-1] // 2:])
            return jnp.concatenate([x1 * cos + x2 * sin, -x1 * sin + x2 * cos], axis=-1).astype(x.dtype)

        def _causal_bias(L, S, dtype):
            mask = jnp.triu(jnp.ones((L, S), bool), k=1)
            return jnp.where(mask, jnp.asarray(-jnp.inf, dtype), jnp.asarray(0.0, dtype))

        def _sdpa(q, k, v, scale):
            scores = jnp.einsum('bhtd,bhsd->bhts', q, k) * scale + _causal_bias(q.shape[-2], k.shape[-2], q.dtype)
            return jnp.einsum('bhts,bhsd->bhtd', jax.nn.softmax(scores, axis=-1), v)

        def _hyp_attn(q, k, v, curv):
            eps = 1e-06
            tq = jnp.sqrt(1.0 / curv + jnp.sum(q * q, axis=-1, keepdims=True))
            tk = jnp.sqrt(1.0 / curv + jnp.sum(k * k, axis=-1, keepdims=True))
            inner = jnp.einsum('bhtd,bhsd->bhts', q, k) - tq * jnp.swapaxes(tk, -1, -2)
            arg = jnp.maximum(-curv * inner, 1.0 + 1e-07)
            dis = jnp.sqrt(1.0 / curv) * jnp.arccosh(arg)
            scores = 1.0 / (eps + dis) + _causal_bias(q.shape[-2], k.shape[-2], q.dtype)
            return jnp.einsum('bhts,bhsd->bhtd', jax.nn.softmax(scores, axis=-1), v)
        Bx, Tx, Cx = x.shape
        qkv = x @ qkv_w.T
        q, k, v = jnp.split(qkv, 3, axis=-1)
        q = q.reshape(Bx, Tx, H, HD)
        k = k.reshape(Bx, Tx, H, HD)
        v = v.reshape(Bx, Tx, H, HD)
        cos, sin = _rotary(Tx, HD, x.dtype)
        q = _apply_rot(q, cos, sin)
        k = _apply_rot(k, cos, sin)
        q, k, v = (jnp.swapaxes(t, 1, 2) for t in (q, k, v))
        outs = []
        outs.append(_sdpa(q[:, :N1], k[:, :N1], v[:, :N1], 1.0 / math.sqrt(HD)))
        outs.append(_hyp_attn(q[:, N1:N1 + N2], k[:, N1:N1 + N2], v[:, N1:N1 + N2], curvature))
        qn = q[:, N1 + N2:] / jnp.maximum(jnp.linalg.norm(q[:, N1 + N2:], axis=-1, keepdims=True), 1e-12)
        kn = k[:, N1 + N2:] / jnp.maximum(jnp.linalg.norm(k[:, N1 + N2:], axis=-1, keepdims=True), 1e-12)
        outs.append(_sdpa(qn, kn, v[:, N1 + N2:], math.sqrt(HD)))
        y = jnp.concatenate(outs, axis=1)
        y = jnp.swapaxes(y, 1, 2).reshape(Bx, Tx, Cx)
        return y @ proj_w.T + proj_b

    def _L1_xattn_ref(query, key, value, Wq, bq, Wk, bk, Wv, bv, Wo, bo):
        import jax, jax.numpy as jnp
        import numpy as np
        HEAD = 16
        EMB = 256
        B, S = (8, 1024)

        def _proj_heads(x, W, b, H, d):
            Bx, Sx, _ = x.shape
            y = x @ W.T + b
            return y.reshape(Bx, Sx, H, d).transpose(0, 2, 1, 3)
        Bx, Sx, E = query.shape
        H = HEAD
        d = E // H
        q = jax.nn.elu(_proj_heads(query, Wq, bq, H, d))
        k = jax.nn.elu(_proj_heads(key, Wk, bk, H, d))
        v = _proj_heads(value, Wv, bv, H, d)
        sqrt_S = jnp.asarray(np.sqrt(Sx), jnp.float32)
        k = k / (jnp.linalg.norm(k, axis=2, keepdims=True) * sqrt_S)
        sqrt_d = jnp.asarray(np.sqrt(d), jnp.float32)
        q = q / (jnp.linalg.norm(q, axis=3, keepdims=True) * sqrt_d)
        scores = jnp.einsum('bhsd,bhse->bhde', k, v)
        x = jnp.einsum('bhsd,bhde->bhse', q, scores)
        x = x.transpose(0, 2, 1, 3).reshape(Bx, Sx, E)
        return x @ Wo.T + bo

    def _L1_ffn_ref(x, w_ln1, w_ln2, W_kvd, W_qd, W_ku, W_qu, W_vu, W_ropeq, W_ropek, W_o, Wg_s, Wu_s, Wd_s, Wg_r, Wu_r, Wd_r, W_router, routing_bias):
        import jax, jax.numpy as jnp
        import numpy as np
        H = 256
        NH = 16
        HD = H // NH
        HH = HD // 2
        L = H // 4
        I = int(H * 1.0)
        ER = 7
        TOPK = 2
        BASE = 10000.0
        EPS = 1e-05

        def rmsnorm(x, w):
            norm = jnp.sqrt(jnp.mean(x * x, axis=-1, keepdims=True)) + EPS
            return x / norm * w

        def rope_tables(seq_len):
            inv_freq = 1.0 / BASE ** (jnp.arange(0, HH, 2, dtype=jnp.float32) / HH)
            t = jnp.arange(seq_len, dtype=jnp.float32)
            freqs = jnp.einsum('i,j->ij', t, inv_freq)
            emb = jnp.concatenate([freqs, freqs], axis=-1)
            cos = jnp.cos(emb)[None, :, None, :]
            sin = jnp.sin(emb)[None, :, None, :]
            return (cos, sin)

        def rotate_half(x):
            x1, x2 = jnp.split(x, 2, axis=-1)
            return jnp.concatenate([-x2, x1], axis=-1)

        def silu(x):
            return x * jax.nn.sigmoid(x)

        def mla(xn, W_kvd, W_qd, W_ku, W_qu, W_vu, W_ropeq, W_ropek, W_o):
            B, S, _ = xn.shape
            kv_lat = xn @ W_kvd
            q_lat = xn @ W_qd
            k = (kv_lat @ W_ku).reshape(B, S, NH, HH)
            q = (q_lat @ W_qu).reshape(B, S, NH, HH)
            v = (kv_lat @ W_vu).reshape(B, S, NH, HD)
            q_rope = (q_lat @ W_ropeq).reshape(B, S, NH, HH)
            k_rope = (xn @ W_ropek).reshape(B, S, NH, HH)
            cos, sin = rope_tables(S)
            k_rope = k_rope * cos + rotate_half(k_rope) * sin
            q_rope = q_rope * cos + rotate_half(q_rope) * sin
            kk = jnp.concatenate([k, k_rope], axis=-1)
            qq = jnp.concatenate([q, q_rope], axis=-1)
            scale = 1.0 / jnp.sqrt(jnp.float32(HD))
            scores = jnp.einsum('bqhd,bkhd->bhqk', qq, kk) * scale
            causal = jnp.tril(jnp.ones((S, S), dtype=bool))
            scores = jnp.where(causal[None, None], scores, jnp.finfo(scores.dtype).min)
            probs = jax.nn.softmax(scores, axis=-1)
            y = jnp.einsum('bhqk,bkhd->bqhd', probs, v).reshape(B, S, H)
            return y @ W_o

        def moe(xn, Wg_s, Wu_s, Wd_s, Wg_r, Wu_r, Wd_r, W_router, routing_bias):
            B, S, _ = xn.shape
            xt = xn.reshape(B * S, H)
            shared = silu(xt @ Wg_s) * (xt @ Wu_s) @ Wd_s
            logits = xt @ W_router + routing_bias
            probs = jax.nn.sigmoid(logits)
            scores, idx = jax.lax.top_k(probs, TOPK)
            scores = scores / jnp.sum(scores, axis=-1, keepdims=True)
            wts = jnp.sum(jax.nn.one_hot(idx, ER, dtype=xt.dtype) * scores[..., None], axis=1)
            g = jnp.einsum('th,ehi->tei', xt, Wg_r)
            u = jnp.einsum('th,ehi->tei', xt, Wu_r)
            hmid = silu(g) * u
            combined = jnp.einsum('tei,eih,te->th', hmid, Wd_r, wts)
            return (shared + combined).reshape(B, S, H)
        x = x + mla(rmsnorm(x, w_ln1), W_kvd, W_qd, W_ku, W_qu, W_vu, W_ropeq, W_ropek, W_o)
        x = x + moe(rmsnorm(x, w_ln2), Wg_s, Wu_s, Wd_s, Wg_r, Wu_r, Wd_r, W_router, routing_bias)
        return x
    x = x + _L0_attn_ref(_layernorm(x, axis=-1), L0_attn_W_DKV, L0_attn_W_UK, L0_attn_W_UV, L0_attn_W_UQ, L0_attn_W_O)
    x = x + _L0_xattn_ref(_layernorm(x, axis=-1), ctx_1024, mask_BxSxS2_ff0, L0_xattn_Wq, L0_xattn_bq, L0_xattn_Wk, L0_xattn_bk, L0_xattn_Wv, L0_xattn_bv, L0_xattn_Wo, L0_xattn_bo)
    x = x + _L0_ffn_ref(_layernorm(x, axis=-1), L0_ffn_W_r, L0_ffn_W_k, L0_ffn_W_v, L0_ffn_mu_r, L0_ffn_mu_k)
    x = x + _L1_attn_ref(_layernorm(x, axis=-1), L1_attn_qkv_w, L1_attn_proj_w, L1_attn_proj_b, L1_attn_curvature)
    x = x + _L1_xattn_ref(_layernorm(x, axis=-1), ctx_1024, ctx_1024, L1_xattn_Wq, L1_xattn_bq, L1_xattn_Wk, L1_xattn_bk, L1_xattn_Wv, L1_xattn_bv, L1_xattn_Wo, L1_xattn_bo)
    x = x + _L1_ffn_ref(_layernorm(x, axis=-1), L1_ffn_w_ln1, L1_ffn_w_ln2, L1_ffn_W_kvd, L1_ffn_W_qd, L1_ffn_W_ku, L1_ffn_W_qu, L1_ffn_W_vu, L1_ffn_W_ropeq, L1_ffn_W_ropek, L1_ffn_W_o, L1_ffn_Wg_s, L1_ffn_Wu_s, L1_ffn_Wd_s, L1_ffn_Wg_r, L1_ffn_Wu_r, L1_ffn_Wd_r, L1_ffn_W_router, L1_ffn_routing_bias)
    return x

_drawn_inputs = setup_inputs


def setup_inputs(seed=0):
    import zlib

    import numpy as np

    out = dict(_drawn_inputs(seed))
    spreads = {'L0_xattn_bq': (0.0, 0.353),
     'L0_xattn_bk': (0.0, 0.8),
     'L0_xattn_bv': (0.0, 0.1),
     'L0_xattn_bo': (0.0, 0.1),
     'L1_attn_proj_b': (0.0, 0.1),
     'L1_attn_curvature': (1.0, 0.6),
     'L1_xattn_bq': (0.0, 0.782),
     'L1_xattn_bk': (0.0, 0.469),
     'L1_xattn_bv': (0.0, 0.507),
     'L1_xattn_bo': (0.0, 0.1),
     'L1_ffn_w_ln1': (1.0, 0.6),
     'L1_ffn_w_ln2': (1.0, 0.6),
     'L1_ffn_routing_bias': (0.0, 0.8)}
    factors = {'L0_attn_W_DKV': 8.0,
     'L0_attn_W_UK': 8.0,
     'L0_attn_W_UV': 8.0,
     'L0_attn_W_UQ': 8.0,
     'L0_attn_W_O': 8.0,
     'L0_ffn_W_r': 3.283,
     'L0_ffn_mu_r': 8.0,
     'L1_ffn_W_kvd': 8.0,
     'L1_ffn_W_qd': 8.0,
     'L1_ffn_W_ku': 8.0,
     'L1_ffn_W_qu': 8.0,
     'L1_ffn_W_vu': 8.0,
     'L1_ffn_W_ropeq': 8.0,
     'L1_ffn_W_ropek': 8.0,
     'L1_ffn_W_o': 8.0,
     'L1_ffn_Wg_s': 7.076,
     'L1_ffn_Wu_s': 7.2,
     'L1_ffn_Wd_s': 7.167,
     'L1_ffn_Wg_r': 8.0,
     'L1_ffn_Wu_r': 8.0,
     'L1_ffn_Wd_r': 8.0,
     'L1_ffn_W_router': 8.0}
    for name, (base, spread) in spreads.items():
        noise = np.random.default_rng([zlib.crc32(name.encode()), seed]).standard_normal(out[name].shape)
        drawn = base * np.exp(spread * noise) if base else spread * noise
        out[name] = jnp.asarray(drawn.astype(out[name].dtype))
    for name, factor in factors.items():
        out[name] = (out[name] * factor).astype(out[name].dtype)
    return out
```

```python
from contextlib import ExitStack

import concourse.bass as bass
from concourse import mybir

F32 = mybir.dt.float32
BF16 = mybir.dt.bfloat16
U32 = mybir.dt.uint32
ALU = mybir.AluOpType
ACT = mybir.ActivationFunctionType
AX = mybir.AxisListType

P = 128
NB, S, D = 8, 512, 256
H, HD = 16, 16
CTX = 1601
T = S // P
FT = D // P
GH = 4
NG = H // GH
VW = 32
NEG = -1.0e30
K_LEVEL = (0, 1, 2, 0, 1, 0)
Q_LEVEL = (0, 0, 0, 1, 1, 2)
NSLOT = len(K_LEVEL)
STACK = NSLOT * HD
SHIFT = 3
EPS = 1e-5
TINY = 2.0 ** -23


def tiles_of(n):
    return [(i, min(P, n - i)) for i in range(0, n, P)]


class Steps:

    def __init__(self, eng, sem):
        self.eng, self.sem, self.n = eng, sem, 0

    def mark(self, instruction):
        self.n += 1
        return instruction.then_inc(self.sem, 1)

    def settle(self):
        if self.n:
            self.eng.wait_ge(self.sem, self.n)


class Stage:

    def __init__(self, nc, ctx, name):
        self.nc, self.ctx, self.name, self.nums = nc, ctx, name, []

    def sb(self, name, shape, dt=F32):
        return self.ctx.enter_context(self.nc.sbuf_tensor(f"{self.name}_{name}", shape, dt))

    def psum(self):
        return self.ctx.enter_context(self.nc.psum_tensor(f"{self.name}_ps", [P, 8, 512], F32))

    def sem(self, name):
        s = self.ctx.enter_context(self.nc.semaphore(f"{self.name}_{name}"))
        self.nums.append(s.num)
        return s

    def runs(self):
        nums, out = sorted(self.nums), []
        for n in nums:
            if out and n == out[-1].stop:
                out[-1] = range(out[-1].start, n + 1)
            else:
                out.append(range(n, n + 1))
        return out


def stage_loop(nc, st, programs):
    with nc.Fori(0, NB) as b:
        with nc.Block() as block:
            @block.sync
            def _(sp):
                programs["sync"](sp, b)

            @block.tensor
            def _(pe):
                programs["tensor"](pe)

            @block.vector
            def _(dve):
                programs["vector"](dve)

            @block.scalar
            def _(act):
                programs["scalar"](act)

            @block.gpsimd
            def _(pool):
                if "gpsimd" in programs:
                    programs["gpsimd"](pool)
        for run in st.runs():
            nc.all_engine_barrier(sems_to_clear=run)



class Norm:

    def __init__(self, st, ps, x, identf, rms=False, weight=None, banks=(0, 1)):
        self.ps, self.x, self.identf, self.rms, self.weight, self.banks = ps, x, identf, rms, weight, banks
        self.xn = st.sb("xn", [P, T, D])
        self.xnT = st.sb("xnT", [P, FT, S + 1])
        self.stats = st.sb("stats", [P, T, 6])
        self.mv = st.sb("mv", [P, T, 2])
        self.var = st.sb("var", [P, T])
        self.lnv = st.sb("lnv", [P, T])
        self.rstd = st.sb("rstd", [P, T])
        self.x_loaded = st.sem("x_loaded")
        self.outer_var_ready, self.outer_rstd_ready = st.sem("outer_var_ready"), st.sem("outer_rstd_ready")
        self.var_ready = st.sem("var_ready")
        self.rstd_ready = st.sem("rstd_ready")
        self.xn_ready = st.sem("xn_ready")
        self.xnT_in_psum = st.sem("xnT_in_psum")
        self.xnT_ready = st.sem("xnT_ready")

    def outer_vector(self, dve, steps):
        dve.wait_ge(self.x_loaded, 16)
        for t in range(T):
            steps.mark(dve.bn_stats(self.stats[:, t, :], self.x[:, t, :]))
        steps.settle()
        for t in range(T):
            steps.mark(dve.bn_aggr(self.mv[:, t, :], self.stats[:, t, :]))
        steps.settle()
        dve.tensor_scalar(self.var[:, :], self.mv[:, :, 1], EPS, None, ALU.add).then_inc(self.outer_var_ready, 1)
        dve.wait_ge(self.outer_rstd_ready, 1)
        for t in range(T):
            steps.mark(dve.tensor_scalar(self.x[:, t, :], self.x[:, t, :], self.mv[:, t, 0:1],
                                         self.rstd[:, t:t + 1], ALU.subtract, ALU.mult))
        steps.settle()

    def outer_scalar(self, act, steps):
        act.wait_ge(self.outer_var_ready, 1)
        steps.mark(act.activation(self.lnv[:, :], self.var[:, :], ACT.Ln))
        steps.settle()
        act.activation(self.rstd[:, :], self.lnv[:, :], ACT.Exp, scale=-0.5).then_inc(self.outer_rstd_ready, 1)

    def vector(self, dve, steps):
        dve.wait_ge(self.x_loaded, 16)
        for t in range(T):
            steps.mark(dve.bn_stats(self.stats[:, t, :], self.x[:, t, :]))
        steps.settle()
        for t in range(T):
            steps.mark(dve.bn_aggr(self.mv[:, t, :], self.stats[:, t, :]))
        steps.settle()
        if self.rms:
            steps.mark(dve.tensor_tensor(self.lnv[:, :], self.mv[:, :, 0], self.mv[:, :, 0], ALU.mult))
            steps.settle()
            steps.mark(dve.scalar_tensor_tensor(out=self.var[:, :], in0=self.mv[:, :, 1], scalar=1e-18,
                                                in1=self.lnv[:, :], op0=ALU.add, op1=ALU.add))
            steps.settle()
            dve.sem_inc(self.var_ready, 1)
            dve.wait_ge(self.rstd_ready, 1)
            steps.mark(dve.tensor_scalar(self.var[:, :], self.rstd[:, :], EPS, None, ALU.add))
            steps.settle()
            steps.mark(dve.reciprocal(self.rstd[:, :], self.var[:, :]))
            steps.settle()
            for t in range(T):
                dve.tensor_scalar(self.xn[:, t, :], self.x[:, t, :], self.rstd[:, t:t + 1], None,
                                  ALU.mult).then_inc(self.xn_ready, 1)
            return
        dve.tensor_scalar(self.var[:, :], self.mv[:, :, 1], EPS, None, ALU.add).then_inc(self.var_ready, 1)
        dve.wait_ge(self.rstd_ready, 1)
        for t in range(T):
            dve.tensor_scalar(self.xn[:, t, :], self.x[:, t, :], self.mv[:, t, 0:1], self.rstd[:, t:t + 1],
                              ALU.subtract, ALU.mult).then_inc(self.xn_ready, 1)

    def scalar(self, act, steps):
        act.wait_ge(self.var_ready, 1)
        steps.mark(act.activation(self.lnv[:, :], self.var[:, :], ACT.Ln))
        steps.settle()
        act.activation(self.rstd[:, :], self.lnv[:, :], ACT.Exp,
                       scale=0.5 if self.rms else -0.5).then_inc(self.rstd_ready, 1)
        for f in range(FT):
            act.wait_ge(self.xnT_in_psum, f + 1)
            scale = 1.0 if self.weight is None else self.weight[:, f:f + 1]
            act.activation(self.xnT[:, f, 1:S + 1], self.ps[:, self.banks[f], :], ACT.Identity,
                           scale=scale).then_inc(self.xnT_ready, 1)

    def tensor(self, pe):
        for f in range(FT):
            for t in range(T):
                if f == 0:
                    pe.wait_ge(self.xn_ready, t + 1)
                last = pe.transpose(self.ps[:, self.banks[f], t * P:(t + 1) * P],
                                    self.xn[:, t, f * P:(f + 1) * P], self.identf[:, :])
            last.then_inc(self.xnT_in_psum, 1)



class Split:

    def __init__(self, st, width, items, tag=""):
        self.items = items
        self.full = st.sb(f"full{tag}", [P, 2, width])
        self.level = st.sb(f"level{tag}", [P, 2, 3, width], BF16)
        self.full_ready = st.sem(f"full_ready{tag}")
        self.level0_ready = st.sem(f"level0_ready{tag}")
        self.levels_ready = st.sem(f"levels_ready{tag}")
        self.written = [st.sem(f"levels_written{tag}{i}") for i in range(items)]

    def writes(self, i):
        return 16 * NSLOT

    def vector(self, dve, steps, i, w):
        full, level = self.full[:, i % 2, 0:w], self.level[:, i % 2]
        dve.wait_ge(self.level0_ready, i + 1)
        steps.mark(dve.tensor_tensor(full, full, level[:, 0, 0:w], ALU.subtract))
        steps.settle()
        if i >= 2:
            dve.wait_ge(self.written[i - 2], self.writes(i - 2))
        steps.mark(dve.tensor_copy(level[:, 1, 0:w], full))
        steps.settle()
        steps.mark(dve.tensor_tensor(level[:, 2, 0:w], full, level[:, 1, 0:w], ALU.subtract))
        steps.settle()
        dve.sem_inc(self.levels_ready, 1)

    def scalar(self, act, i, w):
        act.wait_ge(self.full_ready, i + 1)
        if i >= 2:
            act.wait_ge(self.written[i - 2], self.writes(i - 2))
        act.activation(self.level[:, i % 2, 0, 0:w], self.full[:, i % 2, 0:w], ACT.Copy)\
            .then_inc(self.level0_ready, 1)

    def sync(self, sp, i, w, scratch, heads, slots):
        sp.wait_ge(self.levels_ready, i + 1)
        for s, lev in enumerate(slots):
            sp.dma_start(scratch[heads[0]:heads[1], s, :, 0:w], self.level[:, i % 2, lev, 0:w])\
                .then_inc(self.written[i], 16)



class Attention:

    def __init__(self, st, ps, identf, identb, otok, keys, groups, causal, masked=False):
        self.ps, self.identf, self.identb = ps, identf, identb
        self.keys, self.groups, self.causal, self.masked = tiles_of(keys), groups, causal, masked
        self.nslots = 4 if causal else 2
        self.npt = 4
        self.kst = st.sb("kstack", [P, self.nslots, GH, keys], BF16)
        self.qst = st.sb("qstack", [P, self.nslots, GH, S], BF16)
        self.v = st.sb("v", [P, len(self.keys), H, VW])
        self.probs = st.sb("probs", [P, self.npt, 2, S])
        self.nchunk = 1 if causal else 4
        self.chunk = -(-keys // self.nchunk)
        self.cmax = st.sb("cmax", [P, 2, T * GH, 4])
        self.nmax = st.sb("nmax", [P, 2, T, GH])
        self.rest = st.sb("rest", [P, 2, T, GH])
        self.shift = st.sb("shift", [P, 2, T, SHIFT * GH], BF16)
        self.shiftT = st.sb("shiftT", [SHIFT * GH, 2, S], BF16)
        self.oT = st.sb("oT", [P, S])
        self.inv = st.sb("inv", [P, T, GH])
        self.otok = otok
        if masked:
            self.junk = st.sb("junk", [P, 2, self.chunk])
        self.stacks_loaded = [st.sem(f"stacks_loaded{g}") for g in range(groups)]
        self.shift_loaded = [st.sem(f"shift_loaded{g}") for g in range(groups)]
        self.v_ready = st.sem("v_ready")
        self.max_scored = st.sem("max_scored")
        self.max_taken = st.sem("max_taken")
        self.shift_split = st.sem("shift_split")
        self.shift_turned = st.sem("shift_turned")
        self.shift_copied = st.sem("shift_copied")
        self.scored = st.sem("scored")
        self.exped = st.sem("exped")
        self.pv_done = st.sem("pv_done")
        self.oT_copied = st.sem("oT_copied")
        self.o_turned = st.sem("o_turned")
        self.o_divided = st.sem("o_divided")
        self.units = [(j, t, c, (t + 1) * P if causal else min(self.chunk, keys - c * self.chunk))
                      for t in range(T) for j in range(GH) for c in range(self.nchunk)]
        self.order = self.plan()

    def plan(self):
        out, pv, post = [], [], []
        ngr, nu = self.groups, len(self.units)
        steps = [(g, k, p) for g in range(ngr) for k in range(len(self.keys)) for p in range(2)]
        per = 2 * len(self.keys)
        ahead = 2 if self.causal else 1
        unit = [("max", g, i) for g in range(ngr) for i in range(nu)]
        done = 0

        def units_until(n):
            nonlocal done
            while done < min(n, len(unit)):
                out.append(unit[done])
                done += 1
                if done % nu == 0:
                    out.append(("split", done // nu - 1))
                    out.append(("shift", done // nu - 1))

        units_until(nu * ahead)
        for i, (g, k, p) in enumerate(steps):
            out.append(("score", g, k, p))
            pv.append(("pv", g, k, p))
            if len(pv) > 2:
                out.append(pv.pop(0))
                if out[-1][2] == len(self.keys) - 1 and out[-1][3] == 1:
                    out.append(("copy", out[-1][1]))
                    post.append((i + 2, out[-1][1]))
            if post and i >= post[0][0]:
                out.append(("post", post.pop(0)[1]))
            begin = 0.0 if self.nslots > 2 else 0.25
            fraction = min(1.0, max(0.0, (i % per + 1) / per - begin) / (0.85 - begin))
            units_until(int(nu * (ahead + g + fraction)) if g + ahead < ngr else 0)
        for item in pv:
            out.append(item)
            if item[2] == len(self.keys) - 1 and item[3] == 1:
                out.append(("copy", item[1]))
                post.append((0, item[1]))
        out += [("post", g) for _, g in post]
        return out

    def load_stacks(self, sp, g, kscratch, qscratch, w):
        heads = slice(g * GH, (g + 1) * GH)
        if g >= self.nslots:
            sp.wait_ge(self.scored, 2 * len(self.keys) * (g - self.nslots + 1))
        sp.dma_start(self.kst[0:STACK, g % self.nslots, :, 0:w],
                     kscratch[heads, :, :, 0:w].rearrange("h s d w -> (s d) h w"))\
            .then_inc(self.stacks_loaded[g], 16)
        sp.dma_start(self.qst[0:STACK, g % self.nslots, :, :],
                     qscratch[heads].rearrange("h s d w -> (s d) h w")).then_inc(self.stacks_loaded[g], 16)

    def sync(self, sp, refill=None):
        for item in self.order:
            if item[0] == "shift":
                g = item[1]
                sp.wait_ge(self.shift_copied, g + 1)
                for lev in range(SHIFT):
                    sp.dma_start(self.qst[STACK + lev:STACK + lev + 1, g % self.nslots, :, :],
                                 self.shiftT[lev * GH:(lev + 1) * GH, g % 2, :])\
                        .then_inc(self.shift_loaded[g], 16)
            if item[0] == "copy" and refill and item[1] + 2 < self.groups:
                self.load_stacks(sp, item[1] + 2, *refill)

    def tensor(self, pe, maskT=None, tri=None, triT=None):
        ps, nk = self.ps, len(self.keys)
        nmax = nscore = npv = 0
        b7_readers = []
        for item in self.order:
            if item[0] == "max":
                g, (j, t, c, n) = item[1], self.units[item[2]]
                if item[2] == 0:
                    pe.wait_ge(self.stacks_loaded[g], 32)
                if nmax >= 2:
                    pe.wait_ge(self.max_taken, nmax - 1)
                bank, sl = 4 + nmax % 2, g % self.nslots
                k0 = c * self.chunk
                mm = pe.matmul(ps[:, bank, 0:n], self.qst[0:STACK, sl, j, t * P:(t + 1) * P],
                               self.kst[0:STACK, sl, j, k0:k0 + n], start=True, stop=not self.causal)
                if self.causal:
                    mm = pe.matmul(ps[:, bank, n - P:n], self.identb[:, :], tri[:, :], start=False, stop=True)
                mm.then_inc(self.max_scored, 1)
                nmax += 1
            elif item[0] == "shift":
                g = item[1]
                pe.wait_ge(self.shift_split, g + 1)
                if b7_readers:
                    pe.wait_ge(*b7_readers[-1])
                for t in range(T):
                    mm = pe.matmul(ps[0:SHIFT * GH, 7, t * P:(t + 1) * P], self.shift[:, g % 2, t, :],
                                   self.identb[:, :], start=True, stop=True)
                mm.then_inc(self.shift_turned, 1)
                b7_readers.append((self.shift_copied, g + 1))
            elif item[0] == "score":
                _, g, k, p = item
                sl = g % self.nslots
                if k == 0 and p == 0:
                    pe.wait_ge(self.shift_loaded[g], 16 * SHIFT)
                if nscore >= 2:
                    pe.wait_ge(self.exped, nscore - 1)
                k0, n = self.keys[k]
                q0 = k0 if self.causal else 0
                for j in (2 * p, 2 * p + 1):
                    bank = 2 * (nscore % 2) + j % 2
                    extra = self.causal or self.masked
                    mm = pe.matmul(ps[0:n, bank, 0:S - q0], self.kst[0:STACK + SHIFT, sl, j, k0:k0 + n],
                                   self.qst[0:STACK + SHIFT, sl, j, q0:S], start=True, stop=not extra)
                    if self.causal:
                        mm = pe.matmul(ps[0:n, bank, 0:P], self.identb[:, :], triT[:, :], start=False, stop=True)
                    if self.masked:
                        mm = pe.matmul(ps[0:n, bank, :], self.identf[0:n, 0:n], maskT[0:n, k, :],
                                       start=False, stop=True)
                mm.then_inc(self.scored, 1)
                nscore += 1
            elif item[0] == "pv":
                _, g, k, p = item
                if k == 0 and p == 0 and g > 0:
                    pe.wait_ge(self.oT_copied, g)
                pe.wait_ge(self.exped, npv + 1)
                k0, n = self.keys[k]
                q0 = k0 if self.causal else 0
                for j in (2 * p, 2 * p + 1):
                    mm = pe.matmul(ps[VW * j:VW * (j + 1), 6, q0:S], self.v[0:n, k, g * GH + j, :],
                                   self.probs[0:n, npv % self.npt, j % 2, q0:S],
                                   start=(k == 0), stop=(k == nk - 1))
                mm.then_inc(self.pv_done, 1)
                npv += 1
            elif item[0] == "post":
                g = item[1]
                pe.wait_ge(self.oT_copied, g + 1)
                if b7_readers:
                    pe.wait_ge(*b7_readers[-1])
                for t in range(T):
                    mm = pe.transpose(ps[:, 7, t * P:(t + 1) * P], self.oT[:, t * P:(t + 1) * P], self.identf[:, :])
                mm.then_inc(self.o_turned, 1)
                b7_readers.append((self.o_divided, g + 1))
        self.b7_free = b7_readers[-1]

    def scalar(self, act):
        ps, nscore = self.ps, 0
        for item in self.order:
            if item[0] == "shift":
                g = item[1]
                act.wait_ge(self.shift_turned, g + 1)
                if g >= 2:
                    act.wait_ge(self.shift_loaded[g - 2], 16 * SHIFT)
                act.activation(self.shiftT[:, g % 2, :], ps[0:SHIFT * GH, 7, :], ACT.Copy)\
                    .then_inc(self.shift_copied, 1)
            elif item[0] == "score":
                _, g, k, p = item
                k0, n = self.keys[k]
                q0 = k0 if self.causal else 0
                act.wait_ge(self.scored, nscore + 1)
                if nscore >= self.npt:
                    act.wait_ge(self.pv_done, nscore - self.npt + 1)
                bank = 2 * (nscore % 2)
                act.activation(self.probs[0:n, nscore % self.npt, :, q0:S], ps[0:n, bank:bank + 2, 0:S - q0],
                               ACT.Exp).then_inc(self.exped, 1)
                nscore += 1
            elif item[0] == "copy":
                g = item[1]
                act.wait_ge(self.pv_done, 2 * len(self.keys) * (g + 1))
                if g >= 1:
                    act.wait_ge(self.o_turned, g)
                act.activation(self.oT[:, :], ps[:, 6, :], ACT.Copy).then_inc(self.oT_copied, 1)

    def vector(self, dve, steps, maskq=None, vbias=None):
        ps, nmax = self.ps, 0
        for item in self.order:
            if item[0] == "max":
                g, (j, t, c, n) = item[1], self.units[item[2]]
                dve.wait_ge(self.max_scored, nmax + 1)
                bank = 4 + nmax % 2
                if self.masked:
                    if nmax >= 2:
                        dve.wait_ge(self.max_taken, nmax - 1)
                    dve.tensor_tensor_reduce(self.junk[:, nmax % 2, 0:n], ps[:, bank, 0:n],
                                             maskq[:, t, c * self.chunk:c * self.chunk + n], 1.0, -3.0e38,
                                             ALU.add, ALU.max, self.cmax[:, g % 2, t * GH + j, c:c + 1])\
                        .then_inc(self.max_taken, 1)
                elif self.nchunk > 1:
                    dve.tensor_reduce(self.cmax[:, g % 2, t * GH + j, c:c + 1], ps[:, bank, 0:n], AX.X,
                                      ALU.max).then_inc(self.max_taken, 1)
                else:
                    dve.tensor_reduce(self.nmax[:, g % 2, t, j:j + 1], ps[:, bank, 0:n], AX.X, ALU.max,
                                      negate=True).then_inc(self.max_taken, 1)
                nmax += 1
            elif item[0] == "split":
                g = item[1]
                dve.wait_ge(self.max_taken, nmax)
                nm, rest = self.nmax[:, g % 2], self.rest[:, g % 2]
                if self.nchunk > 1:
                    steps.mark(dve.tensor_reduce(nm.rearrange("p t j -> p (t j)"), self.cmax[:, g % 2], AX.X,
                                                 ALU.max, negate=True))
                    steps.settle()
                if g >= 2:
                    dve.wait_ge(self.shift_turned, g - 1)
                sh = [self.shift[:, g % 2, :, lev * GH:(lev + 1) * GH] for lev in range(SHIFT)]
                steps.mark(dve.tensor_copy(sh[0], nm))
                steps.settle()
                steps.mark(dve.tensor_tensor(rest, nm, sh[0], ALU.subtract))
                steps.settle()
                steps.mark(dve.tensor_copy(sh[1], rest))
                steps.settle()
                dve.tensor_tensor(sh[2], rest, sh[1], ALU.subtract).then_inc(self.shift_split, 1)
            elif item[0] == "post":
                g = item[1]
                dve.wait_ge(self.o_turned, g + 1)
                o = ps[:, 7, :].rearrange("p (t j w) -> p t j w", t=T, j=GH)
                steps.mark(dve.reciprocal(self.inv[:, :, :], o[:, :, :, HD]))
                steps.settle()
                out = self.otok[:, :, g * GH * HD:(g + 1) * GH * HD].rearrange("p t (j d) -> p t j d", j=GH)
                inv = self.inv[:, :, :].rearrange("p t (j o) -> p t j o", o=1).to_broadcast([P, T, GH, HD])
                ins = dve.tensor_tensor(out, o[:, :, :, 0:HD], inv, ALU.mult)
                if vbias is None:
                    ins.then_inc(self.o_divided, 1)
                    continue
                ins.then_inc(self.o_divided, 1)
                dve.wait_ge(self.o_divided, g + 1)
                o3 = self.otok[:, :, g * GH * HD:(g + 1) * GH * HD]
                vb = vbias[:, g * GH * HD:(g + 1) * GH * HD].rearrange("p (o d) -> p o d", o=1)
                steps.mark(dve.tensor_tensor(o3, o3, vb.to_broadcast([P, T, GH * HD]), ALU.add))
        steps.settle()


class OutProjection:

    def __init__(self, st, ps, identf, otok, oF, wo, x, bias=None):
        self.ps, self.identf, self.otok, self.wo, self.x, self.bias = ps, identf, otok, wo, x, bias
        self.oF = oF
        self.o_ready = st.sem("o_ready")
        self.oF_in_psum = st.sem("oF_in_psum")
        self.oF_ready = st.sem("oF_ready")
        self.projected = st.sem("projected")
        self.x_done = st.sem("x_done")

    def tensor(self, pe, turn=True):
        ps = self.ps
        if turn:
            pe.wait_ge(self.o_ready, 1)
            for f in range(FT):
                for t in range(T):
                    mm = pe.transpose(ps[:, f, t * P:(t + 1) * P], self.otok[:, t, f * P:(f + 1) * P],
                                      self.identf[:, :])
                mm.then_inc(self.oF_in_psum, 1)
        for h in range(2):
            for t in (2 * h, 2 * h + 1):
                for f in range(FT):
                    if h == 0 and t == 0:
                        pe.wait_ge(self.oF_ready, f + 1)
                    mm = pe.matmul(ps[:, 2 + h, (t % 2) * D:(t % 2 + 1) * D], self.oF[:, f, t * P:(t + 1) * P],
                                   self.wo[:, f, :], start=(f == 0), stop=(f == FT - 1))
            mm.then_inc(self.projected, 1)

    def scalar(self, act):
        for f in range(FT):
            act.wait_ge(self.oF_in_psum, f + 1)
            act.activation(self.oF[:, f, :], self.ps[:, f, :], ACT.Copy).then_inc(self.oF_ready, 1)

    def vector(self, dve, steps):
        if self.bias is not None:
            for t in range(T):
                steps.mark(dve.tensor_tensor(self.x[:, t, :], self.x[:, t, :], self.bias[:, :], ALU.add))
            steps.settle()
        for h in range(2):
            dve.wait_ge(self.projected, h + 1)
            xs = self.x[:, 2 * h:2 * h + 2, :].rearrange("p t d -> p (t d)")
            dve.tensor_tensor(xs, xs, self.ps[:, 2 + h, :], ALU.add).then_inc(self.x_done, 1)


def load_x(sp, norm, x, src, b):
    sp.dma_start(x[:, :, :], src[b].rearrange("(t p) d -> p t d", p=P)).then_inc(norm.x_loaded, 16)


def store_x(sp, done, count, stored, x, dst, b):
    sp.wait_ge(done, count)
    sp.dma_start(dst[b].rearrange("(t p) d -> p t d", p=P), x[:, :, :]).then_inc(stored, 16)
    sp.wait_ge(stored, 16)


def load_constants(nc, st, tiles):
    loaded = st.sem("constants_loaded")
    with nc.Block() as block:
        @block.sync
        def _(sp):
            for tile, src in tiles:
                sp.dma_start(tile, src).then_inc(loaded, 16)
            sp.wait_ge(loaded, 16 * len(tiles))


def weight(st, tiles, name, src):
    n_in, n_out = src.shape
    if n_in <= P:
        t = st.sb(name, [n_in, n_out])
        tiles.append((t[:, :], src))
    else:
        t = st.sb(name, [P, n_in // P, n_out])
        tiles.append((t[:, :, :], src.rearrange("(f p) n -> p f n", p=P)))
    return t


def column(st, tiles, name, src):
    t = st.sb(name, [P, FT])
    tiles.append((t[:, :], src))
    return t


def constant(st, tiles, name, src, dt=F32):
    t = st.sb(name, list(src.shape), dt)
    tiles.append((t[tuple(slice(None) for _ in src.shape)], src))
    return t


def bias_row(st, tiles, name, src):
    t = st.sb(name, [P, D])
    tiles.append((t[:, :], src.rearrange("(o d) -> o d", o=1).to_broadcast([P, D])))
    return t


def write_ones(nc, att):
    with nc.Block() as block:
        @block.vector
        def _(dve):
            dve.memset(att.kst[STACK:STACK + SHIFT, :, :, :].rearrange("p a b c -> p (a b c)"), 1.0)

        @block.gpsimd
        def _(pool):
            pool.memset(att.v[:, :, :, HD:VW], 1.0)


def v_heads(ps_bank):
    return ps_bank.rearrange("p (t h d) -> p t h d", t=2, h=H)



def latent_attention(nc, w, x_src, x_dst, kscratch, qscratch):
    with ExitStack() as ctx:
        st = Stage(nc, ctx, "s1")
        ps = st.psum()
        loads = []
        identf = constant(st, loads, "identf", w["identf"])
        identb = constant(st, loads, "identb", w["identb"], BF16)
        tri = constant(st, loads, "tri", w["tri"], BF16)
        triT = constant(st, loads, "triT", w["triT"], BF16)
        wdkv = weight(st, loads, "wdkv", w["L0_attn_W_DKV"])
        wuk = weight(st, loads, "wuk", w["L0_attn_W_UK"])
        wuv = weight(st, loads, "wuv", w["L0_attn_W_UV"])
        wuq = weight(st, loads, "wuq", w["L0_attn_W_UQ"])
        wo = weight(st, loads, "wo", w["L0_attn_W_O"])
        x = st.sb("x", [P, T, D])
        latent = st.sb("latent", [64, S])
        norm = Norm(st, ps, x, identf)
        split = Split(st, S, 4)
        att = Attention(st, ps, identf, identb, norm.xn, S, NG, causal=True)
        proj = OutProjection(st, ps, identf, att.otok, norm.xnT[:, :, 1:], wo, x)
        latent_in_psum, latent_ready = st.sem("latent_in_psum"), st.sem("latent_ready")
        qk_in_psum, v_in_psum = st.sem("qk_in_psum"), st.sem("v_in_psum")
        dve_steps, act_steps, stored = st.sem("dve_steps"), st.sem("act_steps"), st.sem("stored")
        load_constants(nc, st, loads)
        write_ones(nc, att)
        items = [(0, False, 3), (0, True, 5), (1, False, 4), (1, True, 0)]

        def sync(sp, b):
            load_x(sp, norm, x, x_src, b)
            for i, (f, is_q, _) in enumerate(items):
                split.sync(sp, i, S, qscratch if is_q else kscratch, (8 * f, 8 * f + 8),
                           Q_LEVEL if is_q else K_LEVEL)
                if is_q:
                    for n in (i - 1, i):
                        sp.wait_ge(split.written[n], split.writes(n))
                    for g in (2 * f, 2 * f + 1):
                        att.load_stacks(sp, g, kscratch, qscratch, S)
            att.sync(sp)
            store_x(sp, proj.x_done, 2, stored, x, x_dst, b)

        def tensor(pe):
            norm.tensor(pe)
            for f in range(FT):
                pe.wait_ge(norm.xnT_ready, f + 1)
                mm = pe.matmul(ps[0:64, 2, :], wdkv[:, f, :], norm.xnT[:, f, 1:], start=(f == 0), stop=(f == 1))
            mm.then_inc(latent_in_psum, 1)
            for f, is_q, bank in items[1:2] + items[0:1] + items[3:4] + items[2:3]:
                if is_q:
                    for c in range(FT):
                        mm = pe.matmul(ps[:, bank, :], wuq[:, c, f * P:(f + 1) * P], norm.xnT[:, c, 1:],
                                       start=(c == 0), stop=(c == 1))
                else:
                    pe.wait_ge(latent_ready, 1)
                    mm = pe.matmul(ps[:, bank, :], wuk[:, f * P:(f + 1) * P], latent[:, :], start=True, stop=True)
                mm.then_inc(qk_in_psum, 1)
            for t in range(T):
                mm = pe.matmul(ps[:, 1 + t // 2, (t % 2) * D:(t % 2 + 1) * D], latent[:, t * P:(t + 1) * P],
                               wuv[:, :], start=True, stop=True)
                if t % 2:
                    mm.then_inc(v_in_psum, 1)
            pe.wait_ge(att.v_ready, 2)
            att.tensor(pe, tri=tri, triT=triT)
            proj.tensor(pe)

        def scalar(act):
            steps = Steps(act, act_steps)
            norm.scalar(act, steps)
            act.wait_ge(latent_in_psum, 1)
            act.activation(latent[:, :], ps[0:64, 2, :], ACT.Copy).then_inc(latent_ready, 1)
            for i, (f, is_q, bank) in enumerate(items):
                act.wait_ge(qk_in_psum, 2 * (i // 2) + 2)
                if i >= 2:
                    act.wait_ge(split.levels_ready, i - 1)
                act.activation(split.full[:, i % 2, :], ps[:, bank, :], ACT.Copy,
                               scale=HD ** -0.5 if is_q else 1.0).then_inc(split.full_ready, 1)
                split.scalar(act, i, S)
            for n in range(2):
                act.wait_ge(v_in_psum, n + 1)
                act.activation(att.v[:, 2 * n:2 * n + 2, :, 0:HD], v_heads(ps[:, 1 + n, :]), ACT.Copy)\
                    .then_inc(att.v_ready, 1)
            att.scalar(act)
            proj.scalar(act)

        def vector(dve):
            steps = Steps(dve, dve_steps)
            norm.vector(dve, steps)
            for i in range(4):
                split.vector(dve, steps, i, S)
            att.vector(dve, steps)
            dve.wait_ge(att.o_divided, NG)
            dve.sem_inc(proj.o_ready, 1)
            proj.vector(dve, steps)

        stage_loop(nc, st, {"sync": sync, "tensor": tensor, "scalar": scalar, "vector": vector})



def cross_attention(nc, w, x_src, x_dst, kscratch, qscratch):
    with ExitStack() as ctx:
        st = Stage(nc, ctx, "s2")
        ps = st.psum()
        loads = []
        identf = constant(st, loads, "identf", w["identf"])
        identb = constant(st, loads, "identb", w["identb"], BF16)
        wq = weight(st, loads, "wq", w["L0_xattn_Wq"])
        wk = weight(st, loads, "wk", w["L0_xattn_Wk"])
        wv = weight(st, loads, "wv", w["L0_xattn_Wv"])
        wo = weight(st, loads, "wo", w["L0_xattn_Wo"])
        bq = column(st, loads, "bq", w["L0_xattn_bq"])
        bk = column(st, loads, "bk", w["L0_xattn_bk"])
        bv = bias_row(st, loads, "bv", w["L0_xattn_bv"])
        bo = bias_row(st, loads, "bo", w["L0_xattn_bo"])
        x = st.sb("x", [P, T, D])
        ctxT = st.sb("ctxT", [P, FT, CTX])
        maskq = st.sb("maskq", [P, T, CTX])
        keys = tiles_of(CTX)
        full, tail = len(keys) - 1, keys[-1][1]
        maskT = st.sb("maskT", [P, len(keys), S])
        norm = Norm(st, ps, x, identf)
        split = Split(st, CTX, 4)
        att = Attention(st, ps, identf, identb, norm.xn, CTX, NG, causal=False, masked=True)
        proj = OutProjection(st, ps, identf, att.otok, norm.xnT[:, :, 1:], wo, x, bias=bo)
        ctx_loaded, mask_loaded = st.sem("ctx_loaded"), st.sem("mask_loaded")
        proj_in_psum, proj_copied = st.sem("proj_in_psum"), st.sem("proj_copied")
        dve_steps, act_steps, stored = st.sem("dve_steps"), st.sem("act_steps"), st.sem("stored")
        load_constants(nc, st, loads)
        write_ones(nc, att)
        bank_of = (2, 3, 4, 5)
        pieces = [(c, min(512, CTX - c)) for c in range(0, CTX, 512)]
        jobs = []
        for f in range(FT):
            jobs += [("k", f, c, n) for c, n in pieces]
            jobs += [("q", f, 0, S)]
        jobs += [("v", k, 0, n) for k, (_, n) in enumerate(keys)]
        items = [(0, False), (0, True), (1, False), (1, True)]

        def sync(sp, b):
            for f in range(FT):
                sp.dma_start(ctxT[:, f, :], w["ctxT"][b, f * P:(f + 1) * P, :]).then_inc(ctx_loaded, 16)
            load_x(sp, norm, x, x_src, b)
            sp.dma_start(maskq[:, :, :], w["mask"][b].rearrange("(t p) k -> p t k", p=P)).then_inc(mask_loaded, 16)
            sp.dma_start(maskT[:, 0:full, :],
                         w["maskT"][b, 0:full * P, :].rearrange("(k p) q -> p k q", p=P)).then_inc(mask_loaded, 16)
            sp.dma_start(maskT[0:tail, full, :], w["maskT"][b, full * P:CTX, :]).then_inc(mask_loaded, 16)
            for i, (f, is_q) in enumerate(items):
                split.sync(sp, i, S if is_q else CTX, qscratch if is_q else kscratch, (8 * f, 8 * f + 8),
                           Q_LEVEL if is_q else K_LEVEL)
                if is_q:
                    for n in (i - 1, i):
                        sp.wait_ge(split.written[n], split.writes(n))
                    if f == 0:
                        for g in (0, 1):
                            att.load_stacks(sp, g, kscratch, qscratch, CTX)
            att.sync(sp, refill=(kscratch, qscratch, CTX))
            store_x(sp, proj.x_done, 2, stored, x, x_dst, b)

        def tensor(pe):
            norm.tensor(pe)
            for i, (kind, f, c, n) in enumerate(jobs):
                if i == 0:
                    pe.wait_ge(ctx_loaded, 32)
                if i >= 4:
                    pe.wait_ge(proj_copied, i - 3)
                bank = bank_of[i % 4]
                for h in range(FT):
                    first, last = h == 0, h == FT - 1
                    if kind == "k":
                        mm = pe.matmul(ps[:, bank, 0:n], wk[:, h, f * P:(f + 1) * P], ctxT[:, h, c:c + n],
                                       start=first, stop=last)
                    elif kind == "q":
                        pe.wait_ge(norm.xnT_ready, FT)
                        mm = pe.matmul(ps[:, bank, :], wq[:, h, f * P:(f + 1) * P], norm.xnT[:, h, 1:],
                                       start=first, stop=last)
                    else:
                        mm = pe.matmul(ps[0:n, bank, 0:D], ctxT[:, h, keys[f][0]:keys[f][0] + n], wv[:, h, :],
                                       start=first, stop=last)
                mm.then_inc(proj_in_psum, 1)
            pe.wait_ge(mask_loaded, 48)
            pe.wait_ge(proj_copied, len(jobs))
            att.tensor(pe, maskT=maskT)
            proj.tensor(pe)

        def scalar(act):
            steps = Steps(act, act_steps)
            norm.scalar(act, steps)
            item = 0
            for i, (kind, f, c, n) in enumerate(jobs):
                bank = bank_of[i % 4]
                act.wait_ge(proj_in_psum, i + 1)
                if kind == "v":
                    act.activation(att.v[0:n, f, :, 0:HD], ps[0:n, bank, 0:D].rearrange("p (h d) -> p h d", h=H),
                                   ACT.Copy).then_inc(proj_copied, 1)
                    continue
                if item >= 2 and c == 0:
                    act.wait_ge(split.levels_ready, item - 1)
                act.activation(split.full[:, item % 2, c:c + n], ps[:, bank, 0:n], ACT.Identity,
                               bias=(bk if kind == "k" else bq)[:, f:f + 1]).then_inc(proj_copied, 1)
                if c + n == (CTX if kind == "k" else S):
                    act.wait_ge(proj_copied, i + 1)
                    if kind == "q":
                        steps.mark(act.activation(split.full[:, item % 2, 0:S], split.full[:, item % 2, 0:S],
                                                  ACT.Copy, scale=HD ** -0.5))
                        steps.settle()
                    act.sem_inc(split.full_ready, 1)
                    split.scalar(act, item, c + n)
                    item += 1
            att.scalar(act)
            proj.scalar(act)

        def vector(dve):
            steps = Steps(dve, dve_steps)
            norm.vector(dve, steps)
            for i, (f, is_q) in enumerate(items):
                split.vector(dve, steps, i, S if is_q else CTX)
            dve.wait_ge(mask_loaded, 48)
            att.vector(dve, steps, maskq=maskq, vbias=bv)
            dve.sem_inc(proj.o_ready, 1)
            proj.vector(dve, steps)

        stage_loop(nc, st, {"sync": sync, "tensor": tensor, "scalar": scalar, "vector": vector})



def channel_mix(nc, w, x_src, x_dst):
    with ExitStack() as ctx:
        st = Stage(nc, ctx, "s3")
        ps = st.psum()
        loads = []
        identf = constant(st, loads, "identf", w["identf"])
        wr = weight(st, loads, "wr", w["L0_ffn_W_r"])
        wk = weight(st, loads, "wk", w["L0_ffn_W_k"])
        wv = weight(st, loads, "wv", w["L0_ffn_W_v"])
        mu_r = column(st, loads, "mu_r", w["L0_ffn_mu_r"])
        mu_k = column(st, loads, "mu_k", w["L0_ffn_mu_k"])
        x = st.sb("x", [P, T, D])
        norm = Norm(st, ps, x, identf)
        step = st.sb("step", [P, FT, S])
        xr, xk = st.sb("xr", [P, FT, S]), st.sb("xk", [P, FT, S])
        act_k = st.sb("act_k", [P, FT, S])
        gate = st.sb("gate", [P, T, D])
        part = st.sb("part", [P, T, D])
        xk_ready, xr_ready = st.sem("xk_ready"), st.sem("xr_ready")
        k_in_psum, k_relu, act_k_ready = st.sem("k_in_psum"), st.sem("k_relu"), st.sem("act_k_ready")
        r_in_psum, gate_ready, v_in_psum = st.sem("r_in_psum"), st.sem("gate_ready"), st.sem("v_in_psum")
        x_done, gated = st.sem("x_done"), st.sem("gated")
        dve_steps, act_steps, stored = st.sem("dve_steps"), st.sem("act_steps"), st.sem("stored")
        load_constants(nc, st, loads)
        with nc.Block() as block:
            @block.vector
            def _(dve):
                dve.memset(norm.xnT[:, :, 0:1], 0.0)

        def sync(sp, b):
            load_x(sp, norm, x, x_src, b)
            store_x(sp, x_done, 2, stored, x, x_dst, b)

        def tensor(pe):
            norm.tensor(pe)
            for f in range(FT):
                for c in range(FT):
                    if f == 0:
                        pe.wait_ge(xk_ready, c + 1)
                    mm = pe.matmul(ps[:, 2 + f, :], wk[:, c, f * P:(f + 1) * P], xk[:, c, :],
                                   start=(c == 0), stop=(c == 1))
                mm.then_inc(k_in_psum, 1)
            pe.wait_ge(xr_ready, FT)
            for src, wt, base, done in ((xr, wr, 4, r_in_psum), (act_k, wv, 6, v_in_psum)):
                for t in range(T):
                    for c in range(FT):
                        if src is act_k and t == 0:
                            pe.wait_ge(act_k_ready, c + 1)
                        mm = pe.matmul(ps[:, base + t // 2, (t % 2) * D:(t % 2 + 1) * D],
                                       src[:, c, t * P:(t + 1) * P], wt[:, c, :], start=(c == 0), stop=(c == 1))
                    if t % 2:
                        mm.then_inc(done, 1)

        def scalar(act):
            steps = Steps(act, act_steps)
            norm.scalar(act, steps)
            for f in range(FT):
                act.wait_ge(k_in_psum, f + 1)
                act.activation(act_k[:, f, :], ps[:, 2 + f, :], ACT.Relu).then_inc(k_relu, 1)
            for f in range(FT):
                act.wait_ge(k_relu, f + 1)
                act.activation(act_k[:, f, :], act_k[:, f, :], ACT.Square).then_inc(act_k_ready, 1)
            for h in range(2):
                act.wait_ge(r_in_psum, h + 1)
                act.activation(gate[:, 2 * h:2 * h + 2, :], ps[:, 4 + h, :].rearrange("p (t d) -> p t d", t=2),
                               ACT.Tanh, scale=0.5).then_inc(gate_ready, 1)

        def vector(dve):
            steps = Steps(dve, dve_steps)
            norm.vector(dve, steps)
            for f in range(FT):
                dve.wait_ge(norm.xnT_ready, f + 1)
                cur, prev = norm.xnT[:, f, 1:S + 1], norm.xnT[:, f, 0:S]
                steps.mark(dve.tensor_tensor(step[:, f, :], cur, prev, ALU.subtract))
                steps.settle()
                dve.scalar_tensor_tensor(out=xk[:, f, :], in0=step[:, f, :], scalar=mu_k[:, f:f + 1], in1=prev,
                                         op0=ALU.mult, op1=ALU.add).then_inc(xk_ready, 1)
            for f in range(FT):
                dve.scalar_tensor_tensor(out=xr[:, f, :], in0=step[:, f, :], scalar=mu_r[:, f:f + 1],
                                         in1=norm.xnT[:, f, 0:S], op0=ALU.mult, op1=ALU.add).then_inc(xr_ready, 1)
            for h in range(2):
                dve.wait_ge(gate_ready, h + 1)
                dve.wait_ge(v_in_psum, h + 1)
                two = slice(2 * h, 2 * h + 2)
                dve.scalar_tensor_tensor(out=part[:, two, :], in0=gate[:, two, :], scalar=1.0,
                                         in1=ps[:, 6 + h, :].rearrange("p (t d) -> p t d", t=2), op0=ALU.add,
                                         op1=ALU.mult).then_inc(gated, 1)
                dve.wait_ge(gated, h + 1)
                dve.scalar_tensor_tensor(out=x[:, two, :], in0=part[:, two, :], scalar=0.5, in1=x[:, two, :],
                                         op0=ALU.mult, op1=ALU.add).then_inc(x_done, 1)

        stage_loop(nc, st, {"sync": sync, "tensor": tensor, "scalar": scalar, "vector": vector})



def linear_attention(nc, w, x_src, x_dst):
    with ExitStack() as ctx:
        st = Stage(nc, ctx, "s5")
        ps = st.psum()
        loads = []
        identf = constant(st, loads, "identf", w["identf"])
        blocks = constant(st, loads, "blocks", w["blocks"])
        wq = weight(st, loads, "wq", w["L1_xattn_Wq"])
        wk = weight(st, loads, "wk", w["L1_xattn_Wk"])
        wv = weight(st, loads, "wv", w["L1_xattn_Wv"])
        wo = weight(st, loads, "wo", w["L1_xattn_Wo"])
        bq = column(st, loads, "bq", w["L1_xattn_bq"])
        bk = bias_row(st, loads, "bk", w["L1_xattn_bk"])
        bv = bias_row(st, loads, "bv", w["L1_xattn_bv"])
        bo = bias_row(st, loads, "bo", w["L1_xattn_bo"])
        keys = tiles_of(CTX)
        x = st.sb("x", [P, T, D])
        ctxT = st.sb("ctxT", [P, FT, CTX])
        norm = Norm(st, ps, x, identf)
        kraw = st.sb("kraw", [P, 2, D])
        kexp = st.sb("kexp", [P, 2, D])
        k = st.sb("k", [P, 2, D])
        ksq = st.sb("ksq", [P, 2, D])
        v = st.sb("v", [P, 2, D])
        ones = st.sb("ones", [P, 1])
        qraw, qexp = st.sb("qraw", [P, FT, S]), st.sb("qexp", [P, FT, S])
        q, qsq, qn = st.sb("q", [P, FT, S]), st.sb("qsq", [P, FT, S]), st.sb("qn", [P, FT, S])
        kv = st.sb("kv", [P, FT, P])
        knorm, kinv = st.sb("knorm", [P, FT]), st.sb("kinv", [P, FT])
        proj = OutProjection(st, ps, identf, norm.xn, st.sb("oF", [P, FT, S]), wo, x, bias=bo)
        ctx_loaded = st.sem("ctx_loaded")
        kv_in_psum, kraw_ready, kexp_ready = st.sem("kv_in_psum"), st.sem("kraw_ready"), st.sem("kexp_ready")
        k_ready, v_ready, ksq_ready = st.sem("k_ready"), st.sem("v_ready"), st.sem("ksq_ready")
        kv_added, ones_ready = st.sem("kv_added"), st.sem("ones_ready")
        q_in_psum, qraw_ready, qexp_ready = st.sem("q_in_psum"), st.sem("qraw_ready"), st.sem("qexp_ready")
        q_ready, qsq_ready, qsum_in_psum = st.sem("q_ready"), st.sem("qsq_ready"), st.sem("qsum_in_psum")
        qinv_ready, qn_ready, kv_ready = st.sem("qinv_ready"), st.sem("qn_ready"), st.sem("kv_ready")
        ksum_copied, kinv_ready = st.sem("ksum_copied"), st.sem("kinv_ready")
        dve_steps, act_steps, stored = st.sem("dve_steps"), st.sem("act_steps"), st.sem("stored")
        load_constants(nc, st, loads)
        with nc.Block() as block:
            @block.vector
            def _(dve):
                dve.memset(ones[:, :], 1.0)

        def sync(sp, b):
            for f in range(FT):
                sp.dma_start(ctxT[:, f, :], w["ctxT"][b, f * P:(f + 1) * P, :]).then_inc(ctx_loaded, 16)
            load_x(sp, norm, x, x_src, b)
            store_x(sp, proj.x_done, 2, stored, x, x_dst, b)

        def tensor(pe):
            norm.tensor(pe)
            pe.wait_ge(ctx_loaded, 32)

            def accumulate(i):
                n = keys[i][1]
                pe.wait_ge(k_ready, i + 1)
                pe.wait_ge(v_ready, i + 1)
                pe.wait_ge(ksq_ready, i + 1)
                for f in range(FT):
                    pe.matmul(ps[:, 4 + f, 0:P], k[0:n, i % 2, f * P:(f + 1) * P], v[0:n, i % 2, f * P:(f + 1) * P],
                              start=(i == 0), stop=(i == len(keys) - 1))
                for f in range(FT):
                    mm = pe.matmul(ps[:, 6 + f, 0:1], ksq[0:n, i % 2, f * P:(f + 1) * P], ones[0:n, :],
                                   start=(i == 0), stop=(i == len(keys) - 1))
                mm.then_inc(kv_added, 1)

            for i, (k0, n) in enumerate(keys):
                if i >= 2:
                    pe.wait_ge(kraw_ready, i - 1)
                    pe.wait_ge(v_ready, i - 1)
                for c, wt in enumerate((wk, wv)):
                    for f in range(FT):
                        mm = pe.matmul(ps[0:n, 2 + i % 2, c * D:(c + 1) * D], ctxT[:, f, k0:k0 + n], wt[:, f, :],
                                       start=(f == 0), stop=(f == 1))
                mm.then_inc(kv_in_psum, 1)
                if i >= 1:
                    accumulate(i - 1)
            pe.wait_ge(norm.xnT_ready, FT)
            for f in range(FT):
                for c in range(FT):
                    mm = pe.matmul(ps[:, f, :], wq[:, c, f * P:(f + 1) * P], norm.xnT[:, c, 1:],
                                   start=(c == 0), stop=(c == 1))
                mm.then_inc(q_in_psum, 1)
            accumulate(len(keys) - 1)
            pe.wait_ge(kraw_ready, len(keys))
            pe.wait_ge(v_ready, len(keys))
            for f in range(FT):
                pe.wait_ge(qsq_ready, f + 1)
                pe.matmul(ps[:, 2 + f, :], blocks[:, :], qsq[:, f, :], start=True, stop=True)\
                    .then_inc(qsum_in_psum, 1)
            for f in range(FT):
                pe.wait_ge(qn_ready, f + 1)
                pe.wait_ge(kv_ready, f + 1)
                pe.matmul(ps[:, f, :], kv[:, f, :], qn[:, f, :], start=True, stop=True)\
                    .then_inc(proj.oF_in_psum, 1)
            pe.wait_ge(qinv_ready, FT)
            proj.tensor(pe, turn=False)

        def scalar(act):
            steps = Steps(act, act_steps)
            norm.scalar(act, steps)
            for i, (k0, n) in enumerate(keys):
                act.wait_ge(kraw_ready, i + 1)
                if i >= 2:
                    act.wait_ge(k_ready, i - 1)
                act.activation(kexp[0:n, i % 2, :], kraw[0:n, i % 2, :], ACT.Exp).then_inc(kexp_ready, 1)
                act.wait_ge(k_ready, i + 1)
                if i >= 2:
                    act.wait_ge(kv_added, i - 1)
                act.activation(ksq[0:n, i % 2, :], k[0:n, i % 2, :], ACT.Square).then_inc(ksq_ready, 1)
            for f in range(FT):
                act.wait_ge(q_in_psum, f + 1)
                act.activation(qraw[:, f, :], ps[:, f, :], ACT.Identity, bias=bq[:, f:f + 1])\
                    .then_inc(qraw_ready, 1)
            for f in range(FT):
                act.wait_ge(qraw_ready, f + 1)
                act.activation(qexp[:, f, :], qraw[:, f, :], ACT.Exp).then_inc(qexp_ready, 1)
            for f in range(FT):
                act.wait_ge(q_ready, f + 1)
                act.activation(qsq[:, f, :], q[:, f, :], ACT.Square).then_inc(qsq_ready, 1)
            for f in range(FT):
                act.wait_ge(qsum_in_psum, f + 1)
                steps.mark(act.activation(qsq[:, f, :], ps[:, 2 + f, :], ACT.Ln, scale=float(HD)))
                steps.settle()
                act.activation(qsq[:, f, :], qsq[:, f, :], ACT.Exp, scale=-0.5).then_inc(qinv_ready, 1)
            act.wait_ge(ksum_copied, FT)
            steps.mark(act.activation(knorm[:, :], knorm[:, :], ACT.Ln, scale=float(S)))
            steps.settle()
            act.activation(kinv[:, :], knorm[:, :], ACT.Exp, scale=-0.5).then_inc(kinv_ready, 1)
            proj.scalar(act)

        def vector(dve):
            steps = Steps(dve, dve_steps)
            norm.vector(dve, steps)

            def elu(i, n):
                dve.wait_ge(kexp_ready, i + 1)
                steps.mark(dve.tensor_scalar(kraw[0:n, i % 2, :], kraw[0:n, i % 2, :], 0.0, -1.0, ALU.max, ALU.add))
                steps.settle()
                dve.scalar_tensor_tensor(out=k[0:n, i % 2, :], in0=kexp[0:n, i % 2, :], scalar=1.0,
                                         in1=kraw[0:n, i % 2, :], op0=ALU.min, op1=ALU.add).then_inc(k_ready, 1)

            for i, (k0, n) in enumerate(keys):
                dve.wait_ge(kv_in_psum, i + 1)
                if i >= 2:
                    dve.wait_ge(kv_added, i - 1)
                    dve.wait_ge(ksq_ready, i - 1)
                dve.tensor_tensor(kraw[0:n, i % 2, :], ps[0:n, 2 + i % 2, 0:D], bk[0:n, :], ALU.add)\
                    .then_inc(kraw_ready, 1)
                dve.tensor_tensor(v[0:n, i % 2, :], ps[0:n, 2 + i % 2, D:2 * D], bv[0:n, :], ALU.add)\
                    .then_inc(v_ready, 1)
                elu(i, n)
            for f in range(FT):
                dve.wait_ge(qexp_ready, f + 1)
                steps.mark(dve.tensor_scalar(qraw[:, f, :], qraw[:, f, :], 0.0, -1.0, ALU.max, ALU.add))
                steps.settle()
                dve.scalar_tensor_tensor(out=q[:, f, :], in0=qexp[:, f, :], scalar=1.0, in1=qraw[:, f, :],
                                         op0=ALU.min, op1=ALU.add).then_inc(q_ready, 1)
            dve.wait_ge(kv_added, len(keys))
            for f in range(FT):
                dve.tensor_copy(knorm[:, f:f + 1], ps[:, 6 + f, 0:1]).then_inc(ksum_copied, 1)
            dve.wait_ge(kinv_ready, 1)
            for f in range(FT):
                dve.scalar_tensor_tensor(out=kv[:, f, :], in0=ps[:, 4 + f, 0:P], scalar=kinv[:, f:f + 1],
                                         in1=blocks[:, :], op0=ALU.mult, op1=ALU.mult).then_inc(kv_ready, 1)
            for f in range(FT):
                dve.wait_ge(qinv_ready, f + 1)
                dve.tensor_tensor(qn[:, f, :], q[:, f, :], qsq[:, f, :], ALU.mult).then_inc(qn_ready, 1)
            proj.vector(dve, steps)

        stage_loop(nc, st, {"sync": sync, "tensor": tensor, "scalar": scalar, "vector": vector})



class Rotary:

    BANKS = ((2, 3), (4, 5), (6, 7), (0, 1))

    def __init__(self, st, ps, split, cos, sin):
        self.ps, self.split, self.cos, self.sin = ps, split, cos, sin
        self.part = st.sb("rot_part", [P, 2, S])
        self.in_psum = st.sem("rot_in_psum")
        self.read = st.sem("rot_read")
        self.part_ready = st.sem("rot_part_ready")

    def vector(self, dve, steps, i, scale):
        a, b = self.BANKS[i]
        full = self.split.full[:, i % 2, :]
        dve.wait_ge(self.in_psum, i + 1)
        steps.settle()
        steps.mark(dve.scalar_tensor_tensor(out=full, in0=self.ps[:, a, :], scalar=scale, in1=self.cos[:, :],
                                            op0=ALU.mult, op1=ALU.mult))
        dve.scalar_tensor_tensor(out=self.part[:, i % 2, :], in0=self.ps[:, b, :], scalar=scale,
                                 in1=self.sin[:, :], op0=ALU.mult, op1=ALU.mult).then_inc(self.read, 1)
        steps.settle()
        dve.wait_ge(self.read, i + 1)
        steps.mark(dve.tensor_tensor(full, full, self.part[:, i % 2, :], ALU.add))
        steps.settle()


ITEMS = ((0, False), (0, True), (1, False), (1, True))


def sync_self_attention(sp, att, split, kscratch, qscratch, groups_of):
    for i, (f, is_q) in enumerate(ITEMS):
        split.sync(sp, i, S, qscratch if is_q else kscratch, (8 * f, 8 * f + 8), Q_LEVEL if is_q else K_LEVEL)
        if is_q:
            for n in (i - 1, i):
                sp.wait_ge(split.written[n], split.writes(n))
            for g in groups_of[f]:
                att.load_stacks(sp, g, kscratch, qscratch, S)



def rotary_latent_attention(nc, w, x_src, x_dst, kscratch, qscratch):
    with ExitStack() as ctx:
        st = Stage(nc, ctx, "s6")
        ps = st.psum()
        loads = []
        identf = constant(st, loads, "identf", w["identf"])
        identb = constant(st, loads, "identb", w["identb"], BF16)
        tri = constant(st, loads, "tri", w["tri"], BF16)
        triT = constant(st, loads, "triT", w["triT"], BF16)
        cos = constant(st, loads, "cos", w["mla_cos"])
        sin = constant(st, loads, "sin", w["mla_sin"])
        w_ln = column(st, loads, "w_ln", w["L1_ffn_w_ln1"])
        wkvd = weight(st, loads, "wkvd", w["L1_ffn_W_kvd"])
        wqd = weight(st, loads, "wqd", w["L1_ffn_W_qd"])
        wku = weight(st, loads, "wku", w["mla_wku"])
        wkr = weight(st, loads, "wkr", w["mla_wkr"])
        wkr_p = weight(st, loads, "wkr_p", w["mla_wkr_partner"])
        wq = weight(st, loads, "wq", w["mla_wq"])
        wq_p = weight(st, loads, "wq_p", w["mla_wq_partner"])
        wvu = weight(st, loads, "wvu", w["L1_ffn_W_vu"])
        wo = weight(st, loads, "wo", w["L1_ffn_W_o"])
        x = st.sb("x", [P, T, D])
        kv_latent, q_latent = st.sb("kv_latent", [64, S]), st.sb("q_latent", [64, S])
        norm = Norm(st, ps, x, identf, rms=True, weight=w_ln)
        split = Split(st, S, 4)
        rotary = Rotary(st, ps, split, cos, sin)
        att = Attention(st, ps, identf, identb, norm.xn, S, NG, causal=True)
        proj = OutProjection(st, ps, identf, att.otok, norm.xnT[:, :, 1:], wo, x)
        latent_in_psum, latent_ready = st.sem("latent_in_psum"), st.sem("latent_ready")
        v_in_psum = st.sem("v_in_psum")
        dve_steps, act_steps, stored = st.sem("dve_steps"), st.sem("act_steps"), st.sem("stored")
        load_constants(nc, st, loads)
        write_ones(nc, att)

        def sync(sp, b):
            load_x(sp, norm, x, x_src, b)
            sync_self_attention(sp, att, split, kscratch, qscratch, ((0, 1), (2, 3)))
            att.sync(sp)
            store_x(sp, proj.x_done, 2, stored, x, x_dst, b)

        def tensor(pe):
            norm.tensor(pe)
            pe.wait_ge(norm.xnT_ready, FT)
            xnT = norm.xnT[:, :, 1:]
            for bank, wt in ((0, wkvd), (1, wqd)):
                for c in range(FT):
                    mm = pe.matmul(ps[0:64, bank, :], wt[:, c, :], xnT[:, c, :], start=(c == 0), stop=(c == 1))
                mm.then_inc(latent_in_psum, 1)
            for i, (f, is_q) in enumerate(ITEMS):
                cols = slice(f * P, (f + 1) * P)
                a, b = rotary.BANKS[i]
                if i == 0:
                    pe.wait_ge(latent_ready, 2)
                if is_q:
                    pe.matmul(ps[:, a, :], wq[:, cols], q_latent[:, :], start=True, stop=True)
                    mm = pe.matmul(ps[:, b, :], wq_p[:, cols], q_latent[:, :], start=True, stop=True)
                else:
                    pe.matmul(ps[:, a, :], wku[:, cols], kv_latent[:, :], start=True, stop=False)
                    for c in range(FT):
                        pe.matmul(ps[:, a, :], wkr[:, c, cols], xnT[:, c, :], start=False, stop=(c == 1))
                    for c in range(FT):
                        mm = pe.matmul(ps[:, b, :], wkr_p[:, c, cols], xnT[:, c, :], start=(c == 0), stop=(c == 1))
                mm.then_inc(rotary.in_psum, 1)
            pe.wait_ge(rotary.read, 1)
            for t in range(T):
                mm = pe.matmul(ps[:, 2 + t // 2, (t % 2) * D:(t % 2 + 1) * D], kv_latent[:, t * P:(t + 1) * P],
                               wvu[:, :], start=True, stop=True)
                if t % 2:
                    mm.then_inc(v_in_psum, 1)
            pe.wait_ge(att.v_ready, 2)
            pe.wait_ge(rotary.read, 4)
            att.tensor(pe, tri=tri, triT=triT)
            proj.tensor(pe)

        def scalar(act):
            steps = Steps(act, act_steps)
            norm.outer_scalar(act, steps)
            norm.scalar(act, steps)
            for n, dst in enumerate((kv_latent, q_latent)):
                act.wait_ge(latent_in_psum, n + 1)
                act.activation(dst[:, :], ps[0:64, n, :], ACT.Copy).then_inc(latent_ready, 1)
            for i in range(4):
                split.scalar(act, i, S)
                if i == 1:
                    for n in range(2):
                        act.wait_ge(v_in_psum, n + 1)
                        act.activation(att.v[:, 2 * n:2 * n + 2, :, 0:HD], v_heads(ps[:, 2 + n, :]), ACT.Copy)\
                            .then_inc(att.v_ready, 1)
            att.scalar(act)
            proj.scalar(act)

        def vector(dve):
            steps = Steps(dve, dve_steps)
            norm.outer_vector(dve, steps)
            norm.vector(dve, steps)
            for i, (f, is_q) in enumerate(ITEMS):
                rotary.vector(dve, steps, i, HD ** -0.5 if is_q else 1.0)
                dve.sem_inc(split.full_ready, 1)
                split.vector(dve, steps, i, S)
            att.vector(dve, steps)
            dve.wait_ge(att.o_divided, NG)
            dve.sem_inc(proj.o_ready, 1)
            proj.vector(dve, steps)

        stage_loop(nc, st, {"sync": sync, "tensor": tensor, "scalar": scalar, "vector": vector})



class Hyperbolic:

    ROWS = STACK + NSLOT

    def __init__(self, st, ps, identf, trif, att, root_c, eps_c):
        self.ps, self.identf, self.trif, self.att, self.root_c, self.eps_c = ps, identf, trif, att, root_c, eps_c
        self.off = [0, P, 3 * P, 6 * P]
        self.cols = 10 * P
        self.kst = st.sb("hyp_k", [self.ROWS, GH, S], BF16)
        self.qst = st.sb("hyp_q", [self.ROWS, GH, S], BF16)
        self.u = st.sb("hyp_u", [P, 2, self.cols])
        self.root = st.sb("hyp_root", [P, 2, self.cols])
        self.nmax = st.sb("hyp_nmax", [P, 2, T])
        self.bias = st.sb("hyp_bias", [P, 2, T])
        self.pT = st.sb("hyp_pT", [P, 2, T, S])
        self.oT = st.sb("hyp_oT", [P, S])
        self.inv = st.sb("hyp_inv", [P, T, GH])
        self.loaded = st.sem("hyp_loaded")
        self.scored = st.sem("hyp_scored")
        self.u_ready = st.sem("hyp_u_ready")
        self.square_ready = st.sem("hyp_square_ready")
        self.root_ready = st.sem("hyp_root_ready")
        self.sum_ready = st.sem("hyp_sum_ready")
        self.score_ready = st.sem("hyp_score_ready")
        self.bias_ready = st.sem("hyp_bias_ready")
        self.probs_ready = st.sem("hyp_probs_ready")
        self.turned = st.sem("hyp_turned")
        self.pT_ready = st.sem("hyp_pT_ready")
        self.pv_done = st.sem("hyp_pv_done")
        self.oT_copied, self.o_turned = st.sem("hyp_oT_copied"), st.sem("hyp_o_turned")
        self.o_divided = st.sem("hyp_o_divided")

    @staticmethod
    def turned_place(k):
        return ((4, 0), (5, 0), (6, 0), (5, 3 * P))[k]

    def tensor(self, pe):
        ps = self.ps

        def score(j):
            if j == 0:
                pe.wait_ge(self.loaded, 64)
            for t in range(T):
                if j >= 1:
                    pe.wait_ge(self.u_ready, T * (j - 1) + t + 1)
                n = (t + 1) * P
                pe.matmul(ps[:, t, 0:n], self.qst[:, j, t * P:n], self.kst[:, j, 0:n], start=True, stop=True)\
                    .then_inc(self.scored, 1)

        def turn(j):
            pe.wait_ge(self.probs_ready, T * (j + 1))
            if j >= 1:
                pe.wait_ge(self.pT_ready, T * j)
            for k in range(T):
                bank, c0 = self.turned_place(k)
                for t in range(k, T):
                    mm = pe.transpose(ps[:, bank, c0 + (t - k) * P:c0 + (t - k + 1) * P],
                                      self.u[:, j % 2, self.off[t] + k * P:self.off[t] + (k + 1) * P],
                                      self.identf[:, :])
                mm.then_inc(self.turned, 1)

        def pv(j):
            for k in range(T):
                pe.wait_ge(self.pT_ready, T * j + k + 1)
                mm = pe.matmul(ps[VW * j:VW * (j + 1), 7, k * P:S], self.att.v[:, k, H - GH + j, :],
                               self.pT[:, j % 2, k, k * P:S], start=(k == 0), stop=(k == T - 1))
            mm.then_inc(self.pv_done, 1)

        score(0)
        for j in range(GH):
            if j + 1 < GH:
                score(j + 1)
            turn(j)
            if j >= 1:
                pv(j - 1)
        pv(GH - 1)
        pe.wait_ge(self.oT_copied, 1)
        for t in range(T):
            mm = pe.transpose(ps[:, 0, t * P:(t + 1) * P], self.oT[:, t * P:(t + 1) * P], self.identf[:, :])
        mm.then_inc(self.o_turned, 1)

    def vector(self, dve, steps):
        ps = self.ps

        def excess(j):
            u = self.u[:, j % 2, :]
            for t in range(T):
                dve.wait_ge(self.scored, T * j + t + 1)
                if j >= 2 and t == 0:
                    dve.wait_ge(self.turned, T * (j - 1))
                dve.tensor_scalar(u[:, self.off[t]:self.off[t] + (t + 1) * P], ps[:, t, 0:(t + 1) * P],
                                  -1.0, TINY, ALU.add, ALU.max).then_inc(self.u_ready, 1)
            dve.wait_ge(self.u_ready, T * (j + 1))
            dve.scalar_tensor_tensor(out=self.root[:, j % 2, :], in0=u, scalar=2.0, in1=u, op0=ALU.add,
                                     op1=ALU.mult).then_inc(self.square_ready, 1)

        def add_root(j):
            dve.wait_ge(self.root_ready, j + 1)
            u = self.u[:, j % 2, :]
            dve.tensor_tensor(u, u, self.root[:, j % 2, :], ALU.add).then_inc(self.sum_ready, 1)

        def maxima(j):
            dve.wait_ge(self.score_ready, j + 1)
            for t in range(T):
                own = self.u[:, j % 2, self.off[t] + t * P:self.off[t] + (t + 1) * P]
                steps.mark(dve.tensor_tensor(own, own, self.trif[:, :], ALU.add))
            steps.settle()
            for t in range(T):
                steps.mark(dve.tensor_reduce(self.nmax[:, j % 2, t:t + 1],
                                             self.u[:, j % 2, self.off[t]:self.off[t] + (t + 1) * P], AX.X,
                                             ALU.max, negate=True))
            steps.settle()
            dve.tensor_scalar(self.bias[:, j % 2, :], self.nmax[:, j % 2, :], self.root_c[:, j:j + 1], None,
                              ALU.mult).then_inc(self.bias_ready, 1)

        excess(0)
        for j in range(GH):
            add_root(j)
            if j + 1 < GH:
                excess(j + 1)
            maxima(j)
        dve.wait_ge(self.o_turned, 1)
        o = ps[:, 0, :].rearrange("p (t j w) -> p t j w", t=T, j=GH)
        steps.mark(dve.reciprocal(self.inv[:, :, :], o[:, :, :, HD]))
        steps.settle()
        out = self.att.otok[:, :, D - GH * HD:D].rearrange("p t (j d) -> p t j d", j=GH)
        inv = self.inv[:, :, :].rearrange("p t (j o) -> p t j o", o=1).to_broadcast([P, T, GH, HD])
        dve.tensor_tensor(out, o[:, :, :, 0:HD], inv, ALU.mult).then_inc(self.o_divided, 1)

    def scalar(self, act, steps):
        def root(j):
            r = self.root[:, j % 2, :]
            act.wait_ge(self.square_ready, j + 1)
            steps.mark(act.activation(r, r, ACT.Ln))
            steps.settle()
            act.activation(r, r, ACT.Exp, scale=0.5).then_inc(self.root_ready, 1)

        def score(j):
            u = self.u[:, j % 2, :]
            act.wait_ge(self.sum_ready, j + 1)
            steps.mark(act.activation(u, u, ACT.Ln, bias=1.0))
            steps.settle()
            steps.mark(act.activation(u, u, ACT.Ln, bias=self.eps_c[:, j:j + 1]))
            steps.settle()
            act.activation(u, u, ACT.Exp, scale=-1.0).then_inc(self.score_ready, 1)

        def probs(j):
            act.wait_ge(self.bias_ready, j + 1)
            for t in range(T):
                u = self.u[:, j % 2, self.off[t]:self.off[t] + (t + 1) * P]
                act.activation(u, u, ACT.Exp, bias=self.bias[:, j % 2, t:t + 1],
                               scale=self.root_c[:, j:j + 1]).then_inc(self.probs_ready, 1)

        def copy(j):
            for k in range(T):
                act.wait_ge(self.turned, T * j + 1 if k == 0 else T * (j + 1))
                if j >= 2 and k == 0:
                    act.wait_ge(self.pv_done, j - 1)
                bank, c0 = self.turned_place(k)
                act.activation(self.pT[:, j % 2, k, k * P:S], self.ps[:, bank, c0:c0 + S - k * P], ACT.Copy)\
                    .then_inc(self.pT_ready, 1)

        root(0)
        for j in range(GH):
            score(j)
            if j + 1 < GH:
                root(j + 1)
            probs(j)
            copy(j)
        act.wait_ge(self.pv_done, GH)
        act.activation(self.oT[:, :], self.ps[:, 7, :], ACT.Copy).then_inc(self.oT_copied, 1)


def mixed_attention(nc, w, x_src, x_dst, kscratch, qscratch, tscratch):
    with ExitStack() as ctx:
        st = Stage(nc, ctx, "s4")
        ps = st.psum()
        loads = []
        identf = constant(st, loads, "identf", w["identf"])
        identb = constant(st, loads, "identb", w["identb"], BF16)
        tri = constant(st, loads, "tri", w["tri"], BF16)
        triT = constant(st, loads, "triT", w["triT"], BF16)
        trif = constant(st, loads, "trif", w["trif"])
        blocks = constant(st, loads, "blocks", w["blocks"])
        cos = constant(st, loads, "cos", w["rot_cos"])
        sin = constant(st, loads, "sin", w["rot_sin"])
        wts = {n: weight(st, loads, n, w[f"mix_{n}"]) for n in ("wq", "wk", "wq_partner", "wk_partner", "wv")}
        wo = weight(st, loads, "wo", w["mix_wo"])
        bo = bias_row(st, loads, "bo", w["L1_attn_proj_b"])
        c_feature = st.sb("c_feature", [P, 1])
        loads.append((c_feature[:, :], w["curvature_feature"]))
        c_head = st.sb("c_head", [P, GH])
        loads.append((c_head[:, :], w["curvature"].rearrange("(o h) -> o h", o=1).to_broadcast([P, GH])))
        neg_c, inv_c = st.sb("neg_c", [P, 1]), st.sb("inv_c", [P, 1])
        root_c, eps_c = st.sb("root_c", [P, GH]), st.sb("eps_c", [P, GH])
        x = st.sb("x", [P, T, D])
        norm = Norm(st, ps, x, identf)
        split = Split(st, S, 4)
        rotary = Rotary(st, ps, split, cos, sin)
        att = Attention(st, ps, identf, identb, norm.xn, S, 3, causal=True)
        hyp = Hyperbolic(st, ps, identf, trif, att, root_c, eps_c)
        proj = OutProjection(st, ps, identf, att.otok, norm.xnT[:, :, 1:], wo, x, bias=bo)
        square = st.sb("square", [P, 2, S])
        sums = st.sb("sums", [P, 2, S])
        t_full = st.sb("t_full", [P, 2, S])
        t_level = st.sb("t_level", [P, 2, 3, S], BF16)
        rotated, squared, summed = st.sem("rotated"), st.sem("squared"), st.sem("summed")
        sums_ready, factor_ready = st.sem("sums_ready"), st.sem("factor_ready")
        t_levels_ready, t_written = st.sem("t_levels_ready"), st.sem("t_written")
        v_in_psum, setup = st.sem("v_in_psum"), st.sem("setup")
        dve_steps, act_steps, stored = st.sem("dve_steps"), st.sem("act_steps"), st.sem("stored")
        load_constants(nc, st, loads)
        write_ones(nc, att)
        with nc.Block() as block:
            @block.vector
            def _(dve):
                dve.tensor_scalar(neg_c[:, :], c_feature[:, :], -1.0, None, ALU.mult)
                dve.reciprocal(inv_c[:, :], c_feature[:, :])
                dve.wait_ge(setup, 2)
                dve.tensor_scalar(eps_c[:, :], root_c[:, :], 1e-6, None, ALU.mult)

            @block.scalar
            def _(act):
                act.activation(root_c[:, :], c_head[:, :], ACT.Ln).then_inc(setup, 1)
                act.wait_ge(setup, 1)
                act.activation(root_c[:, :], root_c[:, :], ACT.Exp, scale=0.5).then_inc(setup, 1)

        hyp_rows = slice(64, P)
        cos_rows = (slice(96, P), slice(0, 64))

        def sync(sp, b):
            load_x(sp, norm, x, x_src, b)
            sync_self_attention(sp, att, split, kscratch, qscratch, ((0, 1), (2,)))
            for n in range(2):
                sp.wait_ge(t_levels_ready, n + 1)
                for s, lev in enumerate((K_LEVEL, Q_LEVEL)[n]):
                    sp.dma_start(tscratch[n, :, s, :], t_level[64:P:HD, n, lev, :]).then_inc(t_written, 16)
            sp.wait_ge(t_written, 2 * 16 * NSLOT)
            heads = slice(H - GH, H)
            for n, (dst, src) in enumerate(((hyp.kst, kscratch), (hyp.qst, qscratch))):
                sp.dma_start(dst[0:STACK, :, :], src[heads, :, :, 0:S].rearrange("h s d w -> (s d) h w"))\
                    .then_inc(hyp.loaded, 16)
                sp.dma_start(dst[STACK:STACK + NSLOT, :, :], tscratch[n].rearrange("h s w -> s h w"))\
                    .then_inc(hyp.loaded, 16)
            att.sync(sp)
            store_x(sp, proj.x_done, 2, stored, x, x_dst, b)

        def tensor(pe):
            norm.tensor(pe)
            pe.wait_ge(norm.xnT_ready, FT)
            xnT = norm.xnT[:, :, 1:]
            for i, (f, is_q) in enumerate(ITEMS):
                for bank, name in zip(rotary.BANKS[i], ("wq", "wq_partner") if is_q else ("wk", "wk_partner")):
                    for c in range(FT):
                        mm = pe.matmul(ps[:, bank, :], wts[name][:, c, f * P:(f + 1) * P], xnT[:, c, :],
                                       start=(c == 0), stop=(c == 1))
                mm.then_inc(rotary.in_psum, 1)
            for i in range(4):
                pe.wait_ge(squared, i + 1)
                if i >= 2:
                    pe.wait_ge(sums_ready, i - 1)
                pe.matmul(ps[:, 2 + i % 2, :], blocks[:, :], square[:, i % 2, :], start=True, stop=True)\
                    .then_inc(summed, 1)
            pe.wait_ge(rotary.read, 2)
            for t in range(T):
                for c in range(FT):
                    mm = pe.matmul(ps[:, 4 + t // 2, (t % 2) * D:(t % 2 + 1) * D], xnT[:, c, t * P:(t + 1) * P],
                                   wts["wv"][:, c, :], start=(c == 0), stop=(c == 1))
                if t % 2:
                    mm.then_inc(v_in_psum, 1)
            pe.wait_ge(att.v_ready, 2)
            pe.wait_ge(rotary.read, 4)
            pe.wait_ge(sums_ready, 4)
            att.tensor(pe, tri=tri, triT=triT)
            pe.wait_ge(att.exped, 2 * T * 3)
            pe.wait_ge(att.max_taken, 3 * len(att.units))
            pe.wait_ge(*att.b7_free)
            hyp.tensor(pe)
            proj.tensor(pe)

        def scalar(act):
            steps = Steps(act, act_steps)
            norm.scalar(act, steps)
            for i, (f, is_q) in enumerate(ITEMS):
                act.wait_ge(rotated, i + 1)
                if i >= 2:
                    act.wait_ge(summed, i - 1)
                act.activation(square[:, i % 2, :], split.full[:, i % 2, :], ACT.Square).then_inc(squared, 1)
                act.wait_ge(sums_ready, i + 1)
                rows = cos_rows[f]
                steps.mark(act.activation(sums[rows, i % 2, :], sums[rows, i % 2, :], ACT.Ln, scale=2.0 ** 24))
                steps.settle()
                last = act.activation(sums[rows, i % 2, :], sums[rows, i % 2, :], ACT.Exp, scale=-0.5)
                if f == 1:
                    steps.mark(last)
                    steps.mark(act.activation(sums[hyp_rows, i % 2, :], sums[hyp_rows, i % 2, :], ACT.Ln,
                                              bias=inv_c[hyp_rows, :]))
                    steps.settle()
                    last = act.activation(t_full[hyp_rows, i % 2, :], sums[hyp_rows, i % 2, :], ACT.Exp, scale=0.5)
                last.then_inc(factor_ready, 1)
                split.scalar(act, i, S)
            for n in range(2):
                act.wait_ge(v_in_psum, n + 1)
                act.activation(att.v[:, 2 * n:2 * n + 2, :, 0:HD], v_heads(ps[:, 4 + n, :]), ACT.Copy)\
                    .then_inc(att.v_ready, 1)
            att.scalar(act)
            hyp.scalar(act, steps)
            proj.scalar(act)

        def vector(dve):
            steps = Steps(dve, dve_steps)
            norm.vector(dve, steps)
            for i, (f, is_q) in enumerate(ITEMS):
                full = split.full[:, i % 2, :]
                rotary.vector(dve, steps, i, 1.0)
                dve.sem_inc(rotated, 1)
                dve.wait_ge(summed, i + 1)
                dve.tensor_scalar(sums[:, i % 2, :], ps[:, 2 + i % 2, :], 1e-24, None, ALU.max)\
                    .then_inc(sums_ready, 1)
                dve.wait_ge(factor_ready, i + 1)
                rows = cos_rows[f]
                scale = 4.0 if is_q else 1.0
                steps.mark(dve.scalar_tensor_tensor(out=full[rows, :], in0=full[rows, :], scalar=scale * 2.0 ** 12,
                                                    in1=sums[rows, i % 2, :], op0=ALU.mult, op1=ALU.mult))
                if is_q:
                    if f == 0:
                        steps.mark(dve.tensor_scalar(full[0:96, :], full[0:96, :], HD ** -0.5, None, ALU.mult))
                    else:
                        steps.mark(dve.tensor_scalar(full[hyp_rows, :], full[hyp_rows, :], neg_c[hyp_rows, :], None,
                                                     ALU.mult))
                        steps.mark(dve.tensor_scalar(t_full[hyp_rows, i % 2, :], t_full[hyp_rows, i % 2, :],
                                                     c_feature[hyp_rows, :], None, ALU.mult))
                steps.settle()
                dve.sem_inc(split.full_ready, 1)
                split.vector(dve, steps, i, S)
                if f == 1:
                    n = 1 if is_q else 0
                    tf, tl = t_full[hyp_rows, i % 2, :], t_level[hyp_rows, n]
                    for lev in range(3):
                        steps.mark(dve.tensor_copy(tl[:, lev, :], tf))
                        steps.settle()
                        if lev < 2:
                            steps.mark(dve.tensor_tensor(tf, tf, tl[:, lev, :], ALU.subtract))
                            steps.settle()
                    dve.sem_inc(t_levels_ready, 1)
            att.vector(dve, steps)
            hyp.vector(dve, steps)
            dve.wait_ge(att.o_divided, 3)
            dve.wait_ge(hyp.o_divided, 1)
            dve.sem_inc(proj.o_ready, 1)
            proj.vector(dve, steps)

        stage_loop(nc, st, {"sync": sync, "tensor": tensor, "scalar": scalar, "vector": vector})



NE = 7


def experts(nc, w, y_src, x_src, x_dst):
    with ExitStack() as ctx:
        st = Stage(nc, ctx, "s7")
        ps = st.psum()
        loads = []
        identf = constant(st, loads, "identf", w["identf"])
        number = st.sb("number", [P, NE + 1])
        loads.append((number[:, :], w["numbers"].rearrange("(o n) -> o n", o=1).to_broadcast([P, NE + 1])))
        w_ln = column(st, loads, "w_ln", w["L1_ffn_w_ln2"])
        wr = weight(st, loads, "wr", w["L1_ffn_W_router"])
        br = st.sb("br", [P, NE])
        loads.append((br[:, :], w["L1_ffn_routing_bias"].rearrange("(o n) -> o n", o=1).to_broadcast([P, NE])))
        wg, wu, wd = (st.sb(n, [P, NE + 1, FT, D]) for n in ("wg", "wu", "wd"))
        for tile, name in ((wg, "Wg"), (wu, "Wu"), (wd, "Wd")):
            loads.append((tile[:, 0, :, :], w[f"L1_ffn_{name}_s"].rearrange("(f p) n -> p f n", p=P)))
            for e in range(NE):
                loads.append((tile[:, 1 + e, :, :], w[f"L1_ffn_{name}_r"][e].rearrange("(f p) n -> p f n", p=P)))
        y, total = st.sb("y", [P, T, D]), st.sb("total", [P, T, D])
        norm = Norm(st, ps, y, identf, rms=True, weight=w_ln)
        logit, odds = st.sb("logit", [P, T, NE]), st.sb("odds", [P, T, NE])
        prob = st.sb("prob", [P, T, NE + 1])
        top, where = st.sb("top", [P, T, 8]), st.sb("where", [P, T, 8], U32)
        wheref = st.sb("wheref", [P, T, 2])
        picked, both = st.sb("picked", [P, T, NE + 1]), st.sb("both", [P, T])
        share = st.sb("share", [P, T, NE + 1])
        gate, gated = st.sb("gate", [P, 2, S]), st.sb("gated", [P, 2, S])
        mid = st.sb("mid", [P, 2, FT, S])
        y_copied = st.sem("y_copied")
        logit_in_psum, logit_ready, odds_ready = st.sem("logit_in_psum"), st.sem("logit_ready"), st.sem("odds_ready")
        up_in_psum, gate_ready, gated_ready = st.sem("up_in_psum"), st.sem("gate_ready"), st.sem("gated_ready")
        mid_ready, down_in_psum, down_added = st.sem("mid_ready"), st.sem("down_in_psum"), st.sem("down_added")
        residual_loaded = st.sem("residual_loaded")
        dve_steps, act_steps, stored = st.sem("dve_steps"), st.sem("act_steps"), st.sem("stored")
        load_constants(nc, st, loads)
        with nc.Block() as block:
            @block.vector
            def _(dve):
                dve.memset(prob[:, :, NE:NE + 1], -1.0)
        order = []
        for e in range(NE + 1):
            order += [("up", e, 0), ("up", e, 1)] + ([("down", e - 1)] if e else [])
        order.append(("down", NE))

        def sync(sp, b):
            load_x(sp, norm, y, y_src, b)
            sp.dma_start(total[:, :, :], x_src[b].rearrange("(t p) d -> p t d", p=P)).then_inc(residual_loaded, 16)
            store_x(sp, down_added, T * (NE + 1), stored, total, x_dst, b)

        def tensor(pe):
            norm.tensor(pe)
            pe.wait_ge(norm.xnT_ready, FT)
            xnT = norm.xnT[:, :, 1:]
            for t in range(T):
                for c in range(FT):
                    mm = pe.matmul(ps[:, 4, t * NE:(t + 1) * NE], xnT[:, c, t * P:(t + 1) * P], wr[:, c, :],
                                   start=(c == 0), stop=(c == 1))
            mm.then_inc(logit_in_psum, 1)
            pe.wait_ge(logit_ready, 1)
            for item in order:
                e = item[1]
                if item[0] == "up":
                    f = item[2]
                    i = 2 * e + f
                    if i >= 2:
                        pe.wait_ge(mid_ready, i - 1)
                    for bank, wt in ((2 * (i % 2), wg), (2 * (i % 2) + 1, wu)):
                        for c in range(FT):
                            mm = pe.matmul(ps[:, bank, :], wt[:, e, c, f * P:(f + 1) * P], xnT[:, c, :],
                                           start=(c == 0), stop=(c == 1))
                    mm.then_inc(up_in_psum, 1)
                    continue
                pe.wait_ge(mid_ready, 2 * e + 2)
                for t in range(T):
                    bank = 4 + t
                    if e >= 1:
                        pe.wait_ge(down_added, T * (e - 1) + t + 1)
                    for c in range(FT):
                        mm = pe.matmul(ps[:, bank, 0:D], mid[:, e % 2, c, t * P:(t + 1) * P], wd[:, e, c, :],
                                       start=(c == 0), stop=(c == 1))
                    mm.then_inc(down_in_psum, 1)

        def scalar(act):
            steps = Steps(act, act_steps)
            norm.scalar(act, steps)
            act.wait_ge(logit_ready, 1)
            act.activation(odds[:, :, :], logit[:, :, :], ACT.Exp, scale=-1.0).then_inc(odds_ready, 1)
            for i in range(2 * (NE + 1)):
                act.wait_ge(up_in_psum, i + 1)
                if i >= 2:
                    act.wait_ge(gated_ready, i - 1)
                act.activation(gate[:, i % 2, :], ps[:, 2 * (i % 2), :], ACT.Tanh, scale=0.5).then_inc(gate_ready, 1)

        def vector(dve):
            steps = Steps(dve, dve_steps)

            def do(instruction):
                steps.mark(instruction)
                steps.settle()

            norm.vector(dve, steps)
            dve.wait_ge(logit_in_psum, 1)
            dve.tensor_tensor(logit[:, :, :], ps[:, 4, 0:T * NE].rearrange("p (t n) -> p t n", t=T),
                              br[:, :].rearrange("p (o n) -> p o n", o=1).to_broadcast([P, T, NE]), ALU.add)\
                .then_inc(logit_ready, 1)
            dve.wait_ge(residual_loaded, 16)
            do(dve.tensor_tensor(total[:, :, :], total[:, :, :], y[:, :, :], ALU.add))
            dve.wait_ge(odds_ready, 1)
            do(dve.tensor_scalar(odds[:, :, :], odds[:, :, :], 1.0, None, ALU.add))
            do(dve.reciprocal(prob[:, :, 0:NE], odds[:, :, :]))
            for t in range(T):
                steps.mark(dve.max(top[:, t, :], prob[:, t, :]))
            steps.settle()
            for t in range(T):
                steps.mark(dve.max_index(where[:, t, :], top[:, t, :], prob[:, t, :]))
            do(dve.tensor_tensor(both[:, :], top[:, :, 0], top[:, :, 1], ALU.add))
            do(dve.reciprocal(both[:, :], both[:, :]))
            do(dve.tensor_copy(wheref[:, :, :], where[:, :, 0:2]))
            for t in range(T):
                steps.mark(dve.tensor_scalar(picked[:, t, :], number[:, :], wheref[:, t, 0:1], None, ALU.is_equal))
            steps.settle()
            for t in range(T):
                steps.mark(dve.scalar_tensor_tensor(out=picked[:, t, :], in0=number[:, :],
                                                    scalar=wheref[:, t, 1:2], in1=picked[:, t, :],
                                                    op0=ALU.is_equal, op1=ALU.add))
            steps.settle()
            for t in range(T):
                steps.mark(dve.scalar_tensor_tensor(out=share[:, t, :], in0=prob[:, t, :], scalar=both[:, t:t + 1],
                                                    in1=picked[:, t, :], op0=ALU.mult, op1=ALU.mult))
            steps.settle()
            do(dve.tensor_scalar(share[:, :, :], share[:, :, :], 0.5, None, ALU.mult))

            for item in order:
                e = item[1]
                if item[0] == "up":
                    i = 2 * e + item[2]
                    g, u = 2 * (i % 2), 2 * (i % 2) + 1
                    dve.wait_ge(gate_ready, i + 1)
                    if i >= 2:
                        dve.wait_ge(mid_ready, i - 1)
                    dve.scalar_tensor_tensor(out=gated[:, i % 2, :], in0=gate[:, i % 2, :], scalar=1.0,
                                             in1=ps[:, g, :], op0=ALU.add, op1=ALU.mult).then_inc(gated_ready, 1)
                    dve.wait_ge(gated_ready, i + 1)
                    if e >= 2:
                        dve.wait_ge(down_in_psum, T * (e - 1))
                    dve.tensor_tensor(mid[:, e % 2, item[2], :], gated[:, i % 2, :], ps[:, u, :], ALU.mult)\
                        .then_inc(mid_ready, 1)
                    continue
                for t in range(T):
                    dve.wait_ge(down_in_psum, T * e + t + 1)
                    if e >= 1:
                        dve.wait_ge(down_added, T * (e - 1) + t + 1)
                    dve.scalar_tensor_tensor(out=total[:, t, :], in0=ps[:, 4 + t, 0:D],
                                             scalar=share[:, t, e - 1:e] if e else 0.5, in1=total[:, t, :],
                                             op0=ALU.mult, op1=ALU.add).then_inc(down_added, 1)

        stage_loop(nc, st, {"sync": sync, "tensor": tensor, "scalar": scalar, "vector": vector})



def decoder(nc, w, out):
    def scratch(name, shape, dt):
        return nc.dram_tensor(name, shape, dt, kind="Internal").ap()

    x = [w["x"]] + [scratch(f"x_after_{i}", (NB, S, D), F32) for i in range(1, 7)] + [out]
    kscratch = scratch("k_levels", (H, NSLOT, HD, CTX), BF16)
    qscratch = scratch("q_levels", (H, NSLOT, HD, S), BF16)
    tscratch = scratch("t_levels", (2, GH, NSLOT, S), BF16)
    latent_attention(nc, w, x[0], x[1], kscratch, qscratch)
    cross_attention(nc, w, x[1], x[2], kscratch, qscratch)
    channel_mix(nc, w, x[2], x[3])
    mixed_attention(nc, w, x[3], x[4], kscratch, qscratch, tscratch)
    linear_attention(nc, w, x[4], x[5])
    rotary_latent_attention(nc, w, x[5], x[6], kscratch, qscratch)
    experts(nc, w, x[6], x[5], x[7])


def kernel(**inputs):
    import ml_dtypes as _ml
    import numpy as _np
    import concourse.bacc as _bacc
    from concourse import mybir as _mybir
    from concourse.bass_utils import run_bass_kernel_spmd as _run

    f32 = _np.float32
    src = {name: _np.asarray(value) for name, value in inputs.items()}

    def columns(v):
        return v.reshape(FT, P).T

    a = {"x": src["x"], "mask": src["mask_BxSxS2_ff0"], "maskT": src["mask_BxSxS2_ff0"].transpose(0, 2, 1),
         "ctxT": src["ctx_1024"].transpose(0, 2, 1)}

    i = _np.arange(P)
    causal = _np.where(i[None, :] > i[:, None], NEG, 0.0)
    a["identf"], a["identb"] = _np.eye(P, dtype=f32), _np.eye(P).astype(_ml.bfloat16)
    a["tri"], a["triT"], a["trif"] = causal.astype(_ml.bfloat16), causal.T.astype(_ml.bfloat16), causal.astype(f32)
    a["blocks"] = _np.kron(_np.eye(P // HD), _np.ones((HD, HD))).astype(f32)
    a["numbers"] = _np.arange(NE + 1, dtype=f32)

    def rotary_tables(width):
        steps = f32(1.0) / _np.power(f32(10000.0), _np.arange(0, width, 2, dtype=f32) / f32(width))
        angles = _np.outer(_np.arange(S, dtype=f32), steps.astype(f32)).astype(f32)
        return _np.cos(angles).T, _np.sin(angles).T

    c, s = rotary_tables(HD)
    a["rot_cos"] = _np.tile(_np.concatenate([c, c]), (P // HD, 1))
    a["rot_sin"] = _np.tile(_np.concatenate([s, -s]), (P // HD, 1))
    c, s = rotary_tables(HD // 2)
    a["mla_cos"] = _np.tile(_np.concatenate([_np.ones((HD // 2, S), f32), c, c]), (P // HD, 1))
    a["mla_sin"] = _np.tile(_np.concatenate([_np.zeros((HD // 2, S), f32), -s, s]), (P // HD, 1))

    for name in ("L0_attn_W_DKV", "L0_attn_W_UK", "L0_attn_W_UV", "L0_attn_W_UQ", "L0_attn_W_O",
                 "L0_xattn_bv", "L0_xattn_bo", "L1_xattn_bk", "L1_xattn_bv", "L1_xattn_bo", "L1_attn_proj_b",
                 "L1_ffn_W_kvd", "L1_ffn_W_qd", "L1_ffn_W_vu", "L1_ffn_W_o", "L1_ffn_Wg_s", "L1_ffn_Wu_s",
                 "L1_ffn_Wd_s", "L1_ffn_Wg_r", "L1_ffn_Wu_r", "L1_ffn_Wd_r", "L1_ffn_W_router",
                 "L1_ffn_routing_bias"):
        a[name] = src[name]
    for name in ("L0_xattn_Wq", "L0_xattn_Wk", "L0_xattn_Wv", "L0_xattn_Wo", "L1_xattn_Wq", "L1_xattn_Wk",
                 "L1_xattn_Wv", "L1_xattn_Wo", "L0_ffn_W_r", "L0_ffn_W_k", "L0_ffn_W_v"):
        a[name] = src[name].T
    for name in ("L0_xattn_bq", "L0_xattn_bk", "L1_xattn_bq", "L0_ffn_mu_r", "L0_ffn_mu_k", "L1_ffn_w_ln1",
                 "L1_ffn_w_ln2"):
        a[name] = columns(src[name])

    order = [*range(6), *range(10, 16), *range(6, 10)]
    own = _np.concatenate([HD * h + _np.arange(HD) for h in order])
    partner = _np.concatenate([HD * h + (_np.arange(HD) + HD // 2) % HD for h in order])
    q, k, v = _np.split(src["L1_attn_qkv_w"], 3)
    a["mix_wq"], a["mix_wk"], a["mix_wv"] = q[own].T, k[own].T, v[own].T
    a["mix_wq_partner"], a["mix_wk_partner"] = q[partner].T, k[partner].T
    a["mix_wo"] = src["L1_attn_proj_w"].T[own]
    a["curvature"] = src["L1_attn_curvature"].reshape(GH)
    a["curvature_feature"] = _np.tile(_np.repeat(a["curvature"], HD), P // (GH * HD)).reshape(P, 1)

    def head_columns(plain, rotary, swapped=False):
        n, half = (plain if rotary is None else rotary).shape[0], HD // 2
        cols = _np.zeros((n, H, HD), f32)
        if plain is not None:
            cols[:, :, 0:half] = plain.reshape(n, H, half)
        if rotary is not None:
            order = (_np.arange(half) + half // 2) % half if swapped else _np.arange(half)
            cols[:, :, half:HD] = rotary.reshape(n, H, half)[:, :, order]
        return cols.reshape(n, D)

    a["mla_wku"] = head_columns(src["L1_ffn_W_ku"], None)
    a["mla_wkr"] = head_columns(None, src["L1_ffn_W_ropek"])
    a["mla_wkr_partner"] = head_columns(None, src["L1_ffn_W_ropek"], swapped=True)
    a["mla_wq"] = head_columns(src["L1_ffn_W_qu"], src["L1_ffn_W_ropeq"])
    a["mla_wq_partner"] = head_columns(None, src["L1_ffn_W_ropeq"], swapped=True)

    nc = _bacc.Bacc("TRN2", target_bir_lowering=False, num_devices=1)
    arrays, w = {}, {}
    for name, value in a.items():
        arrays[f"in_{name}"] = value = _np.ascontiguousarray(value)
        w[name] = nc.dram_tensor(f"in_{name}", value.shape, _mybir.dt.from_np(value.dtype),
                                 kind="ExternalInput").ap()
    out = nc.dram_tensor("out_x", (NB, S, D), F32, kind="ExternalOutput").ap()
    decoder(nc, w, out)
    r = _run(nc, [arrays], core_ids=[0])
    return r.results[0]["out_x"]
```

```python
from contextlib import ExitStack

import concourse.bass as bass
from concourse import mybir

F32 = mybir.dt.float32
BF16 = mybir.dt.bfloat16
U32 = mybir.dt.uint32
ALU = mybir.AluOpType
ACT = mybir.ActivationFunctionType
AX = mybir.AxisListType

P = 128
NB, S, D = 8, 512, 256
H, HD = 16, 16
CTX = 1601
T = S // P
FT = D // P
GH = 4
NG = H // GH
VW = 32
NEG = -1.0e30
K_LEVEL = (0, 1, 2, 0, 1, 0)
Q_LEVEL = (0, 0, 0, 1, 1, 2)
NSLOT = len(K_LEVEL)
K_LAYOUT = ((0, 3, 0, 1), (3, 2, 0, 1), (5, 1, 0, 1))
Q_LAYOUT = ((0, 3, 0, 0), (3, 2, 1, 0), (5, 1, 2, 0))
ITEM_DONE = 16 * len(K_LAYOUT)
STACK = NSLOT * HD
ITEMS = ((0, False), (0, True), (1, False), (1, True))
SHIFT = 3
EPS = 1e-5
TINY = 2.0 ** -23
EXP_AND_LN = "natural_log_exp_and_others"


def tiles_of(n):
    return [(i, min(P, n - i)) for i in range(0, n, P)]


class Steps:

    def __init__(self, eng, sem):
        self.eng, self.sem, self.n = eng, sem, 0

    def mark(self, instruction):
        self.n += 1
        return instruction.then_inc(self.sem, 1)

    def settle(self):
        if self.n:
            self.eng.wait_ge(self.sem, self.n)


class Stage:

    def __init__(self, nc, ctx, name):
        self.nc, self.ctx, self.name, self.nums = nc, ctx, name, []

    def sb(self, name, shape, dt=F32):
        return self.ctx.enter_context(self.nc.sbuf_tensor(f"{self.name}_{name}", shape, dt))

    def psum(self):
        return self.ctx.enter_context(self.nc.psum_tensor(f"{self.name}_ps", [P, 8, 512], F32))

    def sem(self, name):
        s = self.ctx.enter_context(self.nc.semaphore(f"{self.name}_{name}"))
        self.nums.append(s.num)
        return s

    def runs(self):
        nums, out = sorted(self.nums), []
        for n in nums:
            if out and n == out[-1].stop:
                out[-1] = range(out[-1].start, n + 1)
            else:
                out.append(range(n, n + 1))
        return out


def stage_loop(nc, st, programs):
    with nc.Fori(0, NB) as b:
        with nc.Block() as block:
            @block.sync
            def _(sp):
                programs["sync"](sp, b)

            @block.tensor
            def _(pe):
                programs["tensor"](pe)

            @block.vector
            def _(dve):
                programs["vector"](dve)

            @block.scalar
            def _(act):
                programs["scalar"](act)

            @block.gpsimd
            def _(pool):
                if "gpsimd" in programs:
                    programs["gpsimd"](pool)
        for run in st.runs():
            nc.all_engine_barrier(sems_to_clear=run)


def pipelined_loop(nc, st, prologue, body):
    def everything(block, run):
        @block.sync
        def _(sp):
            run("sync", sp)

        @block.tensor
        def _(pe):
            run("tensor", pe)

        @block.vector
        def _(dve):
            run("vector", dve)

        @block.scalar
        def _(act):
            run("scalar", act)

        @block.gpsimd
        def _(pool):
            run("gpsimd", pool)

    def barrier():
        for run in st.runs():
            nc.all_engine_barrier(sems_to_clear=run)

    with nc.Block() as block:
        everything(block, lambda name, e: exhaust(prologue[name](e, 0, True)))
    barrier()
    with nc.Fori(0, NB - 1) as b:
        with nc.Block() as block:
            everything(block, lambda name, e: body[name](e, b, lambda: prologue[name](e, b + 1, False)))
        barrier()
    with nc.Block() as block:
        everything(block, lambda name, e: body[name](e, NB - 1, NO_SIDE))
    barrier()


def NO_SIDE():
    return iter(())


def exhaust(steps):
    for _ in steps:
        pass


def skip(n):
    for _ in range(n):
        yield


class SharedBank:

    def __init__(self, index):
        self.index, self.freed = index, None

    def take(self, pe):
        if self.freed:
            pe.wait_ge(*self.freed)

    def freed_by(self, sem, value):
        self.freed = (sem, value)



class Norm:

    def __init__(self, st, ps, x, identf, rms=False, weight=None, banks=(0, 1), shared=None):
        if shared:
            banks = (shared.index, shared.index)
        self.shared = shared
        self.ps, self.x, self.identf, self.rms, self.weight, self.banks = ps, x, identf, rms, weight, banks
        self.xn = st.sb("xn", [P, T, D])
        self.xnT = st.sb("xnT", [P, FT, S + 1])
        self.stats = st.sb("stats", [P, T, 6])
        self.mv = st.sb("mv", [P, T, 2])
        self.var = st.sb("var", [P, T])
        self.lnv = st.sb("lnv", [P, T])
        self.rstd = st.sb("rstd", [P, T])
        self.x_loaded = st.sem("x_loaded")
        self.outer_var_ready, self.outer_rstd_ready = st.sem("outer_var_ready"), st.sem("outer_rstd_ready")
        self.var_ready = st.sem("var_ready")
        self.rstd_ready = st.sem("rstd_ready")
        self.xn_ready = st.sem("xn_ready")
        self.xnT_in_psum = st.sem("xnT_in_psum")
        self.xnT_ready = st.sem("xnT_ready")

    STEPS, OUTER_STEPS = 5, 3

    def outer_vector(self, dve, steps):
        dve.wait_ge(self.x_loaded, 16)
        for t in range(T):
            steps.mark(dve.bn_stats(self.stats[:, t, :], self.x[:, t, :]))
        steps.settle()
        for t in range(T):
            steps.mark(dve.bn_aggr(self.mv[:, t, :], self.stats[:, t, :]))
        steps.settle()
        dve.tensor_scalar(self.var[:, :], self.mv[:, :, 1], EPS, None, ALU.add).then_inc(self.outer_var_ready, 1)
        yield
        yield
        dve.wait_ge(self.outer_rstd_ready, 1)
        for t in range(T):
            steps.mark(dve.tensor_scalar(self.x[:, t, :], self.x[:, t, :], self.mv[:, t, 0:1],
                                         self.rstd[:, t:t + 1], ALU.subtract, ALU.mult))
        steps.settle()
        yield

    def outer_scalar(self, act, steps):
        yield
        act.wait_ge(self.outer_var_ready, 1)
        steps.mark(act.activation(self.lnv[:, :], self.var[:, :], ACT.Ln))
        steps.settle()
        act.activation(self.rstd[:, :], self.lnv[:, :], ACT.Exp, scale=-0.5).then_inc(self.outer_rstd_ready, 1)
        yield
        yield

    def vector(self, dve, steps):
        dve.wait_ge(self.x_loaded, 16)
        for t in range(T):
            steps.mark(dve.bn_stats(self.stats[:, t, :], self.x[:, t, :]))
        steps.settle()
        for t in range(T):
            steps.mark(dve.bn_aggr(self.mv[:, t, :], self.stats[:, t, :]))
        steps.settle()
        if self.rms:
            steps.mark(dve.tensor_tensor(self.lnv[:, :], self.mv[:, :, 0], self.mv[:, :, 0], ALU.mult))
            steps.settle()
            steps.mark(dve.scalar_tensor_tensor(out=self.var[:, :], in0=self.mv[:, :, 1], scalar=1e-18,
                                                in1=self.lnv[:, :], op0=ALU.add, op1=ALU.add))
            steps.settle()
            dve.sem_inc(self.var_ready, 1)
            yield
            yield
            dve.wait_ge(self.rstd_ready, 1)
            steps.mark(dve.tensor_scalar(self.var[:, :], self.rstd[:, :], EPS, None, ALU.add))
            steps.settle()
            steps.mark(dve.reciprocal(self.rstd[:, :], self.var[:, :]))
            steps.settle()
            for t in range(T):
                dve.tensor_scalar(self.xn[:, t, :], self.x[:, t, :], self.rstd[:, t:t + 1], None,
                                  ALU.mult).then_inc(self.xn_ready, 1)
            yield from skip(3)
            return
        dve.tensor_scalar(self.var[:, :], self.mv[:, :, 1], EPS, None, ALU.add).then_inc(self.var_ready, 1)
        yield
        yield
        dve.wait_ge(self.rstd_ready, 1)
        for t in range(T):
            dve.tensor_scalar(self.xn[:, t, :], self.x[:, t, :], self.mv[:, t, 0:1], self.rstd[:, t:t + 1],
                              ALU.subtract, ALU.mult).then_inc(self.xn_ready, 1)
        yield from skip(3)

    def scalar(self, act, steps):
        yield
        act.wait_ge(self.var_ready, 1)
        steps.mark(act.activation(self.lnv[:, :], self.var[:, :], ACT.Ln))
        steps.settle()
        act.activation(self.rstd[:, :], self.lnv[:, :], ACT.Exp,
                       scale=0.5 if self.rms else -0.5).then_inc(self.rstd_ready, 1)
        yield
        yield
        for f in range(FT):
            act.wait_ge(self.xnT_in_psum, f + 1)
            scale = 1.0 if self.weight is None else self.weight[:, f:f + 1]
            act.activation(self.xnT[:, f, 1:S + 1], self.ps[:, self.banks[f], :], ACT.Identity,
                           scale=scale).then_inc(self.xnT_ready, 1)
            yield

    def tensor(self, pe):
        yield from skip(3)
        for f in range(FT):
            if self.shared:
                self.shared.take(pe)
                self.shared.freed_by(self.xnT_ready, f + 1)
            for t in range(T):
                if f == 0:
                    pe.wait_ge(self.xn_ready, t + 1)
                last = pe.transpose(self.ps[:, self.banks[f], t * P:(t + 1) * P],
                                    self.xn[:, t, f * P:(f + 1) * P], self.identf[:, :])
            last.then_inc(self.xnT_in_psum, 1)
            yield



class Split:

    def __init__(self, st, width, items, bufs=2):
        self.items, self.bufs = items, bufs
        self.full = st.sb("full", [P, bufs, width])
        self.level = st.sb("level", [P, bufs, 3, width], BF16)
        self.full_ready = st.sem("full_ready")
        self.level0_ready = st.sem("level0_ready")
        self.levels_ready = st.sem("levels_ready")
        self.in_dram = [st.sem(f"levels_in_dram{i}") for i in range(items)]

    def wait_in_dram(self, sp, items):
        for i in items:
            sp.wait_ge(self.in_dram[i], ITEM_DONE)

    def vector(self, dve, steps, i, w):
        full, level = self.full[:, i % self.bufs, 0:w], self.level[:, i % self.bufs]
        dve.wait_ge(self.level0_ready, i + 1)
        steps.mark(dve.tensor_tensor(full, full, level[:, 0, 0:w], ALU.subtract))
        steps.settle()
        if i >= self.bufs:
            dve.wait_ge(self.in_dram[i - self.bufs], ITEM_DONE)
        steps.mark(dve.tensor_copy(level[:, 1, 0:w], full))
        steps.settle()
        steps.mark(dve.tensor_tensor(level[:, 2, 0:w], full, level[:, 1, 0:w], ALU.subtract))
        steps.settle()
        dve.sem_inc(self.levels_ready, 1)

    def scalar(self, act, i, w):
        act.wait_ge(self.full_ready, i + 1)
        if i >= self.bufs:
            act.wait_ge(self.in_dram[i - self.bufs], ITEM_DONE)
        act.activation(self.level[:, i % self.bufs, 0, 0:w], self.full[:, i % self.bufs, 0:w], ACT.Copy)\
            .then_inc(self.level0_ready, 1)

    def sync(self, sp, i, w, scratch, heads, slots):
        sp.wait_ge(self.levels_ready, i + 1)
        for first, n, lev, step in slots:
            if step:
                src = self.level[:, i % self.bufs, lev:lev + n, 0:w]
            else:
                src = self.level[:, i % self.bufs, lev, 0:w].rearrange("p (o w) -> p o w", o=1)\
                    .to_broadcast([P, n, w])
            sp.dma_start(scratch[heads[0]:heads[1], :, first:first + n, 0:w].rearrange("h d s w -> (h d) s w"), src)\
                .then_inc(self.in_dram[i], 16)



class Attention:

    UNIT_TIME, SCORE_TIME, PV_TIME = 0.4, 0.43, 0.85

    def __init__(self, st, ps, identf, identb, otok, keys, groups, causal, masked=False, bank7=None, own=0, side=0, side_until=0.95,
                 late=0, preloaded=0):
        self.own, self.side, self.late, self.preloaded = own, side, late, preloaded
        self.own_ready, self.side_until = None, side_until
        self.bank7 = bank7 or SharedBank(7)
        self.ps, self.identf, self.identb = ps, identf, identb
        self.keys, self.groups, self.causal, self.masked = tiles_of(keys), groups, causal, masked
        self.nslots = 4
        self.npt = 4
        self.kst = st.sb("kstack", [P, self.nslots, GH, keys], BF16)
        self.qst = st.sb("qstack", [P, self.nslots, GH, S], BF16)
        self.v = st.sb("v", [P, len(self.keys), H, VW])
        self.probs = st.sb("probs", [P, self.npt, 2, S])
        self.nchunk = 1 if causal else 4
        self.chunk = -(-keys // self.nchunk)
        self.cmax = st.sb("cmax", [P, 2, T * GH, 4])
        self.nmax = st.sb("nmax", [P, 2, T, GH])
        self.rest = st.sb("rest", [P, 2, T, GH])
        self.shift = st.sb("shift", [P, 2, T, SHIFT * GH], BF16)
        self.shiftT = st.sb("shiftT", [SHIFT * GH, 2, S], BF16)
        self.oT = st.sb("oT", [P, S])
        self.inv = st.sb("inv", [P, T, GH])
        self.otok = otok
        if masked:
            self.junk = st.sb("junk", [P, 2, self.chunk])
        self.stacks_loaded = [st.sem(f"stacks_loaded{g}") for g in range(groups)]
        self.stacks_preloaded = st.sem("stacks_preloaded")
        self.shift_loaded = [st.sem(f"shift_loaded{g}") for g in range(groups)]
        self.v_ready = st.sem("v_ready")
        self.max_scored = st.sem("max_scored")
        self.max_taken = st.sem("max_taken")
        self.shift_split = st.sem("shift_split")
        self.shift_turned = st.sem("shift_turned")
        self.shift_copied = st.sem("shift_copied")
        self.scored = st.sem("scored")
        self.exped = st.sem("exped")
        self.pv_done = st.sem("pv_done")
        self.oT_copied = st.sem("oT_copied")
        self.o_turned = st.sem("o_turned")
        self.o_divided = st.sem("o_divided")
        self.units = [(j, t, c, (t + 1) * P if causal else min(self.chunk, keys - c * self.chunk))
                      for t in range(T) for j in range(GH) for c in range(self.nchunk)]
        self.order = self.plan()

    def plan(self):
        out, post = [], []
        ngr, nu, nk = self.groups, len(self.units), len(self.keys)
        ahead = 1.5 if self.causal else 1.2
        unit = [("max", g, i) for g in range(ngr) for i in range(nu)]
        lead = nu * ahead * self.UNIT_TIME
        total = lead + ngr * nk * (2 * self.SCORE_TIME + self.PV_TIME + self.UNIT_TIME * nu / nk * 0.3)
        own, side = [("own",)] * self.own, [("side",)] * self.side
        done, shifts, now = 0, [], 0.0

        def advance(time):
            nonlocal now
            now += time
            while own and now * self.own >= (self.own - len(own)) * lead * 0.7:
                out.append(own.pop())
            while side and (now - lead * 0.7) * self.side >= (self.side - len(side) + 1) * (total * self.side_until - lead * 0.7):
                out.append(side.pop())

        def units_until(n):
            nonlocal done
            while done < min(n, len(unit)):
                out.append(unit[done])
                done += 1
                if done % nu == 0:
                    out.append(("split", done // nu - 1))
                    shifts.append((done + 3, done // nu - 1))
                if shifts and done >= shifts[0][0]:
                    out.append(("shift", shifts.pop(0)[1]))
                if now < lead:
                    advance(self.UNIT_TIME)

        def spread(g, k, part):
            units_until(int(nu * (ahead + g + (k + part) / nk)))
            if done == len(unit) and shifts:
                out.append(("shift", shifts.pop(0)[1]))

        units_until(int(nu * ahead))
        last = None
        for g in range(ngr):
            for k in range(nk):
                step = 2 * self.SCORE_TIME + self.PV_TIME
                for p in range(2):
                    out.append(("score", g, k, p))
                    advance(self.SCORE_TIME)
                    spread(g, k, (p + 1) * self.SCORE_TIME / step)
                if last:
                    out.append(("pv",) + last)
                    if last[1] == nk - 1:
                        out.append(("copy", last[0]))
                        post.append(last[0])
                if k == 1 and post:
                    out.append(("post", post.pop(0)))
                advance(self.PV_TIME)
                spread(g, k, 1.0)
                last = (g, k)
        out += [("pv",) + last, ("copy", last[0])] + side + [("side",)] * self.late + [("post", last[0])]
        return out

    def preload(self, sp, g, kscratch, qscratch, w, first):
        users = [u for u in range(self.groups) if u % self.nslots == g]
        if not first:
            sp.wait_ge(self.scored, 2 * len(self.keys) * (users[-1] + 1))
        self.load_stacks(sp, g, kscratch, qscratch, w, self.stacks_preloaded)

    def load_stacks(self, sp, g, kscratch, qscratch, w, loaded=None):
        loaded = loaded or self.stacks_loaded[g]
        heads = slice(g * GH, (g + 1) * GH)
        if g >= self.nslots:
            sp.wait_ge(self.scored, 2 * len(self.keys) * (g - self.nslots + 1))
        sp.dma_start(self.kst[0:STACK, g % self.nslots, :, 0:w],
                     kscratch[heads, :, :, 0:w].rearrange("h d s w -> (d s) h w"))\
            .then_inc(loaded, 16)
        sp.dma_start(self.qst[0:STACK, g % self.nslots, :, :],
                     qscratch[heads].rearrange("h d s w -> (d s) h w")).then_inc(loaded, 16)

    def sync(self, sp, refill=None, side=iter(()), after_shifts=None):
        for item in self.order:
            if item[0] == "shift":
                g = item[1]
                sp.wait_ge(self.shift_copied, g + 1)
                sp.dma_start(self.qst[STACK:STACK + SHIFT, g % self.nslots, :, :], self.shiftT[:, g % 2, :])\
                    .then_inc(self.shift_loaded[g], 16)
                if g == self.groups - 1 and after_shifts:
                    after_shifts()
            if item[0] == "side":
                next(side, None)
            if item[0] == "copy" and refill and item[1] + 2 < self.groups:
                self.load_stacks(sp, item[1] + 2, *refill)

    def tensor(self, pe, maskq=None, tri=None, triT=None, own=iter(()), side=iter(())):
        ps, nk = self.ps, len(self.keys)
        nmax = nscore = npv = 0
        bank7 = self.bank7
        bank7.freed = None
        for item in self.order:
            if item[0] == "own":
                next(own, None)
            elif item[0] == "side":
                next(side, None)
            elif item[0] == "max":
                g, (j, t, c, n) = item[1], self.units[item[2]]
                if item[2] == 0 and g >= self.preloaded:
                    pe.wait_ge(self.stacks_loaded[g], 32)
                if nmax >= 2:
                    pe.wait_ge(self.max_taken, nmax - 1)
                bank, sl = 4 + nmax % 2, g % self.nslots
                k0 = c * self.chunk
                mm = pe.matmul(ps[:, bank, 0:n], self.qst[0:STACK, sl, j, t * P:(t + 1) * P],
                               self.kst[0:STACK, sl, j, k0:k0 + n], start=True, stop=not self.causal)
                if self.causal:
                    mm = pe.matmul(ps[:, bank, n - P:n], self.identb[:, :], tri[:, :], start=False, stop=True)
                mm.then_inc(self.max_scored, 1)
                nmax += 1
            elif item[0] == "shift":
                g = item[1]
                pe.wait_ge(self.shift_split, g + 1)
                bank7.take(pe)
                for t in range(T):
                    mm = pe.matmul(ps[0:SHIFT * GH, 7, t * P:(t + 1) * P], self.shift[:, g % 2, t, :],
                                   self.identb[:, :], start=True, stop=True)
                mm.then_inc(self.shift_turned, 1)
                bank7.freed_by(self.shift_copied, g + 1)
            elif item[0] == "score":
                _, g, k, p = item
                sl = g % self.nslots
                if k == 0 and p == 0:
                    if g == 0 and self.own_ready:
                        pe.wait_ge(*self.own_ready)
                    pe.wait_ge(self.shift_loaded[g], 16)
                if nscore >= 2:
                    pe.wait_ge(self.exped, nscore - 1)
                k0, n = self.keys[k]
                q0 = k0 if self.causal else 0
                for j in (2 * p, 2 * p + 1):
                    bank = 2 * (nscore % 2) + j % 2
                    extra = self.causal or maskq is not None
                    mm = pe.matmul(ps[0:n, bank, 0:S - q0], self.kst[0:STACK + SHIFT, sl, j, k0:k0 + n],
                                   self.qst[0:STACK + SHIFT, sl, j, q0:S], start=True, stop=not extra)
                    if self.causal:
                        mm = pe.matmul(ps[0:n, bank, 0:P], self.identb[:, :], triT[:, :], start=False, stop=True)
                    if maskq is not None:
                        for t in range(T):
                            mm = pe.matmul(ps[0:n, bank, t * P:(t + 1) * P], maskq[:, t, k0:k0 + n],
                                           self.identf[:, :], start=False, stop=(t == T - 1))
                mm.then_inc(self.scored, 1)
                nscore += 1
            elif item[0] == "pv":
                _, g, k = item
                if k == 0 and g > 0:
                    pe.wait_ge(self.oT_copied, g)
                pe.wait_ge(self.exped, 2 * npv + 2)
                k0, n = self.keys[k]
                q0 = k0 if self.causal else 0
                for j in range(GH):
                    mm = pe.matmul(ps[VW * j:VW * (j + 1), 6, q0:S], self.v[0:n, k, g * GH + j, :],
                                   self.probs[0:n, (2 * npv + j // 2) % self.npt, j % 2, q0:S],
                                   start=(k == 0), stop=(k == nk - 1))
                mm.then_inc(self.pv_done, 1)
                npv += 1
            elif item[0] == "post":
                g = item[1]
                pe.wait_ge(self.oT_copied, g + 1)
                bank7.take(pe)
                for t in range(T):
                    mm = pe.transpose(ps[:, 7, t * P:(t + 1) * P], self.oT[:, t * P:(t + 1) * P], self.identf[:, :])
                mm.then_inc(self.o_turned, 1)
                bank7.freed_by(self.o_divided, g + 1)

    def scalar(self, act, own=iter(()), side=iter(())):
        ps, nscore = self.ps, 0
        for item in self.order:
            if item[0] == "own":
                next(own, None)
            elif item[0] == "side":
                next(side, None)
            elif item[0] == "shift":
                g = item[1]
                act.wait_ge(self.shift_turned, g + 1)
                if g >= 2:
                    act.wait_ge(self.shift_loaded[g - 2], 16)
                act.activation(self.shiftT[:, g % 2, :], ps[0:SHIFT * GH, 7, :], ACT.Copy)\
                    .then_inc(self.shift_copied, 1)
            elif item[0] == "score":
                _, g, k, p = item
                k0, n = self.keys[k]
                q0 = k0 if self.causal else 0
                act.wait_ge(self.scored, nscore + 1)
                if nscore >= self.npt:
                    act.wait_ge(self.pv_done, (nscore - self.npt) // 2 + 1)
                bank = 2 * (nscore % 2)
                act.activation(self.probs[0:n, nscore % self.npt, :, q0:S], ps[0:n, bank:bank + 2, 0:S - q0],
                               ACT.Exp).then_inc(self.exped, 1)
                nscore += 1
            elif item[0] == "copy":
                g = item[1]
                act.wait_ge(self.pv_done, len(self.keys) * (g + 1))
                if g >= 1:
                    act.wait_ge(self.o_turned, g)
                act.activation(self.oT[:, :], ps[:, 6, :], ACT.Copy).then_inc(self.oT_copied, 1)

    def vector(self, dve, steps, maskq=None, vbias=None, own=iter(()), side=iter(())):
        ps, nmax = self.ps, 0
        for item in self.order:
            if item[0] == "own":
                next(own, None)
            elif item[0] == "side":
                next(side, None)
            elif item[0] == "max":
                g, (j, t, c, n) = item[1], self.units[item[2]]
                dve.wait_ge(self.max_scored, nmax + 1)
                bank = 4 + nmax % 2
                if self.masked:
                    if nmax >= 2:
                        dve.wait_ge(self.max_taken, nmax - 1)
                    dve.tensor_tensor_reduce(self.junk[:, nmax % 2, 0:n], ps[:, bank, 0:n],
                                             maskq[:, t, c * self.chunk:c * self.chunk + n], 1.0, -3.0e38,
                                             ALU.add, ALU.max, self.cmax[:, g % 2, t * GH + j, c:c + 1])\
                        .then_inc(self.max_taken, 1)
                elif self.nchunk > 1:
                    dve.tensor_reduce(self.cmax[:, g % 2, t * GH + j, c:c + 1], ps[:, bank, 0:n], AX.X,
                                      ALU.max).then_inc(self.max_taken, 1)
                else:
                    dve.tensor_reduce(self.nmax[:, g % 2, t, j:j + 1], ps[:, bank, 0:n], AX.X, ALU.max,
                                      negate=True).then_inc(self.max_taken, 1)
                nmax += 1
            elif item[0] == "split":
                g = item[1]
                dve.wait_ge(self.max_taken, nmax)
                nm, rest = self.nmax[:, g % 2], self.rest[:, g % 2]
                if self.nchunk > 1:
                    steps.mark(dve.tensor_reduce(nm.rearrange("p t j -> p (t j)"), self.cmax[:, g % 2], AX.X,
                                                 ALU.max, negate=True))
                    steps.settle()
                if g >= 2:
                    dve.wait_ge(self.shift_turned, g - 1)
                sh = [self.shift[:, g % 2, :, lev * GH:(lev + 1) * GH] for lev in range(SHIFT)]
                steps.mark(dve.tensor_copy(sh[0], nm))
                steps.settle()
                steps.mark(dve.tensor_tensor(rest, nm, sh[0], ALU.subtract))
                steps.settle()
                steps.mark(dve.tensor_copy(sh[1], rest))
                steps.settle()
                dve.tensor_tensor(sh[2], rest, sh[1], ALU.subtract).then_inc(self.shift_split, 1)
            elif item[0] == "post":
                g = item[1]
                dve.wait_ge(self.o_turned, g + 1)
                o = ps[:, 7, :].rearrange("p (t j w) -> p t j w", t=T, j=GH)
                steps.mark(dve.reciprocal(self.inv[:, :, :], o[:, :, :, HD]))
                steps.settle()
                out = self.otok[:, :, g * GH * HD:(g + 1) * GH * HD].rearrange("p t (j d) -> p t j d", j=GH)
                inv = self.inv[:, :, :].rearrange("p t (j o) -> p t j o", o=1).to_broadcast([P, T, GH, HD])
                ins = dve.tensor_tensor(out, o[:, :, :, 0:HD], inv, ALU.mult)
                if vbias is None:
                    ins.then_inc(self.o_divided, 1)
                    continue
                ins.then_inc(self.o_divided, 1)
                dve.wait_ge(self.o_divided, g + 1)
                o3 = self.otok[:, :, g * GH * HD:(g + 1) * GH * HD]
                vb = vbias[:, g * GH * HD:(g + 1) * GH * HD].rearrange("p (o d) -> p o d", o=1)
                steps.mark(dve.tensor_tensor(o3, o3, vb.to_broadcast([P, T, GH * HD]), ALU.add))
        steps.settle()


class OutProjection:

    def __init__(self, st, ps, identf, otok, oF, wo, x, bias=None):
        self.ps, self.identf, self.otok, self.wo, self.x, self.bias = ps, identf, otok, wo, x, bias
        self.oF = oF
        self.o_ready = st.sem("o_ready")
        self.oF_in_psum = st.sem("oF_in_psum")
        self.oF_ready = st.sem("oF_ready")
        self.projected = st.sem("projected")
        self.x_done = st.sem("x_done")

    def tensor(self, pe, turn=True):
        ps = self.ps
        if turn:
            pe.wait_ge(self.o_ready, 1)
            for f in range(FT):
                for t in range(T):
                    mm = pe.transpose(ps[:, f, t * P:(t + 1) * P], self.otok[:, t, f * P:(f + 1) * P],
                                      self.identf[:, :])
                mm.then_inc(self.oF_in_psum, 1)
        for h in range(2):
            for t in (2 * h, 2 * h + 1):
                for f in range(FT):
                    if h == 0 and t == 0:
                        pe.wait_ge(self.oF_ready, f + 1)
                    mm = pe.matmul(ps[:, 2 + h, (t % 2) * D:(t % 2 + 1) * D], self.oF[:, f, t * P:(t + 1) * P],
                                   self.wo[:, f, :], start=(f == 0), stop=(f == FT - 1))
            mm.then_inc(self.projected, 1)

    def scalar(self, act):
        for f in range(FT):
            act.wait_ge(self.oF_in_psum, f + 1)
            act.activation(self.oF[:, f, :], self.ps[:, f, :], ACT.Copy).then_inc(self.oF_ready, 1)

    def vector(self, dve, steps):
        if self.bias is not None:
            for t in range(T):
                steps.mark(dve.tensor_tensor(self.x[:, t, :], self.x[:, t, :], self.bias[:, :], ALU.add))
            steps.settle()
        for h in range(2):
            dve.wait_ge(self.projected, h + 1)
            xs = self.x[:, 2 * h:2 * h + 2, :].rearrange("p t d -> p (t d)")
            dve.tensor_tensor(xs, xs, self.ps[:, 2 + h, :], ALU.add).then_inc(self.x_done, 1)


def load_x(sp, norm, x, src, b):
    sp.dma_start(x[:, :, :], src[b].rearrange("(t p) d -> p t d", p=P)).then_inc(norm.x_loaded, 16)


def keep_residual(nc, pool, residual, x, kept):
    pool.tensor_copy(residual[:, :, :], x[:, :, :]).then_inc(kept, 1)


def store_x(sp, done, count, stored, x, dst, b):
    sp.wait_ge(done, count)
    sp.dma_start(dst[b].rearrange("(t p) d -> p t d", p=P), x[:, :, :]).then_inc(stored, 16)
    sp.wait_ge(stored, 16)


def load_constants(nc, st, tiles):
    loaded = st.sem("constants_loaded")
    with nc.Block() as block:
        @block.sync
        def _(sp):
            for tile, src in tiles:
                sp.dma_start(tile, src).then_inc(loaded, 16)
            sp.wait_ge(loaded, 16 * len(tiles))


def weight(st, tiles, name, src):
    n_in, n_out = src.shape
    if n_in <= P:
        t = st.sb(name, [n_in, n_out])
        tiles.append((t[:, :], src))
    else:
        t = st.sb(name, [P, n_in // P, n_out])
        tiles.append((t[:, :, :], src.rearrange("(f p) n -> p f n", p=P)))
    return t


def column(st, tiles, name, src):
    t = st.sb(name, [P, FT])
    tiles.append((t[:, :], src))
    return t


def constant(st, tiles, name, src, dt=F32):
    t = st.sb(name, list(src.shape), dt)
    tiles.append((t[tuple(slice(None) for _ in src.shape)], src))
    return t


def bias_row(st, tiles, name, src):
    t = st.sb(name, [P, D])
    tiles.append((t[:, :], src.rearrange("(o d) -> o d", o=1).to_broadcast([P, D])))
    return t


def write_ones(nc, att):
    with nc.Block() as block:
        @block.vector
        def _(dve):
            dve.memset(att.kst[STACK:STACK + SHIFT, :, :, :].rearrange("p a b c -> p (a b c)"), 1.0)

        @block.gpsimd
        def _(pool):
            pool.memset(att.v[:, :, :, HD:VW], 1.0)


def v_heads(ps_bank):
    return ps_bank.rearrange("p (t h d) -> p t h d", t=2, h=H)



def latent_attention(nc, w, x_src, x_dst, kscratch, qscratch):
    with ExitStack() as ctx:
        st = Stage(nc, ctx, "s1")
        ps = st.psum()
        loads = []
        identf = constant(st, loads, "identf", w["identf"])
        identb = constant(st, loads, "identb", w["identb"], BF16)
        tri = constant(st, loads, "tri", w["tri"], BF16)
        triT = constant(st, loads, "triT", w["triT"], BF16)
        wdkv = weight(st, loads, "wdkv", w["L0_attn_W_DKV"])
        wuk = weight(st, loads, "wuk", w["L0_attn_W_UK"])
        wuv = weight(st, loads, "wuv", w["L0_attn_W_UV"])
        wuq = weight(st, loads, "wuq", w["L0_attn_W_UQ"])
        wo = weight(st, loads, "wo", w["L0_attn_W_O"])
        x = st.sb("x", [P, T, D])
        residual = st.sb("residual", [P, T, D])
        latent = st.sb("latent", [64, S])
        bank7 = SharedBank(7)
        norm = Norm(st, ps, x, identf, shared=bank7)
        split = Split(st, S, 4)
        att = Attention(st, ps, identf, identb, st.sb("otok", [P, T, D]), S, NG, causal=True, bank7=bank7,
                        own=2, side=12, preloaded=2)
        proj = OutProjection(st, ps, identf, att.otok, st.sb("oF", [P, FT, S]), wo, residual)
        latent_in_psum, latent_ready = st.sem("latent_in_psum"), st.sem("latent_ready")
        qk_in_psum, qk_copied = st.sem("qk_in_psum"), st.sem("qk_copied")
        v_in_psum, kept = st.sem("v_in_psum"), st.sem("kept")
        dve_steps, act_steps, stored = st.sem("dve_steps"), st.sem("act_steps"), st.sem("stored")
        side_dve_steps = st.sem("side_dve_steps")
        load_constants(nc, st, loads)
        write_ones(nc, att)
        att.own_ready = (att.v_ready, 2)

        def prologue_sync(sp, b, first):
            if not first:
                sp.wait_ge(kept, 1)
            load_x(sp, norm, x, x_src, b)
            yield from skip(1 + Norm.STEPS + 1)
            for i, (f, is_q) in enumerate(ITEMS):
                split.sync(sp, i, S, (qscratch if is_q else kscratch)[b], (8 * f, 8 * f + 8),
                           Q_LAYOUT if is_q else K_LAYOUT)
                yield
            split.wait_in_dram(sp, (0, 1))
            for g in range(att.preloaded):
                att.preload(sp, g, kscratch[b], qscratch[b], S, first)
            yield
            split.wait_in_dram(sp, (2, 3))
            sp.wait_ge(att.stacks_preloaded, 32 * att.preloaded)

        def prologue_tensor(pe, b, first):
            yield
            yield from norm.tensor(pe)
            bank7.take(pe)
            for c in range(FT):
                pe.wait_ge(norm.xnT_ready, c + 1)
                mm = pe.matmul(ps[0:64, 7, :], wdkv[:, c, :], norm.xnT[:, c, 1:], start=(c == 0), stop=(c == 1))
            mm.then_inc(latent_in_psum, 1)
            bank7.freed_by(latent_ready, 1)
            yield
            for i, (f, is_q) in enumerate(ITEMS):
                bank7.take(pe)
                if is_q:
                    for c in range(FT):
                        mm = pe.matmul(ps[:, 7, :], wuq[:, c, f * P:(f + 1) * P], norm.xnT[:, c, 1:],
                                       start=(c == 0), stop=(c == 1))
                else:
                    pe.wait_ge(latent_ready, 1)
                    mm = pe.matmul(ps[:, 7, :], wuk[:, f * P:(f + 1) * P], latent[:, :], start=True, stop=True)
                mm.then_inc(qk_in_psum, 1)
                bank7.freed_by(qk_copied, i + 1)
                yield
            yield

        def prologue_scalar(act, b, first):
            steps = Steps(act, act_steps)
            if first:
                act.preload_act_table_set(EXP_AND_LN)
            yield
            yield from norm.scalar(act, steps)
            act.wait_ge(latent_in_psum, 1)
            act.activation(latent[:, :], ps[0:64, 7, :], ACT.Copy).then_inc(latent_ready, 1)
            yield
            for i, (f, is_q) in enumerate(ITEMS):
                act.wait_ge(qk_in_psum, i + 1)
                if i >= 2:
                    act.wait_ge(split.levels_ready, i - 1)
                act.activation(split.full[:, i % 2, :], ps[:, 7, :], ACT.Copy,
                               scale=HD ** -0.5 if is_q else 1.0).then_inc(qk_copied, 1)
                act.wait_ge(qk_copied, i + 1)
                act.sem_inc(split.full_ready, 1)
                split.scalar(act, i, S)
                yield
            yield

        def prologue_vector(dve, b, first):
            steps = Steps(dve, side_dve_steps)
            yield
            yield from norm.vector(dve, steps)
            yield
            for i in range(4):
                split.vector(dve, steps, i, S)
                yield
            yield

        def sync(sp, b, side):
            side = side()
            for g in range(att.preloaded, NG):
                att.load_stacks(sp, g, kscratch[b], qscratch[b], S)
            att.sync(sp, side=side)
            store_x(sp, proj.x_done, 2, stored, residual, x_dst, b)
            exhaust(side)

        def tensor(pe, b, side):
            att.tensor(pe, tri=tri, triT=triT, own=v_tensor(pe), side=side())
            proj.tensor(pe)

        def v_tensor(pe):
            for t in range(T):
                mm = pe.matmul(ps[:, t // 2, (t % 2) * D:(t % 2 + 1) * D], latent[:, t * P:(t + 1) * P],
                               wuv[:, :], start=True, stop=True)
                if t % 2:
                    mm.then_inc(v_in_psum, 1)
                    yield

        def v_scalar(act):
            for n in range(2):
                act.wait_ge(v_in_psum, n + 1)
                act.activation(att.v[:, 2 * n:2 * n + 2, :, 0:HD], v_heads(ps[:, n, :]), ACT.Copy)\
                    .then_inc(att.v_ready, 1)
                yield

        def scalar(act, b, side):
            act.preload_act_table_set(EXP_AND_LN)
            att.scalar(act, own=v_scalar(act), side=side())
            proj.scalar(act)

        def vector(dve, b, side):
            steps = Steps(dve, dve_steps)
            att.vector(dve, steps, side=side())
            dve.wait_ge(att.o_divided, NG)
            dve.sem_inc(proj.o_ready, 1)
            dve.wait_ge(kept, 1)
            proj.vector(dve, steps)

        def gpsimd(pool, b, side):
            keep_residual(nc, pool, residual, x, kept)

        pipelined_loop(nc, st,
                       {"sync": prologue_sync, "tensor": prologue_tensor, "scalar": prologue_scalar,
                        "vector": prologue_vector, "gpsimd": lambda pool, b, first: skip(0)},
                       {"sync": sync, "tensor": tensor, "scalar": scalar, "vector": vector, "gpsimd": gpsimd})



def cross_attention(nc, w, x_src, x_dst, kscratch, qscratch):
    with ExitStack() as ctx:
        st = Stage(nc, ctx, "s2")
        ps = st.psum()
        loads = []
        identf = constant(st, loads, "identf", w["identf"])
        identb = constant(st, loads, "identb", w["identb"], BF16)
        wq = weight(st, loads, "wq", w["L0_xattn_Wq"])
        wk = weight(st, loads, "wk", w["L0_xattn_Wk"])
        wv = weight(st, loads, "wv", w["L0_xattn_Wv"])
        wo = weight(st, loads, "wo", w["L0_xattn_Wo"])
        bq = column(st, loads, "bq", w["L0_xattn_bq"])
        bk = column(st, loads, "bk", w["L0_xattn_bk"])
        bv = bias_row(st, loads, "bv", w["L0_xattn_bv"])
        bo = bias_row(st, loads, "bo", w["L0_xattn_bo"])
        x = st.sb("x", [P, T, D])
        ctxT = st.sb("ctxT", [P, FT, CTX])
        maskq = st.sb("maskq", [P, T, CTX])
        keys = tiles_of(CTX)
        residual = st.sb("residual", [P, T, D])
        bank7 = SharedBank(7)
        norm = Norm(st, ps, x, identf, shared=bank7)
        split = Split(st, CTX, 4, bufs=1)
        pieces = [(c, min(512, CTX - c)) for c in range(0, CTX, 512)]
        jobs = [(i, f, is_q, c, n) for i, (f, is_q) in enumerate(ITEMS)
                for c, n in ([(0, S)] if is_q else pieces)]
        att = Attention(st, ps, identf, identb, st.sb("otok", [P, T, D]), CTX, NG, causal=False, masked=True,
                        bank7=bank7, own=len(keys), side=1 + Norm.STEPS + len(jobs) + 1,
                        side_until=0.7, late=2, preloaded=NG)
        proj = OutProjection(st, ps, identf, att.otok, st.sb("oF", [P, FT, S]), wo, residual, bias=bo)
        most, least, nonzero = st.sb("most", [P, 1]), st.sb("least", [P, 1]), st.sb("nonzero", [P, 1])
        flag = st.sb("flag", [1, 1], U32)
        ctx_loaded, mask_loaded = st.sem("ctx_loaded"), st.sem("mask_loaded")
        nonzero_ready, count_in_psum, flag_ready = st.sem("nonzero_ready"), st.sem("count_in_psum"), st.sem("flag_ready")
        flag_read = st.sem("flag_read")
        proj_in_psum, proj_copied = st.sem("proj_in_psum"), st.sem("proj_copied")
        v_in_psum, kept = st.sem("v_in_psum"), st.sem("kept")
        dve_steps, act_steps, stored = st.sem("dve_steps"), st.sem("act_steps"), st.sem("stored")
        side_dve_steps = st.sem("side_dve_steps")
        load_constants(nc, st, loads)
        write_ones(nc, att)
        att.own_ready = (att.v_ready, len(keys))
        sp_register = {}
        all_units, all_steps = NG * len(att.units), NG * 2 * len(keys)

        def prologue_sync(sp, b, first):
            if not first:
                sp.wait_ge(kept, 1)
            load_x(sp, norm, x, x_src, b)
            if not first:
                sp.wait_ge(v_in_psum, len(keys))
            for f in range(FT):
                sp.dma_start(ctxT[:, f, :], w["ctxT"][b, f * P:(f + 1) * P, :]).then_inc(ctx_loaded, 16)
            yield from skip(1 + Norm.STEPS)
            for i, f, is_q, c, n in jobs:
                if c + n == (S if is_q else CTX):
                    split.sync(sp, i, c + n, (qscratch if is_q else kscratch)[b], (8 * f, 8 * f + 8),
                               Q_LAYOUT if is_q else K_LAYOUT)
                yield
            split.wait_in_dram(sp, (0, 1))
            for g in (0, 1):
                att.preload(sp, g, kscratch[b], qscratch[b], CTX, first)
            yield
            if first:
                load_mask(sp, b)
            else:
                load_mask_late(sp, b)
            yield
            split.wait_in_dram(sp, (2, 3))
            for g in (2, 3):
                att.preload(sp, g, kscratch[b], qscratch[b], CTX, first)
            sp.wait_ge(att.stacks_preloaded, 32 * NG)

        def prologue_tensor(pe, b, first):
            yield
            yield from norm.tensor(pe)
            for number, (i, f, is_q, c, n) in enumerate(jobs):
                bank7.take(pe)
                if number == 0:
                    pe.wait_ge(ctx_loaded, 16 * FT)
                    pe.wait_ge(norm.xnT_ready, FT)
                for h in range(FT):
                    if is_q:
                        mm = pe.matmul(ps[:, 7, :], wq[:, h, f * P:(f + 1) * P], norm.xnT[:, h, 1:],
                                       start=(h == 0), stop=(h == 1))
                    else:
                        mm = pe.matmul(ps[:, 7, 0:n], wk[:, h, f * P:(f + 1) * P], ctxT[:, h, c:c + n],
                                       start=(h == 0), stop=(h == 1))
                mm.then_inc(proj_in_psum, 1)
                bank7.freed_by(proj_copied, number + 1)
                yield
            yield from skip(2)
            bank7.take(pe)
            pe.wait_ge(nonzero_ready, 1)
            pe.matmul(ps[0:1, 7, 0:1], nonzero[:, :], att.v[:, 0, 0, HD:HD + 1], start=True, stop=True)\
                .then_inc(count_in_psum, 1)
            bank7.freed_by(flag_ready, 1)
            yield

        def prologue_scalar(act, b, first):
            steps = Steps(act, act_steps)
            if first:
                act.preload_act_table_set(EXP_AND_LN)
            yield
            yield from norm.scalar(act, steps)
            for number, (i, f, is_q, c, n) in enumerate(jobs):
                act.wait_ge(proj_in_psum, number + 1)
                if i >= 1 and c == 0:
                    act.wait_ge(split.levels_ready, i)
                act.activation(split.full[:, 0, c:c + n], ps[:, 7, 0:n], ACT.Identity,
                               bias=(bq if is_q else bk)[:, f:f + 1]).then_inc(proj_copied, 1)
                if c + n == (S if is_q else CTX):
                    act.wait_ge(proj_copied, number + 1)
                    if is_q:
                        steps.mark(act.activation(split.full[:, 0, 0:S], split.full[:, 0, 0:S],
                                                  ACT.Copy, scale=HD ** -0.5))
                        steps.settle()
                    act.sem_inc(split.full_ready, 1)
                    split.scalar(act, i, c + n)
                yield
            yield from skip(3)

        def prologue_vector(dve, b, first):
            steps = Steps(dve, side_dve_steps)
            yield
            yield from norm.vector(dve, steps)
            for i, f, is_q, c, n in jobs:
                if c + n == (S if is_q else CTX):
                    split.vector(dve, steps, i, c + n)
                yield
            yield
            dve.wait_ge(mask_loaded, 16)
            steps.mark(dve.tensor_reduce(most[:, :], maskq[:, :, :], AX.XY, ALU.max))
            steps.mark(dve.tensor_reduce(least[:, :], maskq[:, :, :], AX.XY, ALU.min))
            steps.settle()
            steps.mark(dve.tensor_scalar(least[:, :], least[:, :], 0.0, None, ALU.is_lt))
            steps.settle()
            dve.scalar_tensor_tensor(out=nonzero[:, :], in0=most[:, :], scalar=0.0, in1=least[:, :],
                                     op0=ALU.is_gt, op1=ALU.add).then_inc(nonzero_ready, 1)
            yield
            dve.wait_ge(count_in_psum, 1)
            if not first:
                dve.wait_ge(flag_read, 1)
            dve.tensor_copy(flag[:, :], ps[0:1, 7, 0:1]).then_inc(flag_ready, 1)
            yield

        def load_mask(sp, b):
            sp.dma_start(maskq[:, :, :], w["mask"][b].rearrange("(t p) k -> p t k", p=P)).then_inc(mask_loaded, 16)

        def load_mask_early(sp, b):
            with sp.If(sp_register["flag"] == 0):
                sp.wait_ge(att.max_taken, all_units)
                load_mask(sp, b)

        def load_mask_late(sp, b):
            with sp.If(sp_register["flag"] != 0):
                sp.wait_ge(att.scored, all_steps)
                sp.wait_ge(att.max_taken, all_units)
                load_mask(sp, b)

        def sync(sp, b, side):
            side, more = side(), side is not NO_SIDE
            sp_register["flag"] = sp.value_load(flag[0:1, 0:1])
            sp.sem_inc(flag_read, 1)
            att.sync(sp, side=side, after_shifts=(lambda: load_mask_early(sp, b + 1)) if more else None)
            store_x(sp, proj.x_done, 2, stored, residual, x_dst, b)
            exhaust(side)

        def tensor(pe, b, side):
            any_mask = pe.value_load(flag[0:1, 0:1])
            with pe.If(any_mask != 0):
                att.tensor(pe, maskq=maskq, own=v_tensor(pe), side=side())
            with pe.Else():
                att.tensor(pe, own=v_tensor(pe), side=side())
            proj.tensor(pe)

        def v_tensor(pe):
            for k, (k0, n) in enumerate(keys):
                if k >= 4:
                    pe.wait_ge(att.v_ready, k - 3)
                for h in range(FT):
                    mm = pe.matmul(ps[0:n, k % 4, 0:D], ctxT[:, h, k0:k0 + n], wv[:, h, :],
                                   start=(h == 0), stop=(h == 1))
                mm.then_inc(v_in_psum, 1)
                yield

        def v_scalar(act):
            for k, (k0, n) in enumerate(keys):
                act.wait_ge(v_in_psum, k + 1)
                act.activation(att.v[0:n, k, :, 0:HD], ps[0:n, k % 4, 0:D].rearrange("p (h d) -> p h d", h=H),
                               ACT.Copy).then_inc(att.v_ready, 1)
                yield

        def scalar(act, b, side):
            act.preload_act_table_set(EXP_AND_LN)
            att.scalar(act, own=v_scalar(act), side=side())
            proj.scalar(act)

        def vector(dve, b, side):
            steps = Steps(dve, dve_steps)
            att.vector(dve, steps, maskq=maskq, vbias=bv, side=side())
            dve.sem_inc(proj.o_ready, 1)
            dve.wait_ge(kept, 1)
            proj.vector(dve, steps)

        def gpsimd(pool, b, side):
            keep_residual(nc, pool, residual, x, kept)

        pipelined_loop(nc, st,
                       {"sync": prologue_sync, "tensor": prologue_tensor, "scalar": prologue_scalar,
                        "vector": prologue_vector, "gpsimd": lambda pool, b, first: skip(0)},
                       {"sync": sync, "tensor": tensor, "scalar": scalar, "vector": vector, "gpsimd": gpsimd})



def channel_mix(nc, w, x_src, x_dst):
    with ExitStack() as ctx:
        st = Stage(nc, ctx, "s3")
        ps = st.psum()
        loads = []
        identf = constant(st, loads, "identf", w["identf"])
        wr = weight(st, loads, "wr", w["L0_ffn_W_r"])
        wk = weight(st, loads, "wk", w["L0_ffn_W_k"])
        wv = weight(st, loads, "wv", w["L0_ffn_W_v"])
        mu_r = column(st, loads, "mu_r", w["L0_ffn_mu_r"])
        mu_k = column(st, loads, "mu_k", w["L0_ffn_mu_k"])
        x = st.sb("x", [P, T, D])
        norm = Norm(st, ps, x, identf)
        step = st.sb("step", [P, FT, S])
        xr, xk = st.sb("xr", [P, FT, S]), st.sb("xk", [P, FT, S])
        act_k = st.sb("act_k", [P, FT, S])
        gate = st.sb("gate", [P, T, D])
        part = st.sb("part", [P, T, D])
        xk_ready, xr_ready = st.sem("xk_ready"), st.sem("xr_ready")
        k_in_psum, k_relu, act_k_ready = st.sem("k_in_psum"), st.sem("k_relu"), st.sem("act_k_ready")
        r_in_psum, gate_ready, v_in_psum = st.sem("r_in_psum"), st.sem("gate_ready"), st.sem("v_in_psum")
        x_done, gated = st.sem("x_done"), st.sem("gated")
        dve_steps, act_steps, stored = st.sem("dve_steps"), st.sem("act_steps"), st.sem("stored")
        load_constants(nc, st, loads)
        with nc.Block() as block:
            @block.vector
            def _(dve):
                dve.memset(norm.xnT[:, :, 0:1], 0.0)

        def sync(sp, b):
            load_x(sp, norm, x, x_src, b)
            store_x(sp, x_done, 2, stored, x, x_dst, b)

        def tensor(pe):
            exhaust(norm.tensor(pe))
            for f in range(FT):
                for c in range(FT):
                    if f == 0:
                        pe.wait_ge(xk_ready, c + 1)
                    mm = pe.matmul(ps[:, 2 + f, :], wk[:, c, f * P:(f + 1) * P], xk[:, c, :],
                                   start=(c == 0), stop=(c == 1))
                mm.then_inc(k_in_psum, 1)
            pe.wait_ge(xr_ready, FT)
            for src, wt, base, done in ((xr, wr, 4, r_in_psum), (act_k, wv, 6, v_in_psum)):
                for t in range(T):
                    for c in range(FT):
                        if src is act_k and t == 0:
                            pe.wait_ge(act_k_ready, c + 1)
                        mm = pe.matmul(ps[:, base + t // 2, (t % 2) * D:(t % 2 + 1) * D],
                                       src[:, c, t * P:(t + 1) * P], wt[:, c, :], start=(c == 0), stop=(c == 1))
                    if t % 2:
                        mm.then_inc(done, 1)

        def scalar(act):
            act.preload_act_table_set(EXP_AND_LN)
            steps = Steps(act, act_steps)
            exhaust(norm.scalar(act, steps))
            for f in range(FT):
                act.wait_ge(k_in_psum, f + 1)
                act.activation(act_k[:, f, :], ps[:, 2 + f, :], ACT.Relu).then_inc(k_relu, 1)
            for f in range(FT):
                act.wait_ge(k_relu, f + 1)
                act.activation(act_k[:, f, :], act_k[:, f, :], ACT.Square).then_inc(act_k_ready, 1)
            for h in range(2):
                act.wait_ge(r_in_psum, h + 1)
                act.activation(gate[:, 2 * h:2 * h + 2, :], ps[:, 4 + h, :].rearrange("p (t d) -> p t d", t=2),
                               ACT.Tanh, scale=0.5).then_inc(gate_ready, 1)

        def vector(dve):
            steps = Steps(dve, dve_steps)
            exhaust(norm.vector(dve, steps))
            for f in range(FT):
                dve.wait_ge(norm.xnT_ready, f + 1)
                cur, prev = norm.xnT[:, f, 1:S + 1], norm.xnT[:, f, 0:S]
                steps.mark(dve.tensor_tensor(step[:, f, :], cur, prev, ALU.subtract))
                steps.settle()
                dve.scalar_tensor_tensor(out=xk[:, f, :], in0=step[:, f, :], scalar=mu_k[:, f:f + 1], in1=prev,
                                         op0=ALU.mult, op1=ALU.add).then_inc(xk_ready, 1)
            for f in range(FT):
                dve.scalar_tensor_tensor(out=xr[:, f, :], in0=step[:, f, :], scalar=mu_r[:, f:f + 1],
                                         in1=norm.xnT[:, f, 0:S], op0=ALU.mult, op1=ALU.add).then_inc(xr_ready, 1)
            for h in range(2):
                dve.wait_ge(gate_ready, h + 1)
                dve.wait_ge(v_in_psum, h + 1)
                two = slice(2 * h, 2 * h + 2)
                dve.scalar_tensor_tensor(out=part[:, two, :], in0=gate[:, two, :], scalar=1.0,
                                         in1=ps[:, 6 + h, :].rearrange("p (t d) -> p t d", t=2), op0=ALU.add,
                                         op1=ALU.mult).then_inc(gated, 1)
                dve.wait_ge(gated, h + 1)
                dve.scalar_tensor_tensor(out=x[:, two, :], in0=part[:, two, :], scalar=0.5, in1=x[:, two, :],
                                         op0=ALU.mult, op1=ALU.add).then_inc(x_done, 1)

        stage_loop(nc, st, {"sync": sync, "tensor": tensor, "scalar": scalar, "vector": vector})



def linear_attention(nc, w, x_src, x_dst):
    with ExitStack() as ctx:
        st = Stage(nc, ctx, "s5")
        ps = st.psum()
        loads = []
        identf = constant(st, loads, "identf", w["identf"])
        blocks = constant(st, loads, "blocks", w["blocks"])
        wq = weight(st, loads, "wq", w["L1_xattn_Wq"])
        wk = weight(st, loads, "wk", w["L1_xattn_Wk"])
        wv = weight(st, loads, "wv", w["L1_xattn_Wv"])
        wo = weight(st, loads, "wo", w["L1_xattn_Wo"])
        bq = column(st, loads, "bq", w["L1_xattn_bq"])
        bk = bias_row(st, loads, "bk", w["L1_xattn_bk"])
        bv = bias_row(st, loads, "bv", w["L1_xattn_bv"])
        bo = bias_row(st, loads, "bo", w["L1_xattn_bo"])
        keys = tiles_of(CTX)
        x = st.sb("x", [P, T, D])
        ctxT = st.sb("ctxT", [P, FT, CTX])
        bank7 = SharedBank(7)
        norm = Norm(st, ps, x, identf, shared=bank7)
        kraw = st.sb("kraw", [P, 2, D])
        kexp = st.sb("kexp", [P, 2, D])
        k = st.sb("k", [P, 2, D])
        ksq = st.sb("ksq", [P, 2, D])
        v = st.sb("v", [P, 2, D])
        ones = st.sb("ones", [P, 1])
        qraw, qexp = st.sb("qraw", [P, FT, S]), st.sb("qexp", [P, FT, S])
        q, qsq, qn = st.sb("q", [P, FT, S]), st.sb("qsq", [P, FT, S]), st.sb("qn", [P, FT, S])
        kv = st.sb("kv", [P, FT, P])
        knorm, kinv = st.sb("knorm", [P, FT]), st.sb("kinv", [P, FT])
        proj = OutProjection(st, ps, identf, norm.xn, st.sb("oF", [P, FT, S]), wo, x, bias=bo)
        ctx_loaded = st.sem("ctx_loaded")
        kv_in_psum, kraw_ready, kexp_ready = st.sem("kv_in_psum"), st.sem("kraw_ready"), st.sem("kexp_ready")
        k_ready, v_ready, ksq_ready = st.sem("k_ready"), st.sem("v_ready"), st.sem("ksq_ready")
        kv_added, ones_ready = st.sem("kv_added"), st.sem("ones_ready")
        q_in_psum, qraw_ready, qexp_ready = st.sem("q_in_psum"), st.sem("qraw_ready"), st.sem("qexp_ready")
        q_ready, qsq_ready, qsum_in_psum = st.sem("q_ready"), st.sem("qsq_ready"), st.sem("qsum_in_psum")
        qinv_ready, qn_ready, kv_ready = st.sem("qinv_ready"), st.sem("qn_ready"), st.sem("kv_ready")
        ksum_copied, kinv_ready = st.sem("ksum_copied"), st.sem("kinv_ready")
        norm_dve_steps = st.sem("norm_dve_steps")
        dve_steps, act_steps, stored = st.sem("dve_steps"), st.sem("act_steps"), st.sem("stored")
        load_constants(nc, st, loads)
        with nc.Block() as block:
            @block.vector
            def _(dve):
                dve.memset(ones[:, :], 1.0)

        def prologue_sync(sp, b, first):
            if not first:
                sp.wait_ge(kv_in_psum, len(keys))
            for f in range(FT):
                sp.dma_start(ctxT[:, f, :], w["ctxT"][b, f * P:(f + 1) * P, :]).then_inc(ctx_loaded, 16)
            yield
            sp.wait_ge(ctx_loaded, 16 * FT)

        def nothing(e, b, first):
            yield

        def sync(sp, b, side):
            side = side()
            load_x(sp, norm, x, x_src, b)
            next(side, None)
            store_x(sp, proj.x_done, 2, stored, x, x_dst, b)
            exhaust(side)

        def tensor(pe, b, side):
            bank7.freed = None
            norming = norm.tensor(pe)

            def accumulate(i):
                n = keys[i][1]
                pe.wait_ge(k_ready, i + 1)
                pe.wait_ge(v_ready, i + 1)
                pe.wait_ge(ksq_ready, i + 1)
                for f in range(FT):
                    pe.matmul(ps[:, 4 + f, 0:P], k[0:n, i % 2, f * P:(f + 1) * P], v[0:n, i % 2, f * P:(f + 1) * P],
                              start=(i == 0), stop=(i == len(keys) - 1))
                for f in range(FT):
                    mm = pe.matmul(ps[:, f, 0:1], ksq[0:n, i % 2, f * P:(f + 1) * P], ones[0:n, :],
                                   start=(i == 0), stop=(i == len(keys) - 1))
                mm.then_inc(kv_added, 1)

            for i, (k0, n) in enumerate(keys):
                if i >= 2:
                    pe.wait_ge(kraw_ready, i - 1)
                    pe.wait_ge(v_ready, i - 1)
                for c, wt in enumerate((wk, wv)):
                    for f in range(FT):
                        mm = pe.matmul(ps[0:n, 2 + i % 2, c * D:(c + 1) * D], ctxT[:, f, k0:k0 + n], wt[:, f, :],
                                       start=(f == 0), stop=(f == 1))
                mm.then_inc(kv_in_psum, 1)
                if i >= 1:
                    accumulate(i - 1)
                if i >= 2:
                    next(norming, None)
            exhaust(norming)
            pe.wait_ge(norm.xnT_ready, FT)
            for f in range(FT):
                for c in range(FT):
                    mm = pe.matmul(ps[:, 6 + f, :], wq[:, c, f * P:(f + 1) * P], norm.xnT[:, c, 1:],
                                   start=(c == 0), stop=(c == 1))
                mm.then_inc(q_in_psum, 1)
            accumulate(len(keys) - 1)
            pe.wait_ge(kraw_ready, len(keys))
            pe.wait_ge(v_ready, len(keys))
            for f in range(FT):
                pe.wait_ge(qsq_ready, f + 1)
                pe.matmul(ps[:, 2 + f, :], blocks[:, :], qsq[:, f, :], start=True, stop=True)\
                    .then_inc(qsum_in_psum, 1)
            for f in range(FT):
                pe.wait_ge(qn_ready, f + 1)
                pe.wait_ge(kv_ready, f + 1)
                pe.wait_ge(ksum_copied, FT)
                pe.matmul(ps[:, f, :], kv[:, f, :], qn[:, f, :], start=True, stop=True)\
                    .then_inc(proj.oF_in_psum, 1)
            pe.wait_ge(qinv_ready, FT)
            proj.tensor(pe, turn=False)

        def scalar(act, b, side):
            act.preload_act_table_set(EXP_AND_LN)
            steps = Steps(act, act_steps)
            norming = norm.scalar(act, steps)
            for i, (k0, n) in enumerate(keys):
                act.wait_ge(kraw_ready, i + 1)
                if i >= 2:
                    act.wait_ge(k_ready, i - 1)
                act.activation(kexp[0:n, i % 2, :], kraw[0:n, i % 2, :], ACT.Exp).then_inc(kexp_ready, 1)
                act.wait_ge(k_ready, i + 1)
                if i >= 2:
                    act.wait_ge(kv_added, i - 1)
                act.activation(ksq[0:n, i % 2, :], k[0:n, i % 2, :], ACT.Square).then_inc(ksq_ready, 1)
                if i >= 2:
                    next(norming, None)
            exhaust(norming)
            for f in range(FT):
                act.wait_ge(q_in_psum, f + 1)
                act.activation(qraw[:, f, :], ps[:, 6 + f, :], ACT.Identity, bias=bq[:, f:f + 1])\
                    .then_inc(qraw_ready, 1)
            for f in range(FT):
                act.wait_ge(qraw_ready, f + 1)
                act.activation(qexp[:, f, :], qraw[:, f, :], ACT.Exp).then_inc(qexp_ready, 1)
            for f in range(FT):
                act.wait_ge(q_ready, f + 1)
                act.activation(qsq[:, f, :], q[:, f, :], ACT.Square).then_inc(qsq_ready, 1)
            for f in range(FT):
                act.wait_ge(qsum_in_psum, f + 1)
                steps.mark(act.activation(qsq[:, f, :], ps[:, 2 + f, :], ACT.Ln, scale=float(HD)))
                steps.settle()
                act.activation(qsq[:, f, :], qsq[:, f, :], ACT.Exp, scale=-0.5).then_inc(qinv_ready, 1)
            act.wait_ge(ksum_copied, FT)
            steps.mark(act.activation(knorm[:, :], knorm[:, :], ACT.Ln, scale=float(S)))
            steps.settle()
            act.activation(kinv[:, :], knorm[:, :], ACT.Exp, scale=-0.5).then_inc(kinv_ready, 1)
            proj.scalar(act)

        def vector(dve, b, side):
            steps = Steps(dve, dve_steps)
            norming = norm.vector(dve, Steps(dve, norm_dve_steps))

            def elu(i, n):
                dve.wait_ge(kexp_ready, i + 1)
                steps.mark(dve.tensor_scalar(kraw[0:n, i % 2, :], kraw[0:n, i % 2, :], 0.0, -1.0, ALU.max, ALU.add))
                steps.settle()
                dve.scalar_tensor_tensor(out=k[0:n, i % 2, :], in0=kexp[0:n, i % 2, :], scalar=1.0,
                                         in1=kraw[0:n, i % 2, :], op0=ALU.min, op1=ALU.add).then_inc(k_ready, 1)

            for i, (k0, n) in enumerate(keys):
                dve.wait_ge(kv_in_psum, i + 1)
                if i >= 2:
                    dve.wait_ge(kv_added, i - 1)
                    dve.wait_ge(ksq_ready, i - 1)
                dve.tensor_tensor(kraw[0:n, i % 2, :], ps[0:n, 2 + i % 2, 0:D], bk[0:n, :], ALU.add)\
                    .then_inc(kraw_ready, 1)
                dve.tensor_tensor(v[0:n, i % 2, :], ps[0:n, 2 + i % 2, D:2 * D], bv[0:n, :], ALU.add)\
                    .then_inc(v_ready, 1)
                elu(i, n)
                if i >= 2:
                    next(norming, None)
            exhaust(norming)
            for f in range(FT):
                dve.wait_ge(qexp_ready, f + 1)
                steps.mark(dve.tensor_scalar(qraw[:, f, :], qraw[:, f, :], 0.0, -1.0, ALU.max, ALU.add))
                steps.settle()
                dve.scalar_tensor_tensor(out=q[:, f, :], in0=qexp[:, f, :], scalar=1.0, in1=qraw[:, f, :],
                                         op0=ALU.min, op1=ALU.add).then_inc(q_ready, 1)
            dve.wait_ge(kv_added, len(keys))
            for f in range(FT):
                dve.tensor_copy(knorm[:, f:f + 1], ps[:, f, 0:1]).then_inc(ksum_copied, 1)
            dve.wait_ge(kinv_ready, 1)
            for f in range(FT):
                dve.scalar_tensor_tensor(out=kv[:, f, :], in0=ps[:, 4 + f, 0:P], scalar=kinv[:, f:f + 1],
                                         in1=blocks[:, :], op0=ALU.mult, op1=ALU.mult).then_inc(kv_ready, 1)
            for f in range(FT):
                dve.wait_ge(qinv_ready, f + 1)
                dve.tensor_tensor(qn[:, f, :], q[:, f, :], qsq[:, f, :], ALU.mult).then_inc(qn_ready, 1)
            proj.vector(dve, steps)

        pipelined_loop(nc, st,
                       {"sync": prologue_sync, "tensor": nothing, "scalar": nothing, "vector": nothing,
                        "gpsimd": nothing},
                       {"sync": sync, "tensor": tensor, "scalar": scalar, "vector": vector,
                        "gpsimd": lambda pool, b, side: None})



class Rotary:

    def __init__(self, st, ps, split, bank7, cos, sin):
        self.ps, self.split, self.bank7, self.cos, self.sin = ps, split, bank7, cos, sin
        self.part = st.sb("rot_part", [P, S])
        self.in_psum = st.sem("rot_in_psum")
        self.taken = st.sem("rot_taken")

    def hand_over(self, product, n):
        product.then_inc(self.in_psum, 1)
        self.bank7.freed_by(self.taken, n + 1)

    def vector_a(self, dve, steps, i, scale):
        dve.wait_ge(self.in_psum, 2 * i + 1)
        steps.settle()
        dve.scalar_tensor_tensor(out=self.split.full[:, i % 2, :], in0=self.ps[:, 7, :], scalar=scale,
                                 in1=self.cos[:, :], op0=ALU.mult, op1=ALU.mult).then_inc(self.taken, 1)

    def vector_b(self, dve, steps, i, scale):
        full = self.split.full[:, i % 2, :]
        dve.wait_ge(self.in_psum, 2 * i + 2)
        dve.scalar_tensor_tensor(out=self.part[:, :], in0=self.ps[:, 7, :], scalar=scale,
                                 in1=self.sin[:, :], op0=ALU.mult, op1=ALU.mult).then_inc(self.taken, 1)
        dve.wait_ge(self.taken, 2 * i + 2)
        steps.mark(dve.tensor_tensor(full, full, self.part[:, :], ALU.add))
        steps.settle()



def rotary_latent_attention(nc, w, x_src, x_dst, kscratch, qscratch):
    with ExitStack() as ctx:
        st = Stage(nc, ctx, "s6")
        ps = st.psum()
        loads = []
        identf = constant(st, loads, "identf", w["identf"])
        identb = constant(st, loads, "identb", w["identb"], BF16)
        tri = constant(st, loads, "tri", w["tri"], BF16)
        triT = constant(st, loads, "triT", w["triT"], BF16)
        cos = constant(st, loads, "cos", w["mla_cos"])
        sin = constant(st, loads, "sin", w["mla_sin"])
        w_ln = column(st, loads, "w_ln", w["L1_ffn_w_ln1"])
        wkvd = weight(st, loads, "wkvd", w["L1_ffn_W_kvd"])
        wqd = weight(st, loads, "wqd", w["L1_ffn_W_qd"])
        wku = weight(st, loads, "wku", w["mla_wku"])
        wkr = weight(st, loads, "wkr", w["mla_wkr"])
        wkr_p = weight(st, loads, "wkr_p", w["mla_wkr_partner"])
        wq = weight(st, loads, "wq", w["mla_wq"])
        wq_p = weight(st, loads, "wq_p", w["mla_wq_partner"])
        wvu = weight(st, loads, "wvu", w["L1_ffn_W_vu"])
        wo = weight(st, loads, "wo", w["L1_ffn_W_o"])
        x = st.sb("x", [P, T, D])
        residual = st.sb("residual", [P, T, D])
        kv_latent, q_latent = st.sb("kv_latent", [64, S]), st.sb("q_latent", [64, S])
        bank7 = SharedBank(7)
        norm = Norm(st, ps, x, identf, rms=True, weight=w_ln, shared=bank7)
        split = Split(st, S, 4)
        rotary = Rotary(st, ps, split, bank7, cos, sin)
        att = Attention(st, ps, identf, identb, st.sb("otok", [P, T, D]), S, NG, causal=True, bank7=bank7,
                        own=2, side=1 + Norm.OUTER_STEPS + Norm.STEPS + 2 + 8 + 1, preloaded=2)
        proj = OutProjection(st, ps, identf, att.otok, st.sb("oF", [P, FT, S]), wo, residual)
        latent_in_psum, latent_ready = st.sem("latent_in_psum"), st.sem("latent_ready")
        v_in_psum, kept = st.sem("v_in_psum"), st.sem("kept")
        dve_steps, act_steps, stored = st.sem("dve_steps"), st.sem("act_steps"), st.sem("stored")
        side_dve_steps = st.sem("side_dve_steps")
        load_constants(nc, st, loads)
        write_ones(nc, att)
        att.own_ready = (att.v_ready, 2)

        def prologue_sync(sp, b, first):
            if not first:
                sp.wait_ge(kept, 1)
            load_x(sp, norm, x, x_src, b)
            yield from skip(1 + Norm.OUTER_STEPS + Norm.STEPS + 2)
            for i, (f, is_q) in enumerate(ITEMS):
                yield
                split.sync(sp, i, S, (qscratch if is_q else kscratch)[b], (8 * f, 8 * f + 8),
                           Q_LAYOUT if is_q else K_LAYOUT)
                yield
            split.wait_in_dram(sp, (0, 1))
            for g in range(att.preloaded):
                att.preload(sp, g, kscratch[b], qscratch[b], S, first)
            yield
            split.wait_in_dram(sp, (2, 3))
            sp.wait_ge(att.stacks_preloaded, 32 * att.preloaded)

        def prologue_tensor(pe, b, first):
            xnT = norm.xnT[:, :, 1:]
            yield from skip(1 + Norm.OUTER_STEPS)
            yield from norm.tensor(pe)
            pe.wait_ge(norm.xnT_ready, FT)
            for n, wt in enumerate((wkvd, wqd)):
                bank7.take(pe)
                for c in range(FT):
                    mm = pe.matmul(ps[0:64, 7, :], wt[:, c, :], xnT[:, c, :], start=(c == 0), stop=(c == 1))
                mm.then_inc(latent_in_psum, 1)
                bank7.freed_by(latent_ready, n + 1)
                yield
            for i, (f, is_q) in enumerate(ITEMS):
                cols = slice(f * P, (f + 1) * P)
                bank7.take(pe)
                if is_q:
                    pe.wait_ge(latent_ready, 2)
                    mm = pe.matmul(ps[:, 7, :], wq[:, cols], q_latent[:, :], start=True, stop=True)
                else:
                    pe.matmul(ps[:, 7, :], wku[:, cols], kv_latent[:, :], start=True, stop=False)
                    for c in range(FT):
                        mm = pe.matmul(ps[:, 7, :], wkr[:, c, cols], xnT[:, c, :], start=False, stop=(c == 1))
                rotary.hand_over(mm, 2 * i)
                yield
                bank7.take(pe)
                if is_q:
                    mm = pe.matmul(ps[:, 7, :], wq_p[:, cols], q_latent[:, :], start=True, stop=True)
                else:
                    for c in range(FT):
                        mm = pe.matmul(ps[:, 7, :], wkr_p[:, c, cols], xnT[:, c, :], start=(c == 0), stop=(c == 1))
                rotary.hand_over(mm, 2 * i + 1)
                yield
            yield

        def prologue_scalar(act, b, first):
            steps = Steps(act, act_steps)
            if first:
                act.preload_act_table_set(EXP_AND_LN)
            yield
            yield from norm.outer_scalar(act, steps)
            yield from norm.scalar(act, steps)
            for n, dst in enumerate((kv_latent, q_latent)):
                act.wait_ge(latent_in_psum, n + 1)
                act.activation(dst[:, :], ps[0:64, 7, :], ACT.Copy).then_inc(latent_ready, 1)
                yield
            for i in range(4):
                yield
                split.scalar(act, i, S)
                yield
            yield

        def prologue_vector(dve, b, first):
            steps = Steps(dve, side_dve_steps)
            yield
            yield from norm.outer_vector(dve, steps)
            yield from norm.vector(dve, steps)
            yield from skip(2)
            for i, (f, is_q) in enumerate(ITEMS):
                scale = HD ** -0.5 if is_q else 1.0
                rotary.vector_a(dve, steps, i, scale)
                yield
                rotary.vector_b(dve, steps, i, scale)
                dve.sem_inc(split.full_ready, 1)
                split.vector(dve, steps, i, S)
                yield
            yield

        def v_tensor(pe):
            for t in range(T):
                mm = pe.matmul(ps[:, t // 2, (t % 2) * D:(t % 2 + 1) * D], kv_latent[:, t * P:(t + 1) * P],
                               wvu[:, :], start=True, stop=True)
                if t % 2:
                    mm.then_inc(v_in_psum, 1)
                    yield

        def v_scalar(act):
            for n in range(2):
                act.wait_ge(v_in_psum, n + 1)
                act.activation(att.v[:, 2 * n:2 * n + 2, :, 0:HD], v_heads(ps[:, n, :]), ACT.Copy)\
                    .then_inc(att.v_ready, 1)
                yield

        def sync(sp, b, side):
            side = side()
            for g in range(att.preloaded, NG):
                att.load_stacks(sp, g, kscratch[b], qscratch[b], S)
            att.sync(sp, side=side)
            store_x(sp, proj.x_done, 2, stored, residual, x_dst, b)
            exhaust(side)

        def tensor(pe, b, side):
            att.tensor(pe, tri=tri, triT=triT, own=v_tensor(pe), side=side())
            proj.tensor(pe)

        def scalar(act, b, side):
            act.preload_act_table_set(EXP_AND_LN)
            att.scalar(act, own=v_scalar(act), side=side())
            proj.scalar(act)

        def vector(dve, b, side):
            steps = Steps(dve, dve_steps)
            att.vector(dve, steps, side=side())
            dve.wait_ge(att.o_divided, NG)
            dve.sem_inc(proj.o_ready, 1)
            dve.wait_ge(kept, 1)
            proj.vector(dve, steps)

        def gpsimd(pool, b, side):
            keep_residual(nc, pool, residual, x, kept)

        pipelined_loop(nc, st,
                       {"sync": prologue_sync, "tensor": prologue_tensor, "scalar": prologue_scalar,
                        "vector": prologue_vector, "gpsimd": lambda pool, b, first: skip(0)},
                       {"sync": sync, "tensor": tensor, "scalar": scalar, "vector": vector, "gpsimd": gpsimd})



class Hyperbolic:

    ROWS = STACK + NSLOT
    SIDE = (1, 0)

    def __init__(self, st, ps, identf, trif, att, root_c, eps_c):
        self.ps, self.identf, self.trif, self.att, self.root_c, self.eps_c = ps, identf, trif, att, root_c, eps_c
        self.off = [0, P, 3 * P, 6 * P]
        self.place = [(0, 0), (2, 0), (0, P), (1, 0)]
        self.cols = 10 * P
        self.kst = st.sb("hyp_k", [self.ROWS, GH, S], BF16)
        self.qst = st.sb("hyp_q", [self.ROWS, GH, S], BF16)
        self.u = st.sb("hyp_u", [P, 2, self.cols])
        self.root = st.sb("hyp_root", [P, 2, self.cols])
        self.nmax = st.sb("hyp_nmax", [P, 2, T])
        self.bias = st.sb("hyp_bias", [P, 2, T])
        self.pT = st.sb("hyp_pT", [P, 2, T, S])
        self.oT = st.sb("hyp_oT", [P, S])
        self.inv = st.sb("hyp_inv", [P, T, GH])
        self.loaded = st.sem("hyp_loaded")
        self.scored = st.sem("hyp_scored")
        self.u_ready = st.sem("hyp_u_ready")
        self.square_ready = st.sem("hyp_square_ready")
        self.root_ready = st.sem("hyp_root_ready")
        self.sum_ready = st.sem("hyp_sum_ready")
        self.score_ready = st.sem("hyp_score_ready")
        self.bias_ready = st.sem("hyp_bias_ready")
        self.probs_ready = st.sem("hyp_probs_ready")
        self.turned = st.sem("hyp_turned")
        self.pT_ready = st.sem("hyp_pT_ready")
        self.pv_done = st.sem("hyp_pv_done")
        self.oT_copied, self.o_turned = st.sem("hyp_oT_copied"), st.sem("hyp_o_turned")
        self.o_divided = st.sem("hyp_o_divided")

    @staticmethod
    def turned_place(k):
        return ((4, 0), (5, 0), (6, 0), (5, 3 * P))[k]

    def beside(self, side, half):
        for _ in range(self.SIDE[half]):
            next(side, None)

    def tensor(self, pe, side):
        ps = self.ps

        def score(j):
            if j == 0:
                pe.wait_ge(self.loaded, 64)
            for t in range(T):
                if j >= 1:
                    pe.wait_ge(self.u_ready, T * j)
                n = (t + 1) * P
                bank, c0 = self.place[t]
                pe.matmul(ps[:, bank, c0:c0 + n], self.qst[:, j, t * P:n], self.kst[:, j, 0:n], start=True, stop=True)\
                    .then_inc(self.scored, 1)

        def turn(j):
            pe.wait_ge(self.probs_ready, T * (j + 1))
            if j >= 1:
                pe.wait_ge(self.pT_ready, T * j)
            for k in range(T):
                bank, c0 = self.turned_place(k)
                for t in range(k, T):
                    mm = pe.transpose(ps[:, bank, c0 + (t - k) * P:c0 + (t - k + 1) * P],
                                      self.u[:, j % 2, self.off[t] + k * P:self.off[t] + (k + 1) * P],
                                      self.identf[:, :])
                mm.then_inc(self.turned, 1)

        def pv(j):
            for k in range(T):
                pe.wait_ge(self.pT_ready, T * j + k + 1)
                mm = pe.matmul(ps[VW * j:VW * (j + 1), 3, k * P:S], self.att.v[:, k, H - GH + j, :],
                               self.pT[:, j % 2, k, k * P:S], start=(k == 0), stop=(k == T - 1))
            mm.then_inc(self.pv_done, 1)

        score(0)
        for j in range(GH):
            self.beside(side, 0)
            if j + 1 < GH:
                score(j + 1)
            self.beside(side, 1)
            turn(j)
            if j >= 1:
                pv(j - 1)
        pv(GH - 1)
        pe.wait_ge(self.oT_copied, 1)
        for t in range(T):
            mm = pe.transpose(ps[:, 0, t * P:(t + 1) * P], self.oT[:, t * P:(t + 1) * P], self.identf[:, :])
        mm.then_inc(self.o_turned, 1)

    def vector(self, dve, steps, side):
        ps = self.ps

        def excess(j):
            u = self.u[:, j % 2, :]
            for t in range(T):
                dve.wait_ge(self.scored, T * j + max(t + 1, T - 1))
                if j >= 2 and t == 0:
                    dve.wait_ge(self.turned, T * (j - 1))
                dve.tensor_scalar(u[:, self.off[t]:self.off[t] + (t + 1) * P],
                                  ps[:, self.place[t][0], self.place[t][1]:self.place[t][1] + (t + 1) * P],
                                  -1.0, TINY, ALU.add, ALU.max).then_inc(self.u_ready, 1)
            dve.wait_ge(self.u_ready, T * (j + 1))
            dve.scalar_tensor_tensor(out=self.root[:, j % 2, :], in0=u, scalar=2.0, in1=u, op0=ALU.add,
                                     op1=ALU.mult).then_inc(self.square_ready, 1)

        def add_root(j):
            dve.wait_ge(self.root_ready, j + 1)
            u = self.u[:, j % 2, :]
            dve.tensor_tensor(u, u, self.root[:, j % 2, :], ALU.add).then_inc(self.sum_ready, 1)

        def maxima(j):
            dve.wait_ge(self.score_ready, j + 1)
            for t in range(T):
                own = self.u[:, j % 2, self.off[t] + t * P:self.off[t] + (t + 1) * P]
                steps.mark(dve.tensor_tensor(own, own, self.trif[:, :], ALU.add))
            steps.settle()
            for t in range(T):
                steps.mark(dve.tensor_reduce(self.nmax[:, j % 2, t:t + 1],
                                             self.u[:, j % 2, self.off[t]:self.off[t] + (t + 1) * P], AX.X,
                                             ALU.max, negate=True))
            steps.settle()
            dve.tensor_scalar(self.bias[:, j % 2, :], self.nmax[:, j % 2, :], self.root_c[:, j:j + 1], None,
                              ALU.mult).then_inc(self.bias_ready, 1)

        excess(0)
        for j in range(GH):
            self.beside(side, 0)
            add_root(j)
            if j + 1 < GH:
                excess(j + 1)
            self.beside(side, 1)
            maxima(j)
        dve.wait_ge(self.o_turned, 1)
        o = ps[:, 0, :].rearrange("p (t j w) -> p t j w", t=T, j=GH)
        steps.mark(dve.reciprocal(self.inv[:, :, :], o[:, :, :, HD]))
        steps.settle()
        out = self.att.otok[:, :, D - GH * HD:D].rearrange("p t (j d) -> p t j d", j=GH)
        inv = self.inv[:, :, :].rearrange("p t (j o) -> p t j o", o=1).to_broadcast([P, T, GH, HD])
        dve.tensor_tensor(out, o[:, :, :, 0:HD], inv, ALU.mult).then_inc(self.o_divided, 1)

    def scalar(self, act, steps, side):
        def root(j):
            r = self.root[:, j % 2, :]
            act.wait_ge(self.square_ready, j + 1)
            steps.mark(act.activation(r, r, ACT.Ln))
            steps.settle()
            act.activation(r, r, ACT.Exp, scale=0.5).then_inc(self.root_ready, 1)

        def score(j):
            u = self.u[:, j % 2, :]
            act.wait_ge(self.sum_ready, j + 1)
            steps.mark(act.activation(u, u, ACT.Ln, bias=1.0))
            steps.settle()
            steps.mark(act.activation(u, u, ACT.Ln, bias=self.eps_c[:, j:j + 1]))
            steps.settle()
            act.activation(u, u, ACT.Exp, scale=-1.0).then_inc(self.score_ready, 1)

        def probs(j):
            act.wait_ge(self.bias_ready, j + 1)
            for t in range(T):
                u = self.u[:, j % 2, self.off[t]:self.off[t] + (t + 1) * P]
                act.activation(u, u, ACT.Exp, bias=self.bias[:, j % 2, t:t + 1],
                               scale=self.root_c[:, j:j + 1]).then_inc(self.probs_ready, 1)

        def copy(j):
            for k in range(T):
                act.wait_ge(self.turned, T * j + 1 if k == 0 else T * (j + 1))
                if j >= 2 and k == 0:
                    act.wait_ge(self.pv_done, j - 1)
                bank, c0 = self.turned_place(k)
                act.activation(self.pT[:, j % 2, k, k * P:S], self.ps[:, bank, c0:c0 + S - k * P], ACT.Copy)\
                    .then_inc(self.pT_ready, 1)

        root(0)
        for j in range(GH):
            self.beside(side, 0)
            score(j)
            if j + 1 < GH:
                root(j + 1)
            self.beside(side, 1)
            probs(j)
            copy(j)
        act.wait_ge(self.pv_done, GH)
        act.activation(self.oT[:, :], self.ps[:, 3, :], ACT.Copy).then_inc(self.oT_copied, 1)


def mixed_attention(nc, w, x_src, x_dst, kscratch, qscratch, tscratch):
    with ExitStack() as ctx:
        st = Stage(nc, ctx, "s4")
        ps = st.psum()
        loads = []
        identf = constant(st, loads, "identf", w["identf"])
        identb = constant(st, loads, "identb", w["identb"], BF16)
        tri = constant(st, loads, "tri", w["tri"], BF16)
        triT = constant(st, loads, "triT", w["triT"], BF16)
        trif = constant(st, loads, "trif", w["trif"])
        blocks = constant(st, loads, "blocks", w["blocks"])
        cos = constant(st, loads, "cos", w["rot_cos"])
        sin = constant(st, loads, "sin", w["rot_sin"])
        wts = {n: weight(st, loads, n, w[f"mix_{n}"]) for n in ("wq", "wk", "wq_partner", "wk_partner", "wv")}
        wo = weight(st, loads, "wo", w["mix_wo"])
        bo = bias_row(st, loads, "bo", w["L1_attn_proj_b"])
        c_feature = st.sb("c_feature", [P, 1])
        loads.append((c_feature[:, :], w["curvature_feature"]))
        c_head = st.sb("c_head", [P, GH])
        loads.append((c_head[:, :], w["curvature"].rearrange("(o h) -> o h", o=1).to_broadcast([P, GH])))
        neg_c, inv_c = st.sb("neg_c", [P, 1]), st.sb("inv_c", [P, 1])
        root_c, eps_c = st.sb("root_c", [P, GH]), st.sb("eps_c", [P, GH])
        x = st.sb("x", [P, T, D])
        residual = st.sb("residual", [P, T, D])
        bank7 = SharedBank(7)
        norm = Norm(st, ps, x, identf, shared=bank7)
        split = Split(st, S, 4)
        rotary = Rotary(st, ps, split, bank7, cos, sin)
        att = Attention(st, ps, identf, identb, st.sb("otok", [P, T, D]), S, 3, causal=True, bank7=bank7,
                        own=2, side=1 + Norm.STEPS + 4 * 4 + 1 - GH * sum(Hyperbolic.SIDE), preloaded=2)
        hyp = Hyperbolic(st, ps, identf, trif, att, root_c, eps_c)
        proj = OutProjection(st, ps, identf, att.otok, st.sb("oF", [P, FT, S]), wo, residual, bias=bo)
        square = st.sb("square", [P, S])
        sums = st.sb("sums", [P, 2, S])
        t_full = st.sb("t_full", [P, S])
        t_level = st.sb("t_level", [P, 2, 3, S], BF16)
        rotated, squared, summed = st.sem("rotated"), st.sem("squared"), st.sem("summed")
        sums_ready, factor_ready = st.sem("sums_ready"), st.sem("factor_ready")
        t_levels_ready, t_in_dram = st.sem("t_levels_ready"), st.sem("t_in_dram")
        v_in_psum, kept, setup = st.sem("v_in_psum"), st.sem("kept"), st.sem("setup")
        dve_steps, act_steps, stored = st.sem("dve_steps"), st.sem("act_steps"), st.sem("stored")
        side_dve_steps, side_act_steps = st.sem("side_dve_steps"), st.sem("side_act_steps")
        load_constants(nc, st, loads)
        write_ones(nc, att)
        att.own_ready = (att.v_ready, 2)
        with nc.Block() as block:
            @block.vector
            def _(dve):
                dve.tensor_scalar(neg_c[:, :], c_feature[:, :], -1.0, None, ALU.mult)
                dve.reciprocal(inv_c[:, :], c_feature[:, :])
                dve.wait_ge(setup, 2)
                dve.tensor_scalar(eps_c[:, :], root_c[:, :], 1e-6, None, ALU.mult)

            @block.scalar
            def _(act):
                act.activation(root_c[:, :], c_head[:, :], ACT.Ln).then_inc(setup, 1)
                act.wait_ge(setup, 1)
                act.activation(root_c[:, :], root_c[:, :], ACT.Exp, scale=0.5).then_inc(setup, 1)

        hyp_rows = slice(64, P)
        cos_rows = (slice(96, P), slice(0, 64))

        def prologue_sync(sp, b, first):
            if not first:
                sp.wait_ge(kept, 1)
            load_x(sp, norm, x, x_src, b)
            yield from skip(1 + Norm.STEPS)
            for i, (f, is_q) in enumerate(ITEMS):
                yield from skip(3)
                split.sync(sp, i, S, (qscratch if is_q else kscratch)[b], (8 * f, 8 * f + 8),
                           Q_LAYOUT if is_q else K_LAYOUT)
                if f == 1:
                    n = 1 if is_q else 0
                    sp.wait_ge(t_levels_ready, n + 1)
                    for slot, count, lev, step in (K_LAYOUT, Q_LAYOUT)[n]:
                        if step:
                            src = t_level[64:P:HD, n, lev:lev + count, :]
                        else:
                            src = t_level[64:P:HD, n, lev, :].rearrange("p (o w) -> p o w", o=1)\
                                .to_broadcast([GH, count, S])
                        sp.dma_start(tscratch[b, n, :, slot:slot + count, :], src).then_inc(t_in_dram, 16)
                yield
            split.wait_in_dram(sp, (0, 1))
            for g in range(att.preloaded):
                att.preload(sp, g, kscratch[b], qscratch[b], S, first)
            yield
            split.wait_in_dram(sp, (2, 3))
            sp.wait_ge(t_in_dram, 2 * 16 * len(K_LAYOUT))
            sp.wait_ge(att.stacks_preloaded, 32 * att.preloaded)

        def prologue_tensor(pe, b, first):
            xnT = norm.xnT[:, :, 1:]
            yield
            yield from norm.tensor(pe)
            pe.wait_ge(norm.xnT_ready, FT)
            for i, (f, is_q) in enumerate(ITEMS):
                for half, name in enumerate(("wq", "wq_partner") if is_q else ("wk", "wk_partner")):
                    bank7.take(pe)
                    for c in range(FT):
                        mm = pe.matmul(ps[:, 7, :], wts[name][:, c, f * P:(f + 1) * P], xnT[:, c, :],
                                       start=(c == 0), stop=(c == 1))
                    rotary.hand_over(mm, 2 * i + half)
                    yield
                bank7.take(pe)
                pe.wait_ge(squared, i + 1)
                pe.matmul(ps[:, 7, :], blocks[:, :], square[:, :], start=True, stop=True).then_inc(summed, 1)
                bank7.freed_by(sums_ready, i + 1)
                yield
                yield
            yield

        def prologue_scalar(act, b, first):
            steps = Steps(act, side_act_steps)
            if first:
                act.preload_act_table_set(EXP_AND_LN)
            yield
            yield from norm.scalar(act, steps)
            for i, (f, is_q) in enumerate(ITEMS):
                yield
                act.wait_ge(rotated, i + 1)
                if i >= 1:
                    act.wait_ge(summed, i)
                act.activation(square[:, :], split.full[:, i % 2, :], ACT.Square).then_inc(squared, 1)
                yield
                act.wait_ge(sums_ready, i + 1)
                rows = cos_rows[f]
                steps.mark(act.activation(sums[rows, i % 2, :], sums[rows, i % 2, :], ACT.Ln, scale=2.0 ** 24))
                steps.settle()
                last = act.activation(sums[rows, i % 2, :], sums[rows, i % 2, :], ACT.Exp, scale=-0.5)
                if f == 1:
                    steps.mark(last)
                    steps.mark(act.activation(sums[hyp_rows, i % 2, :], sums[hyp_rows, i % 2, :], ACT.Ln,
                                              bias=inv_c[hyp_rows, :]))
                    steps.settle()
                    if is_q:
                        act.wait_ge(t_levels_ready, 1)
                    last = act.activation(t_full[hyp_rows, :], sums[hyp_rows, i % 2, :], ACT.Exp, scale=0.5)
                last.then_inc(factor_ready, 1)
                yield
                split.scalar(act, i, S)
                yield
            yield

        def prologue_vector(dve, b, first):
            steps = Steps(dve, side_dve_steps)
            yield
            yield from norm.vector(dve, steps)
            for i, (f, is_q) in enumerate(ITEMS):
                full = split.full[:, i % 2, :]
                rotary.vector_a(dve, steps, i, 1.0)
                yield
                rotary.vector_b(dve, steps, i, 1.0)
                dve.sem_inc(rotated, 1)
                yield
                dve.wait_ge(summed, i + 1)
                dve.tensor_scalar(sums[:, i % 2, :], ps[:, 7, :], 1e-24, None, ALU.max).then_inc(sums_ready, 1)
                yield
                dve.wait_ge(factor_ready, i + 1)
                rows = cos_rows[f]
                scale = 4.0 if is_q else 1.0
                steps.mark(dve.scalar_tensor_tensor(out=full[rows, :], in0=full[rows, :], scalar=scale * 2.0 ** 12,
                                                    in1=sums[rows, i % 2, :], op0=ALU.mult, op1=ALU.mult))
                if is_q:
                    if f == 0:
                        steps.mark(dve.tensor_scalar(full[0:96, :], full[0:96, :], HD ** -0.5, None, ALU.mult))
                    else:
                        steps.mark(dve.tensor_scalar(full[hyp_rows, :], full[hyp_rows, :], neg_c[hyp_rows, :], None,
                                                     ALU.mult))
                        steps.mark(dve.tensor_scalar(t_full[hyp_rows, :], t_full[hyp_rows, :],
                                                     c_feature[hyp_rows, :], None, ALU.mult))
                steps.settle()
                dve.sem_inc(split.full_ready, 1)
                split.vector(dve, steps, i, S)
                if f == 1:
                    n = 1 if is_q else 0
                    tf, tl = t_full[hyp_rows, :], t_level[hyp_rows, n]
                    for lev in range(3):
                        steps.mark(dve.tensor_copy(tl[:, lev, :], tf))
                        steps.settle()
                        if lev < 2:
                            steps.mark(dve.tensor_tensor(tf, tf, tl[:, lev, :], ALU.subtract))
                            steps.settle()
                    dve.sem_inc(t_levels_ready, 1)
                yield
            yield

        def v_tensor(pe):
            for t in range(T):
                for c in range(FT):
                    mm = pe.matmul(ps[:, t // 2, (t % 2) * D:(t % 2 + 1) * D],
                                   norm.xnT[:, c, 1 + t * P:1 + (t + 1) * P], wts["wv"][:, c, :],
                                   start=(c == 0), stop=(c == 1))
                if t % 2:
                    mm.then_inc(v_in_psum, 1)
                    yield

        def v_scalar(act):
            for n in range(2):
                act.wait_ge(v_in_psum, n + 1)
                act.activation(att.v[:, 2 * n:2 * n + 2, :, 0:HD], v_heads(ps[:, n, :]), ACT.Copy)\
                    .then_inc(att.v_ready, 1)
                yield

        def sync(sp, b, side):
            side = side()
            att.load_stacks(sp, 2, kscratch[b], qscratch[b], S)
            heads = slice(H - GH, H)
            for n, (dst, src) in enumerate(((hyp.kst, kscratch[b]), (hyp.qst, qscratch[b]))):
                sp.dma_start(dst[0:STACK, :, :], src[heads, :, :, 0:S].rearrange("h d s w -> (d s) h w"))\
                    .then_inc(hyp.loaded, 16)
                sp.dma_start(dst[STACK:STACK + NSLOT, :, :], tscratch[b, n].rearrange("h s w -> s h w"))\
                    .then_inc(hyp.loaded, 16)
            att.sync(sp, side=side)
            exhaust(side)
            store_x(sp, proj.x_done, 2, stored, residual, x_dst, b)

        def tensor(pe, b, side):
            side = side()
            att.tensor(pe, tri=tri, triT=triT, own=v_tensor(pe), side=side)
            pe.wait_ge(att.exped, 2 * T * 3)
            pe.wait_ge(att.max_taken, 3 * len(att.units))
            pe.wait_ge(att.oT_copied, 3)
            hyp.tensor(pe, side)
            proj.tensor(pe)

        def scalar(act, b, side):
            act.preload_act_table_set(EXP_AND_LN)
            side = side()
            att.scalar(act, own=v_scalar(act), side=side)
            hyp.scalar(act, Steps(act, act_steps), side)
            proj.scalar(act)

        def vector(dve, b, side):
            steps = Steps(dve, dve_steps)
            side = side()
            att.vector(dve, steps, side=side)
            hyp.vector(dve, steps, side)
            dve.wait_ge(att.o_divided, 3)
            dve.wait_ge(hyp.o_divided, 1)
            dve.sem_inc(proj.o_ready, 1)
            dve.wait_ge(kept, 1)
            proj.vector(dve, steps)

        def gpsimd(pool, b, side):
            keep_residual(nc, pool, residual, x, kept)

        pipelined_loop(nc, st,
                       {"sync": prologue_sync, "tensor": prologue_tensor, "scalar": prologue_scalar,
                        "vector": prologue_vector, "gpsimd": lambda pool, b, first: skip(0)},
                       {"sync": sync, "tensor": tensor, "scalar": scalar, "vector": vector, "gpsimd": gpsimd})



NE = 7


def experts(nc, w, y_src, x_src, x_dst):
    with ExitStack() as ctx:
        st = Stage(nc, ctx, "s7")
        ps = st.psum()
        loads = []
        identf = constant(st, loads, "identf", w["identf"])
        number = st.sb("number", [P, NE + 1])
        loads.append((number[:, :], w["numbers"].rearrange("(o n) -> o n", o=1).to_broadcast([P, NE + 1])))
        w_ln = column(st, loads, "w_ln", w["L1_ffn_w_ln2"])
        wr = weight(st, loads, "wr", w["L1_ffn_W_router"])
        br = st.sb("br", [P, NE])
        loads.append((br[:, :], w["L1_ffn_routing_bias"].rearrange("(o n) -> o n", o=1).to_broadcast([P, NE])))
        wg, wu, wd = (st.sb(n, [P, NE + 1, FT, D]) for n in ("wg", "wu", "wd"))
        for tile, name in ((wg, "Wg"), (wu, "Wu"), (wd, "Wd")):
            loads.append((tile[:, 0, :, :], w[f"L1_ffn_{name}_s"].rearrange("(f p) n -> p f n", p=P)))
            for e in range(NE):
                loads.append((tile[:, 1 + e, :, :], w[f"L1_ffn_{name}_r"][e].rearrange("(f p) n -> p f n", p=P)))
        y, total = st.sb("y", [P, T, D]), st.sb("total", [P, T, D])
        residual = st.sb("residual", [P, T, D])
        bank7 = SharedBank(7)
        norm = Norm(st, ps, y, identf, rms=True, weight=w_ln, shared=bank7)
        xnT = st.sb("xnT_now", [P, FT, S])
        logit, odds = st.sb("logit", [P, T, NE]), st.sb("odds", [P, T, NE])
        prob = st.sb("prob", [P, T, NE + 1])
        top, where = st.sb("top", [P, T, 8]), st.sb("where", [P, T, 8], U32)
        wheref = st.sb("wheref", [P, T, 2])
        picked, both = st.sb("picked", [P, T, NE + 1]), st.sb("both", [P, T])
        share = st.sb("share", [P, T, NE + 1])
        share_next = st.sb("share_next", [P, T, NE + 1])
        gate, gated = st.sb("gate", [P, 2, S]), st.sb("gated", [P, 2, S])
        mid = st.sb("mid", [P, 2, FT, S])
        xnT_kept, total_kept, share_kept = st.sem("xnT_kept"), st.sem("total_kept"), st.sem("share_kept")
        logit_in_psum, logit_ready, odds_ready = st.sem("logit_in_psum"), st.sem("logit_ready"), st.sem("odds_ready")
        up_in_psum, gate_ready, gated_ready = st.sem("up_in_psum"), st.sem("gate_ready"), st.sem("gated_ready")
        mid_ready, down_in_psum, down_added = st.sem("mid_ready"), st.sem("down_in_psum"), st.sem("down_added")
        residual_loaded = st.sem("residual_loaded")
        side_dve_steps = st.sem("side_dve_steps")
        dve_steps, act_steps, stored = st.sem("dve_steps"), st.sem("act_steps"), st.sem("stored")
        load_constants(nc, st, loads)
        with nc.Block() as block:
            @block.vector
            def _(dve):
                dve.memset(prob[:, :, NE:NE + 1], -1.0)
        order = []
        for e in range(NE + 1):
            order += [("up", e, 0), ("up", e, 1)] + ([("down", e - 1)] if e else [])
        order.append(("down", NE))

        def down_bank(e, t):
            return 4 + (T * e + t) % 3

        SIDE = 1 + Norm.STEPS + 3
        side_at = {3 * n: n for n in range(SIDE - 1)}

        def prologue_sync(sp, b, first):
            if not first:
                sp.wait_ge(xnT_kept, 1)
                sp.wait_ge(total_kept, 1)
            load_x(sp, norm, y, y_src, b)
            sp.dma_start(residual[:, :, :], x_src[b].rearrange("(t p) d -> p t d", p=P))\
                .then_inc(residual_loaded, 16)
            yield from skip(SIDE)

        def prologue_tensor(pe, b, first):
            if not first:
                pe.wait_ge(xnT_kept, 1)
            yield
            yield from norm.tensor(pe)
            pe.wait_ge(norm.xnT_ready, FT)
            bank7.take(pe)
            for t in range(T):
                for c in range(FT):
                    mm = pe.matmul(ps[:, 7, t * NE:(t + 1) * NE], norm.xnT[:, c, 1 + t * P:1 + (t + 1) * P],
                                   wr[:, c, :], start=(c == 0), stop=(c == 1))
            mm.then_inc(logit_in_psum, 1)
            bank7.freed_by(logit_ready, 1)
            yield from skip(3)

        def prologue_scalar(act, b, first):
            steps = Steps(act, act_steps)
            yield
            yield from norm.scalar(act, steps)
            act.wait_ge(logit_ready, 1)
            act.activation(odds[:, :, :], logit[:, :, :], ACT.Exp, scale=-1.0).then_inc(odds_ready, 1)
            yield from skip(3)

        def prologue_gpsimd(pool, b, first):
            yield from skip(SIDE)

        def prologue_vector(dve, b, first):
            steps = Steps(dve, side_dve_steps)

            def do(instruction):
                steps.mark(instruction)
                steps.settle()

            yield
            yield from norm.vector(dve, steps)
            dve.wait_ge(logit_in_psum, 1)
            dve.tensor_tensor(logit[:, :, :], ps[:, 7, 0:T * NE].rearrange("p (t n) -> p t n", t=T),
                              br[:, :].rearrange("p (o n) -> p o n", o=1).to_broadcast([P, T, NE]), ALU.add)\
                .then_inc(logit_ready, 1)
            dve.wait_ge(residual_loaded, 16)
            do(dve.tensor_tensor(residual[:, :, :], residual[:, :, :], y[:, :, :], ALU.add))
            yield
            dve.wait_ge(odds_ready, 1)
            do(dve.tensor_scalar(odds[:, :, :], odds[:, :, :], 1.0, None, ALU.add))
            do(dve.reciprocal(prob[:, :, 0:NE], odds[:, :, :]))
            for t in range(T):
                steps.mark(dve.max(top[:, t, :], prob[:, t, :]))
            steps.settle()
            for t in range(T):
                steps.mark(dve.max_index(where[:, t, :], top[:, t, :], prob[:, t, :]))
            do(dve.tensor_tensor(both[:, :], top[:, :, 0], top[:, :, 1], ALU.add))
            do(dve.reciprocal(both[:, :], both[:, :]))
            do(dve.tensor_copy(wheref[:, :, :], where[:, :, 0:2]))
            yield
            for t in range(T):
                steps.mark(dve.tensor_scalar(picked[:, t, :], number[:, :], wheref[:, t, 0:1], None, ALU.is_equal))
            steps.settle()
            for t in range(T):
                steps.mark(dve.scalar_tensor_tensor(out=picked[:, t, :], in0=number[:, :],
                                                    scalar=wheref[:, t, 1:2], in1=picked[:, t, :],
                                                    op0=ALU.is_equal, op1=ALU.add))
            steps.settle()
            for t in range(T):
                steps.mark(dve.scalar_tensor_tensor(out=share_next[:, t, :], in0=prob[:, t, :],
                                                    scalar=both[:, t:t + 1], in1=picked[:, t, :],
                                                    op0=ALU.mult, op1=ALU.mult))
            steps.settle()
            do(dve.tensor_scalar(share_next[:, :, :], share_next[:, :, :], 0.5, None, ALU.mult))
            yield

        def sync(sp, b, side):
            side = side()
            next(side, None)
            store_x(sp, down_added, T * (NE + 1), stored, total, x_dst, b)
            exhaust(side)

        def gpsimd(pool, b, side):
            pool.tensor_copy(share[:, :, :], share_next[:, :, :]).then_inc(share_kept, 1)
            pool.tensor_copy(total[:, :, :], residual[:, :, :]).then_inc(total_kept, 1)

        def tensor(pe, b, side):
            side = side()
            bank7.freed = None
            pe.wait_ge(xnT_kept, 1)
            downs = 0
            for place, item in enumerate(order):
                if place in side_at:
                    next(side, None)
                e = item[1]
                if item[0] == "up":
                    f = item[2]
                    i = 2 * e + f
                    if i >= 2:
                        pe.wait_ge(mid_ready, i - 1)
                    for bank, wt in ((2 * (i % 2), wg), (2 * (i % 2) + 1, wu)):
                        for c in range(FT):
                            mm = pe.matmul(ps[:, bank, :], wt[:, e, c, f * P:(f + 1) * P], xnT[:, c, :],
                                           start=(c == 0), stop=(c == 1))
                    mm.then_inc(up_in_psum, 1)
                    continue
                pe.wait_ge(mid_ready, 2 * e + 2)
                for t in range(T):
                    if downs >= 3:
                        pe.wait_ge(down_added, downs - 2)
                    for c in range(FT):
                        mm = pe.matmul(ps[:, down_bank(e, t), 0:D], mid[:, e % 2, c, t * P:(t + 1) * P],
                                       wd[:, e, c, :], start=(c == 0), stop=(c == 1))
                    mm.then_inc(down_in_psum, 1)
                    downs += 1
            exhaust(side)

        def scalar(act, b, side):
            side = side()
            act.activation(xnT[:, :, :], norm.xnT[:, :, 1:], ACT.Copy).then_inc(xnT_kept, 1)
            for place, item in enumerate(order):
                if place in side_at:
                    next(side, None)
                if item[0] == "up":
                    i = 2 * item[1] + item[2]
                    act.wait_ge(up_in_psum, i + 1)
                    if i >= 2:
                        act.wait_ge(gated_ready, i - 1)
                    act.activation(gate[:, i % 2, :], ps[:, 2 * (i % 2), :], ACT.Tanh, scale=0.5)\
                        .then_inc(gate_ready, 1)
            exhaust(side)

        def vector(dve, b, side):
            side = side()
            dve.wait_ge(share_kept, 1)
            dve.wait_ge(total_kept, 1)
            for place, item in enumerate(order):
                if place in side_at:
                    next(side, None)
                e = item[1]
                if item[0] == "up":
                    i = 2 * e + item[2]
                    g, u = 2 * (i % 2), 2 * (i % 2) + 1
                    dve.wait_ge(gate_ready, i + 1)
                    if i >= 2:
                        dve.wait_ge(mid_ready, i - 1)
                    dve.scalar_tensor_tensor(out=gated[:, i % 2, :], in0=gate[:, i % 2, :], scalar=1.0,
                                             in1=ps[:, g, :], op0=ALU.add, op1=ALU.mult).then_inc(gated_ready, 1)
                    dve.wait_ge(gated_ready, i + 1)
                    if e >= 2:
                        dve.wait_ge(down_in_psum, T * (e - 1))
                    dve.tensor_tensor(mid[:, e % 2, item[2], :], gated[:, i % 2, :], ps[:, u, :], ALU.mult)\
                        .then_inc(mid_ready, 1)
                    continue
                for t in range(T):
                    dve.wait_ge(down_in_psum, T * e + t + 1)
                    if e >= 1:
                        dve.wait_ge(down_added, T * (e - 1) + t + 1)
                    dve.scalar_tensor_tensor(out=total[:, t, :], in0=ps[:, down_bank(e, t), 0:D],
                                             scalar=share[:, t, e - 1:e] if e else 0.5, in1=total[:, t, :],
                                             op0=ALU.mult, op1=ALU.add).then_inc(down_added, 1)

            exhaust(side)

        pipelined_loop(nc, st,
                       {"sync": prologue_sync, "tensor": prologue_tensor, "scalar": prologue_scalar,
                        "vector": prologue_vector, "gpsimd": prologue_gpsimd},
                       {"sync": sync, "tensor": tensor, "scalar": scalar, "vector": vector, "gpsimd": gpsimd})



def decoder(nc, w, out):
    def scratch(name, shape, dt):
        return nc.dram_tensor(name, shape, dt, kind="Internal").ap()

    x = [w["x"]] + [scratch(f"x_after_{i}", (NB, S, D), F32) for i in range(1, 7)] + [out]
    kscratch = scratch("k_levels", (NB, H, HD, NSLOT, CTX), BF16)
    qscratch = scratch("q_levels", (NB, H, HD, NSLOT, S), BF16)
    tscratch = scratch("t_levels", (NB, 2, GH, NSLOT, S), BF16)
    latent_attention(nc, w, x[0], x[1], kscratch, qscratch)
    cross_attention(nc, w, x[1], x[2], kscratch, qscratch)
    channel_mix(nc, w, x[2], x[3])
    mixed_attention(nc, w, x[3], x[4], kscratch, qscratch, tscratch)
    linear_attention(nc, w, x[4], x[5])
    rotary_latent_attention(nc, w, x[5], x[6], kscratch, qscratch)
    experts(nc, w, x[6], x[5], x[7])


def kernel(**inputs):
    import ml_dtypes as _ml
    import numpy as _np
    import concourse.bacc as _bacc
    from concourse import mybir as _mybir
    from concourse.bass_utils import run_bass_kernel_spmd as _run

    f32 = _np.float32
    src = {name: _np.asarray(value) for name, value in inputs.items()}

    def columns(v):
        return v.reshape(FT, P).T

    a = {"x": src["x"], "mask": src["mask_BxSxS2_ff0"], "ctxT": src["ctx_1024"].transpose(0, 2, 1)}

    i = _np.arange(P)
    causal = _np.where(i[None, :] > i[:, None], NEG, 0.0)
    a["identf"], a["identb"] = _np.eye(P, dtype=f32), _np.eye(P).astype(_ml.bfloat16)
    a["tri"], a["triT"], a["trif"] = causal.astype(_ml.bfloat16), causal.T.astype(_ml.bfloat16), causal.astype(f32)
    a["blocks"] = _np.kron(_np.eye(P // HD), _np.ones((HD, HD))).astype(f32)
    a["numbers"] = _np.arange(NE + 1, dtype=f32)

    def rotary_tables(width):
        steps = f32(1.0) / _np.power(f32(10000.0), _np.arange(0, width, 2, dtype=f32) / f32(width))
        angles = _np.outer(_np.arange(S, dtype=f32), steps.astype(f32)).astype(f32)
        return _np.cos(angles).T, _np.sin(angles).T

    c, s = rotary_tables(HD)
    a["rot_cos"] = _np.tile(_np.concatenate([c, c]), (P // HD, 1))
    a["rot_sin"] = _np.tile(_np.concatenate([s, -s]), (P // HD, 1))
    c, s = rotary_tables(HD // 2)
    a["mla_cos"] = _np.tile(_np.concatenate([_np.ones((HD // 2, S), f32), c, c]), (P // HD, 1))
    a["mla_sin"] = _np.tile(_np.concatenate([_np.zeros((HD // 2, S), f32), -s, s]), (P // HD, 1))

    for name in ("L0_attn_W_DKV", "L0_attn_W_UK", "L0_attn_W_UV", "L0_attn_W_UQ", "L0_attn_W_O",
                 "L0_xattn_bv", "L0_xattn_bo", "L1_xattn_bk", "L1_xattn_bv", "L1_xattn_bo", "L1_attn_proj_b",
                 "L1_ffn_W_kvd", "L1_ffn_W_qd", "L1_ffn_W_vu", "L1_ffn_W_o", "L1_ffn_Wg_s", "L1_ffn_Wu_s",
                 "L1_ffn_Wd_s", "L1_ffn_Wg_r", "L1_ffn_Wu_r", "L1_ffn_Wd_r", "L1_ffn_W_router",
                 "L1_ffn_routing_bias"):
        a[name] = src[name]
    for name in ("L0_xattn_Wq", "L0_xattn_Wk", "L0_xattn_Wv", "L0_xattn_Wo", "L1_xattn_Wq", "L1_xattn_Wk",
                 "L1_xattn_Wv", "L1_xattn_Wo", "L0_ffn_W_r", "L0_ffn_W_k", "L0_ffn_W_v"):
        a[name] = src[name].T
    for name in ("L0_xattn_bq", "L0_xattn_bk", "L1_xattn_bq", "L0_ffn_mu_r", "L0_ffn_mu_k", "L1_ffn_w_ln1",
                 "L1_ffn_w_ln2"):
        a[name] = columns(src[name])

    order = [*range(6), *range(10, 16), *range(6, 10)]
    own = _np.concatenate([HD * h + _np.arange(HD) for h in order])
    partner = _np.concatenate([HD * h + (_np.arange(HD) + HD // 2) % HD for h in order])
    q, k, v = _np.split(src["L1_attn_qkv_w"], 3)
    a["mix_wq"], a["mix_wk"], a["mix_wv"] = q[own].T, k[own].T, v[own].T
    a["mix_wq_partner"], a["mix_wk_partner"] = q[partner].T, k[partner].T
    a["mix_wo"] = src["L1_attn_proj_w"].T[own]
    a["curvature"] = src["L1_attn_curvature"].reshape(GH)
    a["curvature_feature"] = _np.tile(_np.repeat(a["curvature"], HD), P // (GH * HD)).reshape(P, 1)

    def head_columns(plain, rotary, swapped=False):
        n, half = (plain if rotary is None else rotary).shape[0], HD // 2
        cols = _np.zeros((n, H, HD), f32)
        if plain is not None:
            cols[:, :, 0:half] = plain.reshape(n, H, half)
        if rotary is not None:
            order = (_np.arange(half) + half // 2) % half if swapped else _np.arange(half)
            cols[:, :, half:HD] = rotary.reshape(n, H, half)[:, :, order]
        return cols.reshape(n, D)

    a["mla_wku"] = head_columns(src["L1_ffn_W_ku"], None)
    a["mla_wkr"] = head_columns(None, src["L1_ffn_W_ropek"])
    a["mla_wkr_partner"] = head_columns(None, src["L1_ffn_W_ropek"], swapped=True)
    a["mla_wq"] = head_columns(src["L1_ffn_W_qu"], src["L1_ffn_W_ropeq"])
    a["mla_wq_partner"] = head_columns(None, src["L1_ffn_W_ropeq"], swapped=True)

    nc = _bacc.Bacc("TRN2", target_bir_lowering=False, num_devices=1)
    arrays, w = {}, {}
    for name, value in a.items():
        arrays[f"in_{name}"] = value = _np.ascontiguousarray(value)
        w[name] = nc.dram_tensor(f"in_{name}", value.shape, _mybir.dt.from_np(value.dtype),
                                 kind="ExternalInput").ap()
    out = nc.dram_tensor("out_x", (NB, S, D), F32, kind="ExternalOutput").ap()
    decoder(nc, w, out)
    r = _run(nc, [arrays], core_ids=[0])
    return r.results[0]["out_x"]
```

```python
from contextlib import ExitStack

import concourse.bass as bass
from concourse import mybir

F32 = mybir.dt.float32
BF16 = mybir.dt.bfloat16
U32 = mybir.dt.uint32
ALU = mybir.AluOpType
ACT = mybir.ActivationFunctionType
AX = mybir.AxisListType

P = 128
NB, S, D = 8, 512, 256
H, HD = 16, 16
CTX = 1601
T = S // P
FT = D // P
GH = 4
NG = H // GH
VW = 32
NEG = -1.0e30
PRODUCTS = ((0, 0), (1, 0), (2, 0), (0, 1), (1, 1), (0, 2))
NSLOT = len(PRODUCTS)
K_LAYOUT = ((0, 3, 0, 1), (3, 2, 0, 1), (5, 1, 0, 1))
Q_LAYOUT = ((0, 3, 0, 0), (3, 2, 1, 0), (5, 1, 2, 0))
ITEM_DONE = 16 * len(K_LAYOUT)
STACK = NSLOT * HD
ITEMS = ((0, False), (0, True), (1, False), (1, True))
SHIFT = 3
EPS = 1e-5
TINY = 2.0 ** -23
EXP_AND_LN = "natural_log_exp_and_others"


def tiles_of(n):
    return [(i, min(P, n - i)) for i in range(0, n, P)]


class Steps:

    def __init__(self, eng, sem):
        self.eng, self.sem, self.n = eng, sem, 0

    def mark(self, instruction):
        self.n += 1
        return instruction.then_inc(self.sem, 1)

    def settle(self):
        if self.n:
            self.eng.wait_ge(self.sem, self.n)


class Stage:

    def __init__(self, nc, ctx, name):
        self.nc, self.ctx, self.name, self.nums = nc, ctx, name, []

    def sb(self, name, shape, dt=F32):
        return self.ctx.enter_context(self.nc.sbuf_tensor(f"{self.name}_{name}", shape, dt))

    def psum(self):
        return self.ctx.enter_context(self.nc.psum_tensor(f"{self.name}_ps", [P, 8, 512], F32))

    def sem(self, name):
        s = self.ctx.enter_context(self.nc.semaphore(f"{self.name}_{name}"))
        self.nums.append(s.num)
        return s

    def runs(self):
        nums, out = sorted(self.nums), []
        for n in nums:
            if out and n == out[-1].stop:
                out[-1] = range(out[-1].start, n + 1)
            else:
                out.append(range(n, n + 1))
        return out


def pipelined_loop(nc, st, prologue, body, after_first=None):
    def everything(block, run):
        @block.sync
        def _(sp):
            run("sync", sp)

        @block.tensor
        def _(pe):
            run("tensor", pe)

        @block.vector
        def _(dve):
            run("vector", dve)

        @block.scalar
        def _(act):
            run("scalar", act)

        @block.gpsimd
        def _(pool):
            run("gpsimd", pool)

    def barrier():
        for run in st.runs():
            nc.all_engine_barrier(sems_to_clear=run)

    def first(name, e):
        exhaust(prologue[name](e, 0, True))
        if after_first:
            after_first[name](e)

    with nc.Block() as block:
        everything(block, first)
    barrier()
    with nc.Fori(0, NB - 1) as b:
        with nc.Block() as block:
            everything(block, lambda name, e: body[name](e, b, lambda *a: prologue[name](e, b + 1, False, *a)))
        barrier()
    with nc.Block() as block:
        everything(block, lambda name, e: body[name](e, NB - 1, NO_SIDE))
    barrier()


def NO_SIDE(*_):
    return iter(())


def kind(side):
    return "last" if side is NO_SIDE else "middle"


def exhaust(steps):
    for _ in steps:
        pass


def skip(n):
    for _ in range(n):
        yield


class SharedBank:

    def __init__(self, index):
        self.index, self.freed = index, None

    def take(self, pe):
        if self.freed:
            pe.wait_ge(*self.freed)

    def freed_by(self, sem, value):
        self.freed = (sem, value)



class Norm:

    def __init__(self, st, ps, x, identf, rms=False, weight=None, banks=(0, 1), shared=None):
        if shared:
            banks = (shared.index, shared.index)
        self.shared = shared
        self.ps, self.x, self.identf, self.rms, self.weight, self.banks = ps, x, identf, rms, weight, banks
        self.xn = st.sb("xn", [P, T, D])
        self.xnT = st.sb("xnT", [P, FT, S + 1])
        self.stats = st.sb("stats", [P, T, 6])
        self.mv = st.sb("mv", [P, T, 2])
        self.var = st.sb("var", [P, T])
        self.lnv = st.sb("lnv", [P, T])
        self.rstd = st.sb("rstd", [P, T])
        self.x_loaded = st.sem("x_loaded")
        self.outer_var_ready, self.outer_rstd_ready = st.sem("outer_var_ready"), st.sem("outer_rstd_ready")
        self.var_ready = st.sem("var_ready")
        self.rstd_ready = st.sem("rstd_ready")
        self.xn_ready = st.sem("xn_ready")
        self.xnT_in_psum = st.sem("xnT_in_psum")
        self.xnT_ready = st.sem("xnT_ready")

    STEPS, OUTER_STEPS = 5, 3

    def outer_vector(self, dve, steps):
        dve.wait_ge(self.x_loaded, 16)
        for t in range(T):
            steps.mark(dve.bn_stats(self.stats[:, t, :], self.x[:, t, :]))
        steps.settle()
        for t in range(T):
            steps.mark(dve.bn_aggr(self.mv[:, t, :], self.stats[:, t, :]))
        steps.settle()
        dve.tensor_scalar(self.var[:, :], self.mv[:, :, 1], EPS, None, ALU.add).then_inc(self.outer_var_ready, 1)
        yield
        yield
        dve.wait_ge(self.outer_rstd_ready, 1)
        for t in range(T):
            steps.mark(dve.tensor_scalar(self.x[:, t, :], self.x[:, t, :], self.mv[:, t, 0:1],
                                         self.rstd[:, t:t + 1], ALU.subtract, ALU.mult))
        steps.settle()
        yield

    def outer_scalar(self, act, steps):
        yield
        act.wait_ge(self.outer_var_ready, 1)
        steps.mark(act.activation(self.lnv[:, :], self.var[:, :], ACT.Ln))
        steps.settle()
        act.activation(self.rstd[:, :], self.lnv[:, :], ACT.Exp, scale=-0.5).then_inc(self.outer_rstd_ready, 1)
        yield
        yield

    def vector(self, dve, steps):
        dve.wait_ge(self.x_loaded, 16)
        for t in range(T):
            steps.mark(dve.bn_stats(self.stats[:, t, :], self.x[:, t, :]))
        steps.settle()
        for t in range(T):
            steps.mark(dve.bn_aggr(self.mv[:, t, :], self.stats[:, t, :]))
        steps.settle()
        if self.rms:
            steps.mark(dve.tensor_tensor(self.lnv[:, :], self.mv[:, :, 0], self.mv[:, :, 0], ALU.mult))
            steps.settle()
            steps.mark(dve.scalar_tensor_tensor(out=self.var[:, :], in0=self.mv[:, :, 1], scalar=1e-18,
                                                in1=self.lnv[:, :], op0=ALU.add, op1=ALU.add))
            steps.settle()
            dve.sem_inc(self.var_ready, 1)
            yield
            yield
            dve.wait_ge(self.rstd_ready, 1)
            steps.mark(dve.tensor_scalar(self.var[:, :], self.rstd[:, :], EPS, None, ALU.add))
            steps.settle()
            steps.mark(dve.reciprocal(self.rstd[:, :], self.var[:, :]))
            steps.settle()
            for t in range(T):
                dve.tensor_scalar(self.xn[:, t, :], self.x[:, t, :], self.rstd[:, t:t + 1], None,
                                  ALU.mult).then_inc(self.xn_ready, 1)
            yield from skip(3)
            return
        dve.tensor_scalar(self.var[:, :], self.mv[:, :, 1], EPS, None, ALU.add).then_inc(self.var_ready, 1)
        yield
        yield
        dve.wait_ge(self.rstd_ready, 1)
        for t in range(T):
            dve.tensor_scalar(self.xn[:, t, :], self.x[:, t, :], self.mv[:, t, 0:1], self.rstd[:, t:t + 1],
                              ALU.subtract, ALU.mult).then_inc(self.xn_ready, 1)
        yield from skip(3)

    def scalar(self, act, steps):
        yield
        act.wait_ge(self.var_ready, 1)
        steps.mark(act.activation(self.lnv[:, :], self.var[:, :], ACT.Ln))
        steps.settle()
        act.activation(self.rstd[:, :], self.lnv[:, :], ACT.Exp,
                       scale=0.5 if self.rms else -0.5).then_inc(self.rstd_ready, 1)
        yield
        yield
        for f in range(FT):
            act.wait_ge(self.xnT_in_psum, f + 1)
            scale = 1.0 if self.weight is None else self.weight[:, f:f + 1]
            act.activation(self.xnT[:, f, 1:S + 1], self.ps[:, self.banks[f], :], ACT.Identity,
                           scale=scale).then_inc(self.xnT_ready, 1)
            yield

    def tensor(self, pe):
        yield from skip(3)
        for f in range(FT):
            if self.shared:
                self.shared.take(pe)
                self.shared.freed_by(self.xnT_ready, f + 1)
            for t in range(T):
                if f == 0:
                    pe.wait_ge(self.xn_ready, t + 1)
                last = pe.transpose(self.ps[:, self.banks[f], t * P:(t + 1) * P],
                                    self.xn[:, t, f * P:(f + 1) * P], self.identf[:, :])
            last.then_inc(self.xnT_in_psum, 1)
            yield



class Split:

    def __init__(self, st, k_width, items):
        self.full = [st.sb(f"full{n}", [P, w]) for n, w in enumerate((k_width, S))]
        self.level = [st.sb(f"level{n}", [P, 3, w], BF16) for n, w in enumerate((k_width, S))]
        self.full_ready = st.sem("full_ready")
        self.level0_ready = st.sem("level0_ready")
        self.levels_ready = st.sem("levels_ready")
        self.in_dram = [st.sem(f"levels_in_dram{i}") for i in range(items)]

    def wait_in_dram(self, sp, items):
        for i in items:
            sp.wait_ge(self.in_dram[i], ITEM_DONE)

    def vector(self, dve, steps, i, w):
        full, level = self.full[i % 2][:, 0:w], self.level[i % 2]
        dve.wait_ge(self.level0_ready, i + 1)
        steps.mark(dve.tensor_tensor(full, full, level[:, 0, 0:w], ALU.subtract))
        steps.settle()
        if i >= 2:
            dve.wait_ge(self.in_dram[i - 2], ITEM_DONE)
        steps.mark(dve.tensor_copy(level[:, 1, 0:w], full))
        steps.settle()
        steps.mark(dve.tensor_tensor(level[:, 2, 0:w], full, level[:, 1, 0:w], ALU.subtract))
        steps.settle()
        dve.sem_inc(self.levels_ready, 1)

    def scalar(self, act, i, w):
        act.wait_ge(self.full_ready, i + 1)
        if i >= 2:
            act.wait_ge(self.in_dram[i - 2], ITEM_DONE)
        act.activation(self.level[i % 2][:, 0, 0:w], self.full[i % 2][:, 0:w], ACT.Copy)\
            .then_inc(self.level0_ready, 1)

    def sync(self, sp, i, w, scratch, heads, slots):
        sp.wait_ge(self.levels_ready, i + 1)
        for first, n, lev, step in slots:
            if step:
                src = self.level[i % 2][:, lev:lev + n, 0:w]
            else:
                src = self.level[i % 2][:, lev, 0:w].rearrange("p (o w) -> p o w", o=1)\
                    .to_broadcast([P, n, w])
            sp.dma_start(scratch[heads[0]:heads[1], :, first:first + n, 0:w].rearrange("h d s w -> (h d) s w"), src)\
                .then_inc(self.in_dram[i], 16)



class Attention:

    def __init__(self, st, ps, identf, identb, otok, keys, groups, causal, masked=False, bank7=None, own=0, side=0, side_until=0.8,
                 lead=5, ours_until=None, nexts_from=None, late=0, preloaded=0):
        self.own, self.side, self.late, self.preloaded = own, side, late, preloaded
        self.own_ready, self.side_until = None, side_until
        self.lead = lead
        self.ours_until, self.nexts_from = ours_until or groups - 1.3, nexts_from or groups - 1.3
        self.next_mask = None
        self.bank7 = bank7 or SharedBank(7)
        self.ps, self.identf, self.identb = ps, identf, identb
        self.keys, self.groups, self.causal, self.masked = tiles_of(keys), groups, causal, masked
        self.nslots = groups
        self.npt = 4
        self.kst = st.sb("kstack", [P, self.nslots, GH, keys], BF16)
        self.qst = st.sb("qstack", [P, self.nslots, GH, S], BF16)
        self.v = st.sb("v", [P, len(self.keys), H, VW])
        self.probs = st.sb("probs", [P, self.npt, 2, S])
        self.nchunk = 1 if causal else 4
        self.chunk = -(-keys // self.nchunk)
        self.cmax = st.sb("cmax", [P, 2, T * GH, 4])
        self.nmax = st.sb("nmax", [P, 2, T, GH])
        self.rest = st.sb("rest", [P, 2, T, GH])
        self.shift = st.sb("shift", [P, 2, T, SHIFT * GH], BF16)
        self.shiftT = st.sb("shiftT", [SHIFT * GH, 2, S], BF16)
        self.oT = st.sb("oT", [P, S])
        self.inv = st.sb("inv", [P, T, GH])
        self.otok = otok
        if masked:
            self.junk = st.sb("junk", [P, 2, self.chunk])
        self.stacks_loaded = [st.sem(f"stacks_loaded{g}") for g in range(groups)]
        self.stack0_preloaded = st.sem("stack0_preloaded")
        self.stacks_preloaded = st.sem("stacks_preloaded")
        self.shift_loaded = [st.sem(f"shift_loaded{g}") for g in range(groups + 1)]
        self.v_ready = st.sem("v_ready")
        self.max_scored = st.sem("max_scored")
        self.max_taken = st.sem("max_taken")
        self.shift_split = st.sem("shift_split")
        self.shift_turned = st.sem("shift_turned")
        self.shift_copied = st.sem("shift_copied")
        self.scored = st.sem("scored")
        self.exped = st.sem("exped")
        self.pv_done = st.sem("pv_done")
        self.oT_copied = st.sem("oT_copied")
        self.o_turned = st.sem("o_turned")
        self.o_divided = st.sem("o_divided")
        if causal:
            self.units = [(j, nj, t, 0, (t + 1) * P) for t in range(T)
                          for nj in (min(GH, 512 // ((t + 1) * P)),) for j in range(0, GH, nj)]
        else:
            self.units = [(j, 1, t, c, min(self.chunk, keys - c * self.chunk))
                          for t in range(T) for j in range(GH) for c in range(self.nchunk)]

    def plan(self, kind, masked=False):
        ngr, nu, nk = self.groups, len(self.units), len(self.keys)
        own, side, late = [("own",)] * self.own, [("side",)] * self.side, [("side",)] * self.late
        ours = [("max", g, i) for g in range(1, ngr) for i in range(nu)]
        nexts = [("max", ngr, i) for i in range(nu)] if kind != "last" else []
        if kind == "first":
            return nexts + [("split", ngr), ("shift", ngr)]
        out, post, shifts = [], [], []
        lead = self.lead
        ours_until, nexts_from = self.ours_until, self.nexts_from
        done = 0

        def unit():
            nonlocal done
            item = (ours + nexts)[done]
            out.append(item)
            done += 1
            if item[2] == nu - 1:
                out.append(("split", item[1]))
                shifts.append((done + 3, item[1]))
            if shifts and done >= shifts[0][0]:
                out.append(("shift", shifts.pop(0)[1]))

        def spread(x):
            if shifts and done == len(ours):
                out.append(("shift", shifts.pop(0)[1]))
            while done < min(len(ours), lead + x / ours_until * (len(ours) - lead)):
                unit()
            while side and x * self.side >= (self.side - len(side) + 1) * self.side_until * ngr:
                out.append(side.pop())
            if x >= nexts_from and not masked:
                part = (x - nexts_from) / (ngr - 0.1 - nexts_from)
                while len(late) > 1 and self.late - len(late) <= part * self.late:
                    out.append(late.pop())
                while done < min(len(ours + nexts), len(ours) + part * nu):
                    unit()

        for n in range(lead):
            while own and n * self.own >= (self.own - len(own)) * lead:
                out.append(own.pop())
            unit()
        out += own
        last = None
        for g in range(ngr):
            for k in range(nk):
                for p in range(2):
                    out.append(("score", g, k, p))
                    spread(g + (k + 0.25 * (p + 1)) / nk)
                if last:
                    out.append(("pv",) + last)
                    if last[1] == nk - 1:
                        out.append(("copy", last[0]))
                        post.append(last[0])
                if k == 1 and post:
                    out.append(("post", post.pop(0)))
                spread(g + (k + 1) / nk)
                last = (g, k)
        out += [("pv",) + last, ("copy", last[0])] + side
        out += late[1:]
        while done < len(ours + nexts):
            unit()
        out += [("shift", g) for _, g in shifts] + late[:1] + [("post", last[0])]
        return out

    def preload(self, sp, g, kscratch, qscratch, w, first):
        if not first:
            sp.wait_ge(self.scored, 2 * len(self.keys) * (g + 1))
        self.load_stacks(sp, g, kscratch, qscratch, w, self.stacks_preloaded if g else self.stack0_preloaded)

    def load_stacks(self, sp, g, kscratch, qscratch, w, loaded=None):
        loaded = loaded or self.stacks_loaded[g]
        heads = slice(g * GH, (g + 1) * GH)
        sp.dma_start(self.kst[0:STACK, g, :, 0:w], kscratch[heads, :, :, 0:w].rearrange("h d s w -> (d s) h w"))\
            .then_inc(loaded, 16)
        sp.dma_start(self.qst[0:STACK, g, :, :],
                     qscratch[heads].rearrange("h d s w -> (d s) h w")).then_inc(loaded, 16)

    def sync(self, sp, order, side=iter(()), after_shifts=None):
        n = 0
        for item in order:
            if item[0] == "shift":
                g = item[1]
                sp.wait_ge(self.shift_copied, n + 1)
                sp.dma_start(self.qst[STACK:STACK + SHIFT, g % self.groups, :, :], self.shiftT[:, g % 2, :])\
                    .then_inc(self.shift_loaded[g], 16)
                n += 1
                if g == self.groups:
                    sp.wait_ge(self.shift_loaded[g], 16)
                if g == self.groups - 1 and after_shifts:
                    after_shifts()
            if item[0] == "side":
                next(side, None)

    def tensor(self, pe, order, maskq=None, tri=None, triT=None, own=iter(()), side=iter(())):
        ps, nk = self.ps, len(self.keys)
        nmax = nscore = npv = nshift = 0
        bank7 = self.bank7
        bank7.freed = None
        for item in order:
            if item[0] == "own":
                next(own, None)
            elif item[0] == "side":
                next(side, None)
            elif item[0] == "max":
                g, (j0, nj, t, c, n) = item[1], self.units[item[2]]
                if item[2] == 0 and g == self.groups:
                    pe.wait_ge(self.stack0_preloaded, 32)
                elif item[2] == 0 and g >= self.preloaded:
                    pe.wait_ge(self.stacks_loaded[g], 32)
                if nmax >= 2:
                    pe.wait_ge(self.max_taken, nmax - 1)
                bank, sl = 4 + nmax % 2, g % self.groups
                k0 = c * self.chunk
                for j in range(j0, j0 + nj):
                    c0 = (j - j0) * n
                    mm = pe.matmul(ps[:, bank, c0:c0 + n], self.qst[0:STACK, sl, j, t * P:(t + 1) * P],
                                   self.kst[0:STACK, sl, j, k0:k0 + n], start=True, stop=not self.causal)
                    if self.causal:
                        mm = pe.matmul(ps[:, bank, c0 + n - P:c0 + n], self.identb[:, :], tri[:, :],
                                       start=False, stop=True)
                mm.then_inc(self.max_scored, 1)
                nmax += 1
            elif item[0] == "shift":
                g = item[1]
                nshift += 1
                pe.wait_ge(self.shift_split, nshift)
                bank7.take(pe)
                for t in range(T):
                    mm = pe.matmul(ps[0:SHIFT * GH, 7, t * P:(t + 1) * P], self.shift[:, g % 2, t, :],
                                   self.identb[:, :], start=True, stop=True)
                mm.then_inc(self.shift_turned, 1)
                bank7.freed_by(self.shift_copied, nshift)
            elif item[0] == "score":
                _, g, k, p = item
                sl = g
                if k == 0 and p == 0:
                    if g == 0:
                        pe.wait_ge(*self.own_ready)
                    else:
                        pe.wait_ge(self.shift_loaded[g], 16)
                if nscore >= 2:
                    pe.wait_ge(self.exped, nscore - 1)
                k0, n = self.keys[k]
                q0 = k0 if self.causal else 0
                for j in (2 * p, 2 * p + 1):
                    bank = 2 * (nscore % 2) + j % 2
                    extra = self.causal or maskq is not None
                    mm = pe.matmul(ps[0:n, bank, 0:S - q0], self.kst[0:STACK + SHIFT, sl, j, k0:k0 + n],
                                   self.qst[0:STACK + SHIFT, sl, j, q0:S], start=True, stop=not extra)
                    if self.causal:
                        mm = pe.matmul(ps[0:n, bank, 0:P], self.identb[:, :], triT[:, :], start=False, stop=True)
                    if maskq is not None:
                        for t in range(T):
                            mm = pe.matmul(ps[0:n, bank, t * P:(t + 1) * P], maskq[:, t, k0:k0 + n],
                                           self.identf[:, :], start=False, stop=(t == T - 1))
                mm.then_inc(self.scored, 1)
                nscore += 1
            elif item[0] == "pv":
                _, g, k = item
                if k == 0 and g > 0:
                    pe.wait_ge(self.oT_copied, g)
                pe.wait_ge(self.exped, 2 * npv + 2)
                k0, n = self.keys[k]
                q0 = k0 if self.causal else 0
                for j in range(GH):
                    mm = pe.matmul(ps[VW * j:VW * (j + 1), 6, q0:S], self.v[0:n, k, g * GH + j, :],
                                   self.probs[0:n, (2 * npv + j // 2) % self.npt, j % 2, q0:S],
                                   start=(k == 0), stop=(k == nk - 1))
                mm.then_inc(self.pv_done, 1)
                npv += 1
            elif item[0] == "post":
                g = item[1]
                pe.wait_ge(self.oT_copied, g + 1)
                bank7.take(pe)
                for t in range(T):
                    mm = pe.transpose(ps[:, 7, t * P:(t + 1) * P], self.oT[:, t * P:(t + 1) * P], self.identf[:, :])
                mm.then_inc(self.o_turned, 1)
                bank7.freed_by(self.o_divided, g + 1)

    def scalar(self, act, order, own=iter(()), side=iter(())):
        ps, nscore, nshift = self.ps, 0, 0
        for item in order:
            if item[0] == "own":
                next(own, None)
            elif item[0] == "side":
                next(side, None)
            elif item[0] == "shift":
                g = item[1]
                nshift += 1
                act.wait_ge(self.shift_turned, nshift)
                if nshift > 2:
                    act.wait_ge(self.shift_loaded[g - 2], 16)
                act.activation(self.shiftT[:, g % 2, :], ps[0:SHIFT * GH, 7, :], ACT.Copy)\
                    .then_inc(self.shift_copied, 1)
            elif item[0] == "score":
                _, g, k, p = item
                k0, n = self.keys[k]
                q0 = k0 if self.causal else 0
                act.wait_ge(self.scored, nscore + 1)
                if nscore >= self.npt:
                    act.wait_ge(self.pv_done, (nscore - self.npt) // 2 + 1)
                bank = 2 * (nscore % 2)
                act.activation(self.probs[0:n, nscore % self.npt, :, q0:S], ps[0:n, bank:bank + 2, 0:S - q0],
                               ACT.Exp).then_inc(self.exped, 1)
                nscore += 1
            elif item[0] == "copy":
                g = item[1]
                act.wait_ge(self.pv_done, len(self.keys) * (g + 1))
                if g >= 1:
                    act.wait_ge(self.o_turned, g)
                act.activation(self.oT[:, :], ps[:, 6, :], ACT.Copy).then_inc(self.oT_copied, 1)

    def vector(self, dve, order, steps, maskq=None, vbias=None, own=iter(()), side=iter(())):
        ps, nmax, nshift = self.ps, 0, 0
        for item in order:
            if item[0] == "own":
                next(own, None)
            elif item[0] == "side":
                next(side, None)
            elif item[0] == "max":
                g, (j0, nj, t, c, n) = item[1], self.units[item[2]]
                if item[2] == 0 and g == self.groups and self.next_mask:
                    dve.wait_ge(*self.next_mask)
                dve.wait_ge(self.max_scored, nmax + 1)
                bank = 4 + nmax % 2
                if self.masked:
                    if nmax >= 2:
                        dve.wait_ge(self.max_taken, nmax - 1)
                    dve.tensor_tensor_reduce(self.junk[:, nmax % 2, 0:n], ps[:, bank, 0:n],
                                             maskq[:, t, c * self.chunk:c * self.chunk + n], 1.0, -3.0e38,
                                             ALU.add, ALU.max, self.cmax[:, g % 2, t * GH + j0, c:c + 1])\
                        .then_inc(self.max_taken, 1)
                elif self.nchunk > 1:
                    dve.tensor_reduce(self.cmax[:, g % 2, t * GH + j0, c:c + 1], ps[:, bank, 0:n], AX.X,
                                      ALU.max).then_inc(self.max_taken, 1)
                else:
                    dve.tensor_reduce(self.nmax[:, g % 2, t, j0:j0 + nj],
                                      ps[:, bank, 0:nj * n].rearrange("p (j k) -> p j k", j=nj), AX.X, ALU.max,
                                      negate=True).then_inc(self.max_taken, 1)
                nmax += 1
            elif item[0] == "split":
                g = item[1]
                dve.wait_ge(self.max_taken, nmax)
                nm, rest = self.nmax[:, g % 2], self.rest[:, g % 2]
                if self.nchunk > 1:
                    steps.mark(dve.tensor_reduce(nm.rearrange("p t j -> p (t j)"), self.cmax[:, g % 2], AX.X,
                                                 ALU.max, negate=True))
                    steps.settle()
                if nshift >= 2:
                    dve.wait_ge(self.shift_turned, nshift - 1)
                nshift += 1
                sh = [self.shift[:, g % 2, :, lev * GH:(lev + 1) * GH] for lev in range(SHIFT)]
                steps.mark(dve.tensor_copy(sh[0], nm))
                steps.settle()
                steps.mark(dve.tensor_tensor(rest, nm, sh[0], ALU.subtract))
                steps.settle()
                steps.mark(dve.tensor_copy(sh[1], rest))
                steps.settle()
                dve.tensor_tensor(sh[2], rest, sh[1], ALU.subtract).then_inc(self.shift_split, 1)
            elif item[0] == "post":
                g = item[1]
                dve.wait_ge(self.o_turned, g + 1)
                o = ps[:, 7, :].rearrange("p (t j w) -> p t j w", t=T, j=GH)
                steps.mark(dve.reciprocal(self.inv[:, :, :], o[:, :, :, HD]))
                steps.settle()
                out = self.otok[:, :, g * GH * HD:(g + 1) * GH * HD].rearrange("p t (j d) -> p t j d", j=GH)
                inv = self.inv[:, :, :].rearrange("p t (j o) -> p t j o", o=1).to_broadcast([P, T, GH, HD])
                ins = dve.tensor_tensor(out, o[:, :, :, 0:HD], inv, ALU.mult)
                if vbias is None:
                    ins.then_inc(self.o_divided, 1)
                    continue
                ins.then_inc(self.o_divided, 1)
                dve.wait_ge(self.o_divided, g + 1)
                o3 = self.otok[:, :, g * GH * HD:(g + 1) * GH * HD]
                vb = vbias[:, g * GH * HD:(g + 1) * GH * HD].rearrange("p (o d) -> p o d", o=1)
                steps.mark(dve.tensor_tensor(o3, o3, vb.to_broadcast([P, T, GH * HD]), ALU.add))
        steps.settle()


class OutProjection:

    def __init__(self, st, ps, identf, otok, oF, wo, x, bias=None):
        self.ps, self.identf, self.otok, self.wo, self.x, self.bias = ps, identf, otok, wo, x, bias
        self.oF = oF
        self.o_ready = st.sem("o_ready")
        self.oF_in_psum = st.sem("oF_in_psum")
        self.oF_ready = st.sem("oF_ready")
        self.projected = st.sem("projected")
        self.x_done = st.sem("x_done")

    def tensor(self, pe, turn=True):
        ps = self.ps
        if turn:
            pe.wait_ge(self.o_ready, 1)
            for f in range(FT):
                for t in range(T):
                    mm = pe.transpose(ps[:, f, t * P:(t + 1) * P], self.otok[:, t, f * P:(f + 1) * P],
                                      self.identf[:, :])
                mm.then_inc(self.oF_in_psum, 1)
        for h in range(2):
            for t in (2 * h, 2 * h + 1):
                for f in range(FT):
                    if h == 0 and t == 0:
                        pe.wait_ge(self.oF_ready, f + 1)
                    mm = pe.matmul(ps[:, 2 + h, (t % 2) * D:(t % 2 + 1) * D], self.oF[:, f, t * P:(t + 1) * P],
                                   self.wo[:, f, :], start=(f == 0), stop=(f == FT - 1))
            mm.then_inc(self.projected, 1)

    def scalar(self, act):
        for f in range(FT):
            act.wait_ge(self.oF_in_psum, f + 1)
            act.activation(self.oF[:, f, :], self.ps[:, f, :], ACT.Copy).then_inc(self.oF_ready, 1)

    def vector(self, dve, steps):
        if self.bias is not None:
            for t in range(T):
                steps.mark(dve.tensor_tensor(self.x[:, t, :], self.x[:, t, :], self.bias[:, :], ALU.add))
            steps.settle()
        for h in range(2):
            dve.wait_ge(self.projected, h + 1)
            xs = self.x[:, 2 * h:2 * h + 2, :].rearrange("p t d -> p (t d)")
            dve.tensor_tensor(xs, xs, self.ps[:, 2 + h, :], ALU.add).then_inc(self.x_done, 1)


def load_x(sp, norm, x, src, b):
    sp.dma_start(x[:, :, :], src[b].rearrange("(t p) d -> p t d", p=P)).then_inc(norm.x_loaded, 16)


def first_maxima(att, dve_steps, tri=None, maskq=None):
    order = att.plan("first")
    return {"sync": lambda sp: att.sync(sp, order),
            "tensor": lambda pe: att.tensor(pe, order, tri=tri),
            "vector": lambda dve: att.vector(dve, order, Steps(dve, dve_steps), maskq=maskq),
            "scalar": lambda act: att.scalar(act, order),
            "gpsimd": lambda pool: None}


def keep_residual(nc, pool, residual, x, kept):
    pool.tensor_copy(residual[:, :, :], x[:, :, :]).then_inc(kept, 1)


def store_x(sp, done, count, stored, x, dst, b):
    sp.wait_ge(done, count)
    sp.dma_start(dst[b].rearrange("(t p) d -> p t d", p=P), x[:, :, :]).then_inc(stored, 16)
    sp.wait_ge(stored, 16)


def load_constants(nc, st, tiles, att=None):
    loaded = st.sem("constants_loaded")
    with nc.Block() as block:
        @block.sync
        def _(sp):
            for tile, src in tiles:
                sp.dma_start(tile, src).then_inc(loaded, 16)
            sp.wait_ge(loaded, 16 * len(tiles))

        if att:
            @block.vector
            def _(dve):
                dve.memset(att.kst[STACK:STACK + SHIFT, :, :, :].rearrange("p a b c -> p (a b c)"), 1.0)

            @block.gpsimd
            def _(pool):
                pool.memset(att.v[:, :, :, HD:VW], 1.0)


def weight(st, tiles, name, src):
    n_in, n_out = src.shape
    if n_in <= P:
        t = st.sb(name, [n_in, n_out])
        tiles.append((t[:, :], src))
    else:
        t = st.sb(name, [P, n_in // P, n_out])
        tiles.append((t[:, :, :], src.rearrange("(f p) n -> p f n", p=P)))
    return t


def column(st, tiles, name, src):
    t = st.sb(name, [P, FT])
    tiles.append((t[:, :], src))
    return t


def constant(st, tiles, name, src, dt=F32):
    t = st.sb(name, list(src.shape), dt)
    tiles.append((t[tuple(slice(None) for _ in src.shape)], src))
    return t


def bias_row(st, tiles, name, src):
    t = st.sb(name, [P, D])
    tiles.append((t[:, :], src.rearrange("(o d) -> o d", o=1).to_broadcast([P, D])))
    return t


def v_heads(ps_bank):
    return ps_bank.rearrange("p (t h d) -> p t h d", t=2, h=H)



def latent_attention(nc, w, x_src, x_dst, kscratch, qscratch):
    with ExitStack() as ctx:
        st = Stage(nc, ctx, "s1")
        ps = st.psum()
        loads = []
        identf = constant(st, loads, "identf", w["identf"])
        identb = constant(st, loads, "identb", w["identb"], BF16)
        tri = constant(st, loads, "tri", w["tri"], BF16)
        triT = constant(st, loads, "triT", w["triT"], BF16)
        wdkv = weight(st, loads, "wdkv", w["L0_attn_W_DKV"])
        wuk = weight(st, loads, "wuk", w["L0_attn_W_UK"])
        wuv = weight(st, loads, "wuv", w["L0_attn_W_UV"])
        wuq = weight(st, loads, "wuq", w["L0_attn_W_UQ"])
        wo = weight(st, loads, "wo", w["L0_attn_W_O"])
        x = st.sb("x", [P, T, D])
        residual = st.sb("residual", [P, T, D])
        latent = st.sb("latent", [64, S])
        bank7 = SharedBank(7)
        norm = Norm(st, ps, x, identf, shared=bank7)
        split = Split(st, S, 4)
        att = Attention(st, ps, identf, identb, st.sb("otok", [P, T, D]), S, NG, causal=True, bank7=bank7,
                        own=2, side=13, lead=7, preloaded=2)
        proj = OutProjection(st, ps, identf, att.otok, st.sb("oF", [P, FT, S]), wo, residual)
        latent_in_psum, latent_ready = st.sem("latent_in_psum"), st.sem("latent_ready")
        qk_in_psum, qk_copied = st.sem("qk_in_psum"), st.sem("qk_copied")
        v_in_psum, kept = st.sem("v_in_psum"), st.sem("kept")
        dve_steps, act_steps, stored = st.sem("dve_steps"), st.sem("act_steps"), st.sem("stored")
        side_dve_steps = st.sem("side_dve_steps")
        load_constants(nc, st, loads, att)
        att.own_ready = (att.v_ready, 2)

        def prologue_sync(sp, b, first):
            if not first:
                sp.wait_ge(kept, 1)
            load_x(sp, norm, x, x_src, b)
            yield from skip(1 + Norm.STEPS + 1)
            for i, (f, is_q) in enumerate(ITEMS):
                split.sync(sp, i, S, (qscratch if is_q else kscratch)[b], (8 * f, 8 * f + 8),
                           Q_LAYOUT if is_q else K_LAYOUT)
                yield
                if i == 1:
                    split.wait_in_dram(sp, (0, 1))
                    att.preload(sp, 0, kscratch[b], qscratch[b], S, first)
                    yield
            for g in range(1, att.preloaded):
                att.preload(sp, g, kscratch[b], qscratch[b], S, first)
            yield
            split.wait_in_dram(sp, (2, 3))
            sp.wait_ge(att.stack0_preloaded, 32)
            sp.wait_ge(att.stacks_preloaded, 32 * (att.preloaded - 1))

        def prologue_tensor(pe, b, first):
            yield
            yield from norm.tensor(pe)
            bank7.take(pe)
            for c in range(FT):
                pe.wait_ge(norm.xnT_ready, c + 1)
                mm = pe.matmul(ps[0:64, 7, :], wdkv[:, c, :], norm.xnT[:, c, 1:], start=(c == 0), stop=(c == 1))
            mm.then_inc(latent_in_psum, 1)
            bank7.freed_by(latent_ready, 1)
            yield
            for i, (f, is_q) in enumerate(ITEMS):
                bank7.take(pe)
                if is_q:
                    for c in range(FT):
                        mm = pe.matmul(ps[:, 7, :], wuq[:, c, f * P:(f + 1) * P], norm.xnT[:, c, 1:],
                                       start=(c == 0), stop=(c == 1))
                else:
                    pe.wait_ge(latent_ready, 1)
                    mm = pe.matmul(ps[:, 7, :], wuk[:, f * P:(f + 1) * P], latent[:, :], start=True, stop=True)
                mm.then_inc(qk_in_psum, 1)
                bank7.freed_by(qk_copied, i + 1)
                yield
                if i == 1:
                    yield
            yield

        def prologue_scalar(act, b, first):
            steps = Steps(act, act_steps)
            if first:
                act.preload_act_table_set(EXP_AND_LN)
            yield
            yield from norm.scalar(act, steps)
            act.wait_ge(latent_in_psum, 1)
            act.activation(latent[:, :], ps[0:64, 7, :], ACT.Copy).then_inc(latent_ready, 1)
            yield
            for i, (f, is_q) in enumerate(ITEMS):
                act.wait_ge(qk_in_psum, i + 1)
                if i >= 2:
                    act.wait_ge(split.levels_ready, i - 1)
                act.activation(split.full[i % 2][:, :], ps[:, 7, :], ACT.Copy,
                               scale=HD ** -0.5 if is_q else 1.0).then_inc(qk_copied, 1)
                act.wait_ge(qk_copied, i + 1)
                act.sem_inc(split.full_ready, 1)
                split.scalar(act, i, S)
                yield
                if i == 1:
                    yield
            yield

        def prologue_vector(dve, b, first):
            steps = Steps(dve, side_dve_steps)
            yield
            yield from norm.vector(dve, steps)
            yield
            for i in range(4):
                split.vector(dve, steps, i, S)
                yield
                if i == 1:
                    yield
            yield

        def sync(sp, b, side):
            order = att.plan(kind(side))
            side = side()
            for g in range(att.preloaded, NG):
                att.load_stacks(sp, g, kscratch[b], qscratch[b], S)
            att.sync(sp, order, side=side)
            store_x(sp, proj.x_done, 2, stored, residual, x_dst, b)
            exhaust(side)

        def tensor(pe, b, side):
            att.tensor(pe, att.plan(kind(side)), tri=tri, triT=triT, own=v_tensor(pe), side=side())
            proj.tensor(pe)

        def v_tensor(pe):
            for t in range(T):
                mm = pe.matmul(ps[:, t // 2, (t % 2) * D:(t % 2 + 1) * D], latent[:, t * P:(t + 1) * P],
                               wuv[:, :], start=True, stop=True)
                if t % 2:
                    mm.then_inc(v_in_psum, 1)
                    yield

        def v_scalar(act):
            for n in range(2):
                act.wait_ge(v_in_psum, n + 1)
                act.activation(att.v[:, 2 * n:2 * n + 2, :, 0:HD], v_heads(ps[:, n, :]), ACT.Copy)\
                    .then_inc(att.v_ready, 1)
                yield

        def scalar(act, b, side):
            act.preload_act_table_set(EXP_AND_LN)
            att.scalar(act, att.plan(kind(side)), own=v_scalar(act), side=side())
            proj.scalar(act)

        def vector(dve, b, side):
            steps = Steps(dve, dve_steps)
            att.vector(dve, att.plan(kind(side)), steps, side=side())
            dve.wait_ge(att.o_divided, NG)
            dve.sem_inc(proj.o_ready, 1)
            dve.wait_ge(kept, 1)
            proj.vector(dve, steps)

        def gpsimd(pool, b, side):
            keep_residual(nc, pool, residual, x, kept)

        pipelined_loop(nc, st,
                       {"sync": prologue_sync, "tensor": prologue_tensor, "scalar": prologue_scalar,
                        "vector": prologue_vector, "gpsimd": lambda pool, b, first: skip(0)},
                       {"sync": sync, "tensor": tensor, "scalar": scalar, "vector": vector, "gpsimd": gpsimd},
                       first_maxima(att, dve_steps, tri=tri))



def cross_attention(nc, w, x_src, x_dst, kscratch, qscratch):
    with ExitStack() as ctx:
        st = Stage(nc, ctx, "s2")
        ps = st.psum()
        loads = []
        identf = constant(st, loads, "identf", w["identf"])
        identb = constant(st, loads, "identb", w["identb"], BF16)
        wq = weight(st, loads, "wq", w["L0_xattn_Wq"])
        wk = weight(st, loads, "wk", w["L0_xattn_Wk"])
        wv = weight(st, loads, "wv", w["L0_xattn_Wv"])
        wo = weight(st, loads, "wo", w["L0_xattn_Wo"])
        bq = column(st, loads, "bq", w["L0_xattn_bq"])
        bk = column(st, loads, "bk", w["L0_xattn_bk"])
        bv = bias_row(st, loads, "bv", w["L0_xattn_bv"])
        bo = bias_row(st, loads, "bo", w["L0_xattn_bo"])
        x = st.sb("x", [P, T, D])
        ctxT = st.sb("ctxT", [P, FT, CTX])
        maskq = st.sb("maskq", [P, T, CTX])
        keys = tiles_of(CTX)
        residual = st.sb("residual", [P, T, D])
        bank7 = SharedBank(7)
        norm = Norm(st, ps, x, identf, shared=bank7)
        split = Split(st, CTX, 4)
        pieces = [(c, min(512, CTX - c)) for c in range(0, CTX, 512)]
        jobs = [(i, f, is_q, c, n) for i, (f, is_q) in enumerate(ITEMS)
                for c, n in ([(0, S)] if is_q else pieces)]
        att = Attention(st, ps, identf, identb, st.sb("otok", [P, T, D]), CTX, NG, causal=False, masked=True,
                        bank7=bank7, own=len(keys), side=1 + Norm.STEPS + len(jobs) + 2,
                        side_until=0.7, lead=26, ours_until=2.4, nexts_from=2.85, late=1 + 2 * T, preloaded=NG)
        oF = norm.xn[:, :, :].rearrange("p t d -> p (t d)").rearrange("p (f s) -> p f s", f=FT)
        proj = OutProjection(st, ps, identf, att.otok, oF, wo, residual, bias=bo)
        most, least, nonzero = st.sb("most", [P, T]), st.sb("least", [P, T]), st.sb("nonzero", [P, 1])
        flag = st.sb("flag", [1, 1], U32)
        ctx_loaded, mask_loaded = st.sem("ctx_loaded"), st.sem("mask_loaded")
        nonzero_ready, count_in_psum, flag_ready = st.sem("nonzero_ready"), st.sem("count_in_psum"), st.sem("flag_ready")
        flag_read = st.sem("flag_read")
        proj_in_psum, proj_copied = st.sem("proj_in_psum"), st.sem("proj_copied")
        v_in_psum, kept = st.sem("v_in_psum"), st.sem("kept")
        dve_steps, act_steps, stored = st.sem("dve_steps"), st.sem("act_steps"), st.sem("stored")
        side_dve_steps = st.sem("side_dve_steps")
        load_constants(nc, st, loads, att)
        att.own_ready = (att.v_ready, len(keys))
        att.next_mask = (mask_loaded, 16)
        own_units, all_steps = (NG - 1) * len(att.units), NG * 2 * len(keys)

        def prologue_sync(sp, b, first, masked=False):
            if not first:
                sp.wait_ge(kept, 1)
            load_x(sp, norm, x, x_src, b)
            if not first:
                sp.wait_ge(v_in_psum, len(keys))
            for f in range(FT):
                sp.dma_start(ctxT[:, f, :], w["ctxT"][b, f * P:(f + 1) * P, :]).then_inc(ctx_loaded, 16)
            yield from skip(1 + Norm.STEPS)
            for i, f, is_q, c, n in jobs:
                if c + n == (S if is_q else CTX):
                    split.sync(sp, i, c + n, (qscratch if is_q else kscratch)[b], (8 * f, 8 * f + 8),
                               Q_LAYOUT if is_q else K_LAYOUT)
                yield
                if i == 1:
                    split.wait_in_dram(sp, (0, 1))
                    att.preload(sp, 0, kscratch[b], qscratch[b], CTX, first)
                    yield
            att.preload(sp, 1, kscratch[b], qscratch[b], CTX, first)
            yield
            if masked:
                sp.wait_ge(att.scored, all_steps)
            if first or masked:
                load_mask(sp, b)
            yield from skip(2 * T)
            split.wait_in_dram(sp, (2, 3))
            for g in (2, 3):
                att.preload(sp, g, kscratch[b], qscratch[b], CTX, first)
            sp.wait_ge(att.stack0_preloaded, 32)
            sp.wait_ge(att.stacks_preloaded, 32 * (NG - 1))

        def prologue_tensor(pe, b, first, masked=False):
            yield
            yield from norm.tensor(pe)
            for number, (i, f, is_q, c, n) in enumerate(jobs):
                bank7.take(pe)
                if number == 0:
                    pe.wait_ge(ctx_loaded, 16 * FT)
                    pe.wait_ge(norm.xnT_ready, FT)
                for h in range(FT):
                    if is_q:
                        mm = pe.matmul(ps[:, 7, :], wq[:, h, f * P:(f + 1) * P], norm.xnT[:, h, 1:],
                                       start=(h == 0), stop=(h == 1))
                    else:
                        mm = pe.matmul(ps[:, 7, 0:n], wk[:, h, f * P:(f + 1) * P], ctxT[:, h, c:c + n],
                                       start=(h == 0), stop=(h == 1))
                mm.then_inc(proj_in_psum, 1)
                bank7.freed_by(proj_copied, number + 1)
                yield
                if i == 1:
                    yield
            yield from skip(1 + 2 * T)
            bank7.take(pe)
            pe.wait_ge(nonzero_ready, 1)
            pe.matmul(ps[0:1, 7, 0:1], nonzero[:, :], att.v[:, 0, 0, HD:HD + 1], start=True, stop=True)\
                .then_inc(count_in_psum, 1)
            bank7.freed_by(flag_ready, 1)
            yield

        def prologue_scalar(act, b, first, masked=False):
            steps = Steps(act, act_steps)
            if first:
                act.preload_act_table_set(EXP_AND_LN)
            yield
            yield from norm.scalar(act, steps)
            for number, (i, f, is_q, c, n) in enumerate(jobs):
                act.wait_ge(proj_in_psum, number + 1)
                if i >= 2 and c == 0:
                    act.wait_ge(split.levels_ready, i - 1)
                act.activation(split.full[i % 2][:, c:c + n], ps[:, 7, 0:n], ACT.Identity,
                               bias=(bq if is_q else bk)[:, f:f + 1]).then_inc(proj_copied, 1)
                if c + n == (S if is_q else CTX):
                    act.wait_ge(proj_copied, number + 1)
                    if is_q:
                        steps.mark(act.activation(split.full[i % 2][:, 0:S], split.full[i % 2][:, 0:S],
                                                  ACT.Copy, scale=HD ** -0.5))
                        steps.settle()
                    act.sem_inc(split.full_ready, 1)
                    split.scalar(act, i, c + n)
                yield
                if i == 1:
                    yield
            yield from skip(2 + 2 * T)

        def prologue_vector(dve, b, first, masked=False):
            steps = Steps(dve, side_dve_steps)
            yield
            yield from norm.vector(dve, steps)
            for i, f, is_q, c, n in jobs:
                if c + n == (S if is_q else CTX):
                    split.vector(dve, steps, i, c + n)
                yield
                if i == 1:
                    yield
            yield
            dve.wait_ge(mask_loaded, 16)
            for q in range(T):
                steps.mark(dve.tensor_reduce(most[:, q:q + 1], maskq[:, q, :], AX.X, ALU.max))
                yield
                steps.mark(dve.tensor_reduce(least[:, q:q + 1], maskq[:, q, :], AX.X, ALU.min))
                yield
            steps.settle()
            steps.mark(dve.tensor_scalar(least[:, :], least[:, :], 0.0, None, ALU.is_lt))
            steps.settle()
            steps.mark(dve.scalar_tensor_tensor(out=most[:, :], in0=most[:, :], scalar=0.0, in1=least[:, :],
                                                op0=ALU.is_gt, op1=ALU.add))
            steps.settle()
            dve.tensor_reduce(nonzero[:, :], most[:, :], AX.X, ALU.add).then_inc(nonzero_ready, 1)
            dve.wait_ge(count_in_psum, 1)
            if not first:
                dve.wait_ge(flag_read, 4)
            dve.tensor_copy(flag[:, :], ps[0:1, 7, 0:1]).then_inc(flag_ready, 1)
            yield

        def load_mask(sp, b):
            sp.dma_start(maskq[:, :, :], w["mask"][b].rearrange("(t p) k -> p t k", p=P)).then_inc(mask_loaded, 16)

        def load_mask_early(sp, b):
            sp.wait_ge(att.max_taken, own_units)
            load_mask(sp, b)

        def is_masked(e):
            value = e.value_load(flag[0:1, 0:1])
            e.sem_inc(flag_read, 1)
            return value != 0

        def sync(sp, b, side):
            def run(masked):
                steps = side(masked)
                early = not masked and side is not NO_SIDE
                att.sync(sp, att.plan(kind(side), masked), side=steps,
                         after_shifts=(lambda: load_mask_early(sp, b + 1)) if early else None)
                exhaust(steps)

            with sp.If(is_masked(sp)):
                run(True)
            with sp.Else():
                run(False)
            store_x(sp, proj.x_done, 2, stored, residual, x_dst, b)

        def tensor(pe, b, side):
            with pe.If(is_masked(pe)):
                att.tensor(pe, att.plan(kind(side), True), maskq=maskq, own=v_tensor(pe), side=side(True))
            with pe.Else():
                att.tensor(pe, att.plan(kind(side)), own=v_tensor(pe), side=side(False))
            proj.tensor(pe)

        def v_tensor(pe):
            for k, (k0, n) in enumerate(keys):
                if k >= 4:
                    pe.wait_ge(att.v_ready, k - 3)
                for h in range(FT):
                    mm = pe.matmul(ps[0:n, k % 4, 0:D], ctxT[:, h, k0:k0 + n], wv[:, h, :],
                                   start=(h == 0), stop=(h == 1))
                mm.then_inc(v_in_psum, 1)
                yield

        def v_scalar(act):
            for k, (k0, n) in enumerate(keys):
                act.wait_ge(v_in_psum, k + 1)
                act.activation(att.v[0:n, k, :, 0:HD], ps[0:n, k % 4, 0:D].rearrange("p (h d) -> p h d", h=H),
                               ACT.Copy).then_inc(att.v_ready, 1)
                yield

        def scalar(act, b, side):
            act.preload_act_table_set(EXP_AND_LN)
            with act.If(is_masked(act)):
                att.scalar(act, att.plan(kind(side), True), own=v_scalar(act), side=side(True))
            with act.Else():
                att.scalar(act, att.plan(kind(side)), own=v_scalar(act), side=side(False))
            proj.scalar(act)

        def vector(dve, b, side):
            with dve.If(is_masked(dve)):
                steps = Steps(dve, dve_steps)
                att.vector(dve, att.plan(kind(side), True), steps, maskq=maskq, vbias=bv, side=side(True))
            with dve.Else():
                steps = Steps(dve, dve_steps)
                att.vector(dve, att.plan(kind(side)), steps, maskq=maskq, vbias=bv, side=side(False))
            dve.sem_inc(proj.o_ready, 1)
            dve.wait_ge(kept, 1)
            proj.vector(dve, steps)

        def gpsimd(pool, b, side):
            keep_residual(nc, pool, residual, x, kept)

        pipelined_loop(nc, st,
                       {"sync": prologue_sync, "tensor": prologue_tensor, "scalar": prologue_scalar,
                        "vector": prologue_vector, "gpsimd": lambda pool, b, first: skip(0)},
                       {"sync": sync, "tensor": tensor, "scalar": scalar, "vector": vector, "gpsimd": gpsimd},
                       first_maxima(att, dve_steps, maskq=maskq))



def channel_mix(nc, w, x_src, x_dst):
    with ExitStack() as ctx:
        st = Stage(nc, ctx, "s3")
        ps = st.psum()
        loads = []
        identf = constant(st, loads, "identf", w["identf"])
        wr = weight(st, loads, "wr", w["L0_ffn_W_r"])
        wk = weight(st, loads, "wk", w["L0_ffn_W_k"])
        wv = weight(st, loads, "wv", w["L0_ffn_W_v"])
        mu_r = column(st, loads, "mu_r", w["L0_ffn_mu_r"])
        mu_k = column(st, loads, "mu_k", w["L0_ffn_mu_k"])
        x, residual = st.sb("x", [P, T, D]), st.sb("residual", [P, T, D])
        norm = Norm(st, ps, x, identf)
        step = st.sb("step", [P, FT, S])
        xr, xk = st.sb("xr", [P, FT, S]), st.sb("xk", [P, FT, S])
        act_k = st.sb("act_k", [P, FT, S])
        gate = st.sb("gate", [P, T, D])
        part = st.sb("part", [P, T, D])
        xk_ready, xr_ready = st.sem("xk_ready"), st.sem("xr_ready")
        k_in_psum, k_relu, act_k_ready = st.sem("k_in_psum"), st.sem("k_relu"), st.sem("act_k_ready")
        r_in_psum, gate_ready, v_in_psum = st.sem("r_in_psum"), st.sem("gate_ready"), st.sem("v_in_psum")
        x_done, gated, kept = st.sem("x_done"), st.sem("gated"), st.sem("kept")
        norm_dve_steps = st.sem("norm_dve_steps")
        dve_steps, act_steps, stored = st.sem("dve_steps"), st.sem("act_steps"), st.sem("stored")
        load_constants(nc, st, loads)
        with nc.Block() as block:
            @block.vector
            def _(dve):
                dve.memset(norm.xnT[:, :, 0:1], 0.0)

        def prologue_sync(sp, b, first):
            if not first:
                sp.wait_ge(kept, 1)
            load_x(sp, norm, x, x_src, b)
            yield from skip(Norm.STEPS)

        def prologue_tensor(pe, b, first):
            yield from norm.tensor(pe)

        def prologue_scalar(act, b, first):
            if first:
                act.preload_act_table_set(EXP_AND_LN)
            norming = norm.scalar(act, Steps(act, act_steps))
            yield next(norming)
            yield next(norming)
            if not first:
                act.wait_ge(xr_ready, FT)
            yield from norming

        def prologue_vector(dve, b, first):
            yield from norm.vector(dve, Steps(dve, norm_dve_steps))

        def sync(sp, b, side):
            side = side()
            next(side, None)
            store_x(sp, x_done, 2, stored, residual, x_dst, b)
            exhaust(side)

        def gpsimd(pool, b, side):
            keep_residual(nc, pool, residual, x, kept)

        def tensor(pe, b, side):
            for f in range(FT):
                for c in range(FT):
                    if f == 0:
                        pe.wait_ge(xk_ready, c + 1)
                    mm = pe.matmul(ps[:, 2 + f, :], wk[:, c, f * P:(f + 1) * P], xk[:, c, :],
                                   start=(c == 0), stop=(c == 1))
                mm.then_inc(k_in_psum, 1)
            pe.wait_ge(xr_ready, FT)
            for src, wt, base, done in ((xr, wr, 4, r_in_psum), (act_k, wv, 6, v_in_psum)):
                for t in range(T):
                    for c in range(FT):
                        if src is act_k and t == 0:
                            pe.wait_ge(act_k_ready, c + 1)
                        mm = pe.matmul(ps[:, base + t // 2, (t % 2) * D:(t % 2 + 1) * D],
                                       src[:, c, t * P:(t + 1) * P], wt[:, c, :], start=(c == 0), stop=(c == 1))
                    if t % 2:
                        mm.then_inc(done, 1)
            exhaust(side())

        def scalar(act, b, side):
            side = side()
            next(side, None)
            for f in range(FT):
                act.wait_ge(k_in_psum, f + 1)
                act.activation(act_k[:, f, :], ps[:, 2 + f, :], ACT.Relu).then_inc(k_relu, 1)
            for f in range(FT):
                act.wait_ge(k_relu, f + 1)
                act.activation(act_k[:, f, :], act_k[:, f, :], ACT.Square).then_inc(act_k_ready, 1)
            next(side, None)
            for h in range(2):
                act.wait_ge(r_in_psum, h + 1)
                act.activation(gate[:, 2 * h:2 * h + 2, :], ps[:, 4 + h, :].rearrange("p (t d) -> p t d", t=2),
                               ACT.Tanh, scale=0.5).then_inc(gate_ready, 1)
            exhaust(side)

        def vector(dve, b, side):
            steps, side = Steps(dve, dve_steps), side()
            for f in range(FT):
                cur, prev = norm.xnT[:, f, 1:S + 1], norm.xnT[:, f, 0:S]
                steps.mark(dve.tensor_tensor(step[:, f, :], cur, prev, ALU.subtract))
                steps.settle()
                dve.scalar_tensor_tensor(out=xk[:, f, :], in0=step[:, f, :], scalar=mu_k[:, f:f + 1], in1=prev,
                                         op0=ALU.mult, op1=ALU.add).then_inc(xk_ready, 1)
            for f in range(FT):
                dve.scalar_tensor_tensor(out=xr[:, f, :], in0=step[:, f, :], scalar=mu_r[:, f:f + 1],
                                         in1=norm.xnT[:, f, 0:S], op0=ALU.mult, op1=ALU.add).then_inc(xr_ready, 1)
            for _ in range(3):
                next(side, None)
            dve.wait_ge(kept, 1)
            for h in range(2):
                dve.wait_ge(gate_ready, h + 1)
                dve.wait_ge(v_in_psum, h + 1)
                two = slice(2 * h, 2 * h + 2)
                dve.scalar_tensor_tensor(out=part[:, two, :], in0=gate[:, two, :], scalar=1.0,
                                         in1=ps[:, 6 + h, :].rearrange("p (t d) -> p t d", t=2), op0=ALU.add,
                                         op1=ALU.mult).then_inc(gated, 1)
                dve.wait_ge(gated, h + 1)
                dve.scalar_tensor_tensor(out=residual[:, two, :], in0=part[:, two, :], scalar=0.5,
                                         in1=residual[:, two, :],
                                         op0=ALU.mult, op1=ALU.add).then_inc(x_done, 1)
            exhaust(side)

        pipelined_loop(nc, st,
                       {"sync": prologue_sync, "tensor": prologue_tensor, "scalar": prologue_scalar,
                        "vector": prologue_vector, "gpsimd": lambda pool, b, first: skip(0)},
                       {"sync": sync, "tensor": tensor, "scalar": scalar, "vector": vector, "gpsimd": gpsimd})



def linear_attention(nc, w, x_src, x_dst):
    with ExitStack() as ctx:
        st = Stage(nc, ctx, "s5")
        ps = st.psum()
        loads = []
        identf = constant(st, loads, "identf", w["identf"])
        blocks = constant(st, loads, "blocks", w["blocks"])
        wq = weight(st, loads, "wq", w["L1_xattn_Wq"])
        wk = weight(st, loads, "wk", w["L1_xattn_Wk"])
        wv = weight(st, loads, "wv", w["L1_xattn_Wv"])
        wo = weight(st, loads, "wo", w["L1_xattn_Wo"])
        bq = column(st, loads, "bq", w["L1_xattn_bq"])
        bk = bias_row(st, loads, "bk", w["L1_xattn_bk"])
        bv = bias_row(st, loads, "bv", w["L1_xattn_bv"])
        bo = bias_row(st, loads, "bo", w["L1_xattn_bo"])
        keys = tiles_of(CTX)
        x = st.sb("x", [P, T, D])
        ctxT = st.sb("ctxT", [P, FT, CTX])
        bank7 = SharedBank(7)
        norm = Norm(st, ps, x, identf, shared=bank7)
        kraw = st.sb("kraw", [P, 2, D])
        kexp = st.sb("kexp", [P, 2, D])
        k = st.sb("k", [P, 2, D])
        ksq = st.sb("ksq", [P, 2, D])
        v = st.sb("v", [P, 2, D])
        ones = st.sb("ones", [P, 1])
        qraw, qexp = st.sb("qraw", [P, FT, S]), st.sb("qexp", [P, FT, S])
        q, qsq, qn = st.sb("q", [P, FT, S]), st.sb("qsq", [P, FT, S]), st.sb("qn", [P, FT, S])
        kv = st.sb("kv", [P, FT, P])
        knorm, kinv = st.sb("knorm", [P, FT]), st.sb("kinv", [P, FT])
        proj = OutProjection(st, ps, identf, norm.xn, st.sb("oF", [P, FT, S]), wo, x, bias=bo)
        ctx_loaded = st.sem("ctx_loaded")
        kv_in_psum, kraw_ready, kexp_ready = st.sem("kv_in_psum"), st.sem("kraw_ready"), st.sem("kexp_ready")
        k_ready, v_ready, ksq_ready = st.sem("k_ready"), st.sem("v_ready"), st.sem("ksq_ready")
        kv_added, ones_ready = st.sem("kv_added"), st.sem("ones_ready")
        q_in_psum, qraw_ready, qexp_ready = st.sem("q_in_psum"), st.sem("qraw_ready"), st.sem("qexp_ready")
        q_ready, qsq_ready, qsum_in_psum = st.sem("q_ready"), st.sem("qsq_ready"), st.sem("qsum_in_psum")
        qinv_ready, qn_ready, kv_ready = st.sem("qinv_ready"), st.sem("qn_ready"), st.sem("kv_ready")
        ksum_copied, kinv_ready = st.sem("ksum_copied"), st.sem("kinv_ready")
        norm_dve_steps = st.sem("norm_dve_steps")
        dve_steps, act_steps, stored = st.sem("dve_steps"), st.sem("act_steps"), st.sem("stored")
        load_constants(nc, st, loads)
        with nc.Block() as block:
            @block.vector
            def _(dve):
                dve.memset(ones[:, :], 1.0)

        def prologue_sync(sp, b, first):
            if not first:
                sp.wait_ge(kv_in_psum, len(keys))
            for f in range(FT):
                sp.dma_start(ctxT[:, f, :], w["ctxT"][b, f * P:(f + 1) * P, :]).then_inc(ctx_loaded, 16)
            yield
            sp.wait_ge(ctx_loaded, 16 * FT)

        def nothing(e, b, first):
            yield

        def sync(sp, b, side):
            side = side()
            load_x(sp, norm, x, x_src, b)
            next(side, None)
            store_x(sp, proj.x_done, 2, stored, x, x_dst, b)
            exhaust(side)

        def tensor(pe, b, side):
            bank7.freed = None
            norming = norm.tensor(pe)

            def accumulate(i):
                n = keys[i][1]
                pe.wait_ge(k_ready, i + 1)
                pe.wait_ge(v_ready, i + 1)
                pe.wait_ge(ksq_ready, i + 1)
                for f in range(FT):
                    pe.matmul(ps[:, 4 + f, 0:P], k[0:n, i % 2, f * P:(f + 1) * P], v[0:n, i % 2, f * P:(f + 1) * P],
                              start=(i == 0), stop=(i == len(keys) - 1))
                for f in range(FT):
                    mm = pe.matmul(ps[:, f, 0:1], ksq[0:n, i % 2, f * P:(f + 1) * P], ones[0:n, :],
                                   start=(i == 0), stop=(i == len(keys) - 1))
                mm.then_inc(kv_added, 1)

            for i, (k0, n) in enumerate(keys):
                if i >= 2:
                    pe.wait_ge(kraw_ready, i - 1)
                    pe.wait_ge(v_ready, i - 1)
                for c, wt in enumerate((wk, wv)):
                    for f in range(FT):
                        mm = pe.matmul(ps[0:n, 2 + i % 2, c * D:(c + 1) * D], ctxT[:, f, k0:k0 + n], wt[:, f, :],
                                       start=(f == 0), stop=(f == 1))
                mm.then_inc(kv_in_psum, 1)
                if i >= 1:
                    accumulate(i - 1)
                if i >= 2:
                    next(norming, None)
            exhaust(norming)
            pe.wait_ge(norm.xnT_ready, FT)
            for f in range(FT):
                for c in range(FT):
                    mm = pe.matmul(ps[:, 6 + f, :], wq[:, c, f * P:(f + 1) * P], norm.xnT[:, c, 1:],
                                   start=(c == 0), stop=(c == 1))
                mm.then_inc(q_in_psum, 1)
            accumulate(len(keys) - 1)
            pe.wait_ge(kraw_ready, len(keys))
            pe.wait_ge(v_ready, len(keys))
            for f in range(FT):
                pe.wait_ge(qsq_ready, f + 1)
                pe.matmul(ps[:, 2 + f, :], blocks[:, :], qsq[:, f, :], start=True, stop=True)\
                    .then_inc(qsum_in_psum, 1)
            for f in range(FT):
                pe.wait_ge(qn_ready, f + 1)
                pe.wait_ge(kv_ready, f + 1)
                pe.wait_ge(ksum_copied, FT)
                pe.matmul(ps[:, f, :], kv[:, f, :], qn[:, f, :], start=True, stop=True)\
                    .then_inc(proj.oF_in_psum, 1)
            pe.wait_ge(qinv_ready, FT)
            proj.tensor(pe, turn=False)

        def scalar(act, b, side):
            act.preload_act_table_set(EXP_AND_LN)
            steps = Steps(act, act_steps)
            norming = norm.scalar(act, steps)
            for i, (k0, n) in enumerate(keys):
                act.wait_ge(kraw_ready, i + 1)
                if i >= 2:
                    act.wait_ge(k_ready, i - 1)
                act.activation(kexp[0:n, i % 2, :], kraw[0:n, i % 2, :], ACT.Exp).then_inc(kexp_ready, 1)
                act.wait_ge(k_ready, i + 1)
                if i >= 2:
                    act.wait_ge(kv_added, i - 1)
                act.activation(ksq[0:n, i % 2, :], k[0:n, i % 2, :], ACT.Square).then_inc(ksq_ready, 1)
                if i >= 2:
                    next(norming, None)
            exhaust(norming)
            for f in range(FT):
                act.wait_ge(q_in_psum, f + 1)
                act.activation(qraw[:, f, :], ps[:, 6 + f, :], ACT.Identity, bias=bq[:, f:f + 1])\
                    .then_inc(qraw_ready, 1)
            for f in range(FT):
                act.wait_ge(qraw_ready, f + 1)
                act.activation(qexp[:, f, :], qraw[:, f, :], ACT.Exp).then_inc(qexp_ready, 1)
            for f in range(FT):
                act.wait_ge(q_ready, f + 1)
                act.activation(qsq[:, f, :], q[:, f, :], ACT.Square).then_inc(qsq_ready, 1)
            for f in range(FT):
                act.wait_ge(qsum_in_psum, f + 1)
                steps.mark(act.activation(qsq[:, f, :], ps[:, 2 + f, :], ACT.Ln, scale=float(HD)))
                steps.settle()
                act.activation(qsq[:, f, :], qsq[:, f, :], ACT.Exp, scale=-0.5).then_inc(qinv_ready, 1)
            act.wait_ge(ksum_copied, FT)
            steps.mark(act.activation(knorm[:, :], knorm[:, :], ACT.Ln, scale=float(S)))
            steps.settle()
            act.activation(kinv[:, :], knorm[:, :], ACT.Exp, scale=-0.5).then_inc(kinv_ready, 1)
            proj.scalar(act)

        def vector(dve, b, side):
            steps = Steps(dve, dve_steps)
            norming = norm.vector(dve, Steps(dve, norm_dve_steps))

            def elu(i, n):
                dve.wait_ge(kexp_ready, i + 1)
                steps.mark(dve.tensor_scalar(kraw[0:n, i % 2, :], kraw[0:n, i % 2, :], 0.0, -1.0, ALU.max, ALU.add))
                steps.settle()
                dve.scalar_tensor_tensor(out=k[0:n, i % 2, :], in0=kexp[0:n, i % 2, :], scalar=1.0,
                                         in1=kraw[0:n, i % 2, :], op0=ALU.min, op1=ALU.add).then_inc(k_ready, 1)

            for i, (k0, n) in enumerate(keys):
                dve.wait_ge(kv_in_psum, i + 1)
                if i >= 2:
                    dve.wait_ge(kv_added, i - 1)
                    dve.wait_ge(ksq_ready, i - 1)
                dve.tensor_tensor(kraw[0:n, i % 2, :], ps[0:n, 2 + i % 2, 0:D], bk[0:n, :], ALU.add)\
                    .then_inc(kraw_ready, 1)
                dve.tensor_tensor(v[0:n, i % 2, :], ps[0:n, 2 + i % 2, D:2 * D], bv[0:n, :], ALU.add)\
                    .then_inc(v_ready, 1)
                elu(i, n)
                if i >= 2:
                    next(norming, None)
            exhaust(norming)
            for f in range(FT):
                dve.wait_ge(qexp_ready, f + 1)
                steps.mark(dve.tensor_scalar(qraw[:, f, :], qraw[:, f, :], 0.0, -1.0, ALU.max, ALU.add))
                steps.settle()
                dve.scalar_tensor_tensor(out=q[:, f, :], in0=qexp[:, f, :], scalar=1.0, in1=qraw[:, f, :],
                                         op0=ALU.min, op1=ALU.add).then_inc(q_ready, 1)
            dve.wait_ge(kv_added, len(keys))
            for f in range(FT):
                dve.tensor_copy(knorm[:, f:f + 1], ps[:, f, 0:1]).then_inc(ksum_copied, 1)
            dve.wait_ge(kinv_ready, 1)
            for f in range(FT):
                dve.scalar_tensor_tensor(out=kv[:, f, :], in0=ps[:, 4 + f, 0:P], scalar=kinv[:, f:f + 1],
                                         in1=blocks[:, :], op0=ALU.mult, op1=ALU.mult).then_inc(kv_ready, 1)
            for f in range(FT):
                dve.wait_ge(qinv_ready, f + 1)
                dve.tensor_tensor(qn[:, f, :], q[:, f, :], qsq[:, f, :], ALU.mult).then_inc(qn_ready, 1)
            proj.vector(dve, steps)

        pipelined_loop(nc, st,
                       {"sync": prologue_sync, "tensor": nothing, "scalar": nothing, "vector": nothing,
                        "gpsimd": nothing},
                       {"sync": sync, "tensor": tensor, "scalar": scalar, "vector": vector,
                        "gpsimd": lambda pool, b, side: None})



class Rotary:

    def __init__(self, st, ps, split, bank7, cos, sin):
        self.ps, self.split, self.bank7, self.cos, self.sin = ps, split, bank7, cos, sin
        self.part = st.sb("rot_part", [P, S])
        self.in_psum = st.sem("rot_in_psum")
        self.taken = st.sem("rot_taken")

    def hand_over(self, product, n):
        product.then_inc(self.in_psum, 1)
        self.bank7.freed_by(self.taken, n + 1)

    def vector_a(self, dve, steps, i, scale):
        dve.wait_ge(self.in_psum, 2 * i + 1)
        steps.settle()
        dve.scalar_tensor_tensor(out=self.split.full[i % 2][:, :], in0=self.ps[:, 7, :], scalar=scale,
                                 in1=self.cos[:, :], op0=ALU.mult, op1=ALU.mult).then_inc(self.taken, 1)

    def vector_b(self, dve, steps, i, scale):
        full = self.split.full[i % 2][:, :]
        dve.wait_ge(self.in_psum, 2 * i + 2)
        dve.scalar_tensor_tensor(out=self.part[:, :], in0=self.ps[:, 7, :], scalar=scale,
                                 in1=self.sin[:, :], op0=ALU.mult, op1=ALU.mult).then_inc(self.taken, 1)
        dve.wait_ge(self.taken, 2 * i + 2)
        steps.mark(dve.tensor_tensor(full, full, self.part[:, :], ALU.add))
        steps.settle()



def rotary_latent_attention(nc, w, x_src, x_dst, kscratch, qscratch):
    with ExitStack() as ctx:
        st = Stage(nc, ctx, "s6")
        ps = st.psum()
        loads = []
        identf = constant(st, loads, "identf", w["identf"])
        identb = constant(st, loads, "identb", w["identb"], BF16)
        tri = constant(st, loads, "tri", w["tri"], BF16)
        triT = constant(st, loads, "triT", w["triT"], BF16)
        cos = constant(st, loads, "cos", w["mla_cos"])
        sin = constant(st, loads, "sin", w["mla_sin"])
        w_ln = column(st, loads, "w_ln", w["L1_ffn_w_ln1"])
        wkvd = weight(st, loads, "wkvd", w["L1_ffn_W_kvd"])
        wqd = weight(st, loads, "wqd", w["L1_ffn_W_qd"])
        wku = weight(st, loads, "wku", w["mla_wku"])
        wkr = weight(st, loads, "wkr", w["mla_wkr"])
        wkr_p = weight(st, loads, "wkr_p", w["mla_wkr_partner"])
        wq = weight(st, loads, "wq", w["mla_wq"])
        wq_p = weight(st, loads, "wq_p", w["mla_wq_partner"])
        wvu = weight(st, loads, "wvu", w["L1_ffn_W_vu"])
        wo = weight(st, loads, "wo", w["L1_ffn_W_o"])
        x = st.sb("x", [P, T, D])
        residual = st.sb("residual", [P, T, D])
        kv_latent, q_latent = st.sb("kv_latent", [64, S]), st.sb("q_latent", [64, S])
        bank7 = SharedBank(7)
        norm = Norm(st, ps, x, identf, rms=True, weight=w_ln, shared=bank7)
        split = Split(st, S, 4)
        rotary = Rotary(st, ps, split, bank7, cos, sin)
        att = Attention(st, ps, identf, identb, st.sb("otok", [P, T, D]), S, NG, causal=True, bank7=bank7,
                        own=2, lead=7, side=1 + Norm.OUTER_STEPS + Norm.STEPS + 2 + 8 + 2, preloaded=2)
        proj = OutProjection(st, ps, identf, att.otok, st.sb("oF", [P, FT, S]), wo, residual)
        latent_in_psum, latent_ready = st.sem("latent_in_psum"), st.sem("latent_ready")
        v_in_psum, kept = st.sem("v_in_psum"), st.sem("kept")
        dve_steps, act_steps, stored = st.sem("dve_steps"), st.sem("act_steps"), st.sem("stored")
        side_dve_steps = st.sem("side_dve_steps")
        load_constants(nc, st, loads, att)
        att.own_ready = (att.v_ready, 2)

        def prologue_sync(sp, b, first):
            if not first:
                sp.wait_ge(kept, 1)
            load_x(sp, norm, x, x_src, b)
            yield from skip(1 + Norm.OUTER_STEPS + Norm.STEPS + 2)
            for i, (f, is_q) in enumerate(ITEMS):
                yield
                split.sync(sp, i, S, (qscratch if is_q else kscratch)[b], (8 * f, 8 * f + 8),
                           Q_LAYOUT if is_q else K_LAYOUT)
                yield
                if i == 1:
                    split.wait_in_dram(sp, (0, 1))
                    att.preload(sp, 0, kscratch[b], qscratch[b], S, first)
                    yield
            for g in range(1, att.preloaded):
                att.preload(sp, g, kscratch[b], qscratch[b], S, first)
            yield
            split.wait_in_dram(sp, (2, 3))
            sp.wait_ge(att.stack0_preloaded, 32)
            sp.wait_ge(att.stacks_preloaded, 32 * (att.preloaded - 1))

        def prologue_tensor(pe, b, first):
            xnT = norm.xnT[:, :, 1:]
            yield from skip(1 + Norm.OUTER_STEPS)
            yield from norm.tensor(pe)
            pe.wait_ge(norm.xnT_ready, FT)
            for n, wt in enumerate((wkvd, wqd)):
                bank7.take(pe)
                for c in range(FT):
                    mm = pe.matmul(ps[0:64, 7, :], wt[:, c, :], xnT[:, c, :], start=(c == 0), stop=(c == 1))
                mm.then_inc(latent_in_psum, 1)
                bank7.freed_by(latent_ready, n + 1)
                yield
            for i, (f, is_q) in enumerate(ITEMS):
                cols = slice(f * P, (f + 1) * P)
                bank7.take(pe)
                if is_q:
                    pe.wait_ge(latent_ready, 2)
                    mm = pe.matmul(ps[:, 7, :], wq[:, cols], q_latent[:, :], start=True, stop=True)
                else:
                    pe.matmul(ps[:, 7, :], wku[:, cols], kv_latent[:, :], start=True, stop=False)
                    for c in range(FT):
                        mm = pe.matmul(ps[:, 7, :], wkr[:, c, cols], xnT[:, c, :], start=False, stop=(c == 1))
                rotary.hand_over(mm, 2 * i)
                yield
                bank7.take(pe)
                if is_q:
                    mm = pe.matmul(ps[:, 7, :], wq_p[:, cols], q_latent[:, :], start=True, stop=True)
                else:
                    for c in range(FT):
                        mm = pe.matmul(ps[:, 7, :], wkr_p[:, c, cols], xnT[:, c, :], start=(c == 0), stop=(c == 1))
                rotary.hand_over(mm, 2 * i + 1)
                yield
                if i == 1:
                    yield
            yield

        def prologue_scalar(act, b, first):
            steps = Steps(act, act_steps)
            if first:
                act.preload_act_table_set(EXP_AND_LN)
            yield
            yield from norm.outer_scalar(act, steps)
            yield from norm.scalar(act, steps)
            for n, dst in enumerate((kv_latent, q_latent)):
                act.wait_ge(latent_in_psum, n + 1)
                act.activation(dst[:, :], ps[0:64, 7, :], ACT.Copy).then_inc(latent_ready, 1)
                yield
            for i in range(4):
                yield
                split.scalar(act, i, S)
                yield
                if i == 1:
                    yield
            yield

        def prologue_vector(dve, b, first):
            steps = Steps(dve, side_dve_steps)
            yield
            yield from norm.outer_vector(dve, steps)
            yield from norm.vector(dve, steps)
            yield from skip(2)
            for i, (f, is_q) in enumerate(ITEMS):
                scale = HD ** -0.5 if is_q else 1.0
                rotary.vector_a(dve, steps, i, scale)
                yield
                rotary.vector_b(dve, steps, i, scale)
                dve.sem_inc(split.full_ready, 1)
                split.vector(dve, steps, i, S)
                yield
                if i == 1:
                    yield
            yield

        def v_tensor(pe):
            for t in range(T):
                mm = pe.matmul(ps[:, t // 2, (t % 2) * D:(t % 2 + 1) * D], kv_latent[:, t * P:(t + 1) * P],
                               wvu[:, :], start=True, stop=True)
                if t % 2:
                    mm.then_inc(v_in_psum, 1)
                    yield

        def v_scalar(act):
            for n in range(2):
                act.wait_ge(v_in_psum, n + 1)
                act.activation(att.v[:, 2 * n:2 * n + 2, :, 0:HD], v_heads(ps[:, n, :]), ACT.Copy)\
                    .then_inc(att.v_ready, 1)
                yield

        def sync(sp, b, side):
            order = att.plan(kind(side))
            side = side()
            for g in range(att.preloaded, NG):
                att.load_stacks(sp, g, kscratch[b], qscratch[b], S)
            att.sync(sp, order, side=side)
            store_x(sp, proj.x_done, 2, stored, residual, x_dst, b)
            exhaust(side)

        def tensor(pe, b, side):
            att.tensor(pe, att.plan(kind(side)), tri=tri, triT=triT, own=v_tensor(pe), side=side())
            proj.tensor(pe)

        def scalar(act, b, side):
            act.preload_act_table_set(EXP_AND_LN)
            att.scalar(act, att.plan(kind(side)), own=v_scalar(act), side=side())
            proj.scalar(act)

        def vector(dve, b, side):
            steps = Steps(dve, dve_steps)
            att.vector(dve, att.plan(kind(side)), steps, side=side())
            dve.wait_ge(att.o_divided, NG)
            dve.sem_inc(proj.o_ready, 1)
            dve.wait_ge(kept, 1)
            proj.vector(dve, steps)

        def gpsimd(pool, b, side):
            keep_residual(nc, pool, residual, x, kept)

        pipelined_loop(nc, st,
                       {"sync": prologue_sync, "tensor": prologue_tensor, "scalar": prologue_scalar,
                        "vector": prologue_vector, "gpsimd": lambda pool, b, first: skip(0)},
                       {"sync": sync, "tensor": tensor, "scalar": scalar, "vector": vector, "gpsimd": gpsimd},
                       first_maxima(att, dve_steps, tri=tri))



class Hyperbolic:

    ROWS = STACK + NSLOT
    SIDE = (1, 0)

    def __init__(self, st, ps, identf, trif, att, root_c, eps_c):
        self.ps, self.identf, self.trif, self.att, self.root_c, self.eps_c = ps, identf, trif, att, root_c, eps_c
        self.off = [0, P, 3 * P, 6 * P]
        self.place = [(0, 0), (2, 0), (0, P), (1, 0)]
        self.cols = 10 * P
        self.kst = st.sb("hyp_k", [self.ROWS, GH, S], BF16)
        self.qst = st.sb("hyp_q", [self.ROWS, GH, S], BF16)
        self.u = st.sb("hyp_u", [P, 2, self.cols])
        self.root = st.sb("hyp_root", [P, 2, self.cols])
        self.nmax = st.sb("hyp_nmax", [P, 2, T])
        self.bias = st.sb("hyp_bias", [P, 2, T])
        self.pT = st.sb("hyp_pT", [P, 2, T, S])
        self.oT = st.sb("hyp_oT", [P, S])
        self.inv = st.sb("hyp_inv", [P, T, GH])
        self.loaded = st.sem("hyp_loaded")
        self.scored = st.sem("hyp_scored")
        self.u_ready = st.sem("hyp_u_ready")
        self.square_ready = st.sem("hyp_square_ready")
        self.root_ready = st.sem("hyp_root_ready")
        self.sum_ready = st.sem("hyp_sum_ready")
        self.score_ready = st.sem("hyp_score_ready")
        self.bias_ready = st.sem("hyp_bias_ready")
        self.probs_ready = st.sem("hyp_probs_ready")
        self.turned = st.sem("hyp_turned")
        self.pT_ready = st.sem("hyp_pT_ready")
        self.pv_done = st.sem("hyp_pv_done")
        self.oT_copied, self.o_turned = st.sem("hyp_oT_copied"), st.sem("hyp_o_turned")
        self.o_divided = st.sem("hyp_o_divided")

    @staticmethod
    def turned_place(k):
        return ((4, 0), (5, 0), (6, 0), (5, 3 * P))[k]

    def beside(self, side, half):
        for _ in range(self.SIDE[half]):
            next(side, None)

    def tensor(self, pe, side):
        ps = self.ps

        def score(j):
            if j == 0:
                pe.wait_ge(self.loaded, 64)
            for t in range(T):
                if j >= 1:
                    pe.wait_ge(self.u_ready, T * j)
                n = (t + 1) * P
                bank, c0 = self.place[t]
                pe.matmul(ps[:, bank, c0:c0 + n], self.qst[:, j, t * P:n], self.kst[:, j, 0:n], start=True, stop=True)\
                    .then_inc(self.scored, 1)

        def turn(j):
            pe.wait_ge(self.probs_ready, T * (j + 1))
            if j >= 1:
                pe.wait_ge(self.pT_ready, T * j)
            for k in range(T):
                bank, c0 = self.turned_place(k)
                for t in range(k, T):
                    mm = pe.transpose(ps[:, bank, c0 + (t - k) * P:c0 + (t - k + 1) * P],
                                      self.u[:, j % 2, self.off[t] + k * P:self.off[t] + (k + 1) * P],
                                      self.identf[:, :])
                mm.then_inc(self.turned, 1)

        def pv(j):
            for k in range(T):
                pe.wait_ge(self.pT_ready, T * j + k + 1)
                mm = pe.matmul(ps[VW * j:VW * (j + 1), 3, k * P:S], self.att.v[:, k, H - GH + j, :],
                               self.pT[:, j % 2, k, k * P:S], start=(k == 0), stop=(k == T - 1))
            mm.then_inc(self.pv_done, 1)

        score(0)
        for j in range(GH):
            self.beside(side, 0)
            if j + 1 < GH:
                score(j + 1)
            self.beside(side, 1)
            turn(j)
            if j >= 1:
                pv(j - 1)
        pv(GH - 1)
        pe.wait_ge(self.oT_copied, 1)
        for t in range(T):
            mm = pe.transpose(ps[:, 0, t * P:(t + 1) * P], self.oT[:, t * P:(t + 1) * P], self.identf[:, :])
        mm.then_inc(self.o_turned, 1)

    def vector(self, dve, steps, side):
        ps = self.ps

        def excess(j):
            u = self.u[:, j % 2, :]
            for t in range(T):
                dve.wait_ge(self.scored, T * j + max(t + 1, T - 1))
                if j >= 2 and t == 0:
                    dve.wait_ge(self.turned, T * (j - 1))
                dve.tensor_scalar(u[:, self.off[t]:self.off[t] + (t + 1) * P],
                                  ps[:, self.place[t][0], self.place[t][1]:self.place[t][1] + (t + 1) * P],
                                  -1.0, TINY, ALU.add, ALU.max).then_inc(self.u_ready, 1)
            dve.wait_ge(self.u_ready, T * (j + 1))
            dve.scalar_tensor_tensor(out=self.root[:, j % 2, :], in0=u, scalar=2.0, in1=u, op0=ALU.add,
                                     op1=ALU.mult).then_inc(self.square_ready, 1)

        def add_root(j):
            dve.wait_ge(self.root_ready, j + 1)
            u = self.u[:, j % 2, :]
            dve.tensor_tensor(u, u, self.root[:, j % 2, :], ALU.add).then_inc(self.sum_ready, 1)

        def maxima(j):
            dve.wait_ge(self.score_ready, j + 1)
            for t in range(T):
                own = self.u[:, j % 2, self.off[t] + t * P:self.off[t] + (t + 1) * P]
                steps.mark(dve.tensor_tensor(own, own, self.trif[:, :], ALU.add))
            steps.settle()
            for t in range(T):
                steps.mark(dve.tensor_reduce(self.nmax[:, j % 2, t:t + 1],
                                             self.u[:, j % 2, self.off[t]:self.off[t] + (t + 1) * P], AX.X,
                                             ALU.max, negate=True))
            steps.settle()
            dve.tensor_scalar(self.bias[:, j % 2, :], self.nmax[:, j % 2, :], self.root_c[:, j:j + 1], None,
                              ALU.mult).then_inc(self.bias_ready, 1)

        excess(0)
        for j in range(GH):
            self.beside(side, 0)
            add_root(j)
            if j + 1 < GH:
                excess(j + 1)
            self.beside(side, 1)
            maxima(j)
        dve.wait_ge(self.o_turned, 1)
        o = ps[:, 0, :].rearrange("p (t j w) -> p t j w", t=T, j=GH)
        steps.mark(dve.reciprocal(self.inv[:, :, :], o[:, :, :, HD]))
        steps.settle()
        out = self.att.otok[:, :, D - GH * HD:D].rearrange("p t (j d) -> p t j d", j=GH)
        inv = self.inv[:, :, :].rearrange("p t (j o) -> p t j o", o=1).to_broadcast([P, T, GH, HD])
        dve.tensor_tensor(out, o[:, :, :, 0:HD], inv, ALU.mult).then_inc(self.o_divided, 1)

    def scalar(self, act, steps, side):
        def root(j):
            r = self.root[:, j % 2, :]
            act.wait_ge(self.square_ready, j + 1)
            steps.mark(act.activation(r, r, ACT.Ln))
            steps.settle()
            act.activation(r, r, ACT.Exp, scale=0.5).then_inc(self.root_ready, 1)

        def score(j):
            u = self.u[:, j % 2, :]
            act.wait_ge(self.sum_ready, j + 1)
            steps.mark(act.activation(u, u, ACT.Ln, bias=1.0))
            steps.settle()
            steps.mark(act.activation(u, u, ACT.Ln, bias=self.eps_c[:, j:j + 1]))
            steps.settle()
            act.activation(u, u, ACT.Exp, scale=-1.0).then_inc(self.score_ready, 1)

        def probs(j):
            act.wait_ge(self.bias_ready, j + 1)
            for t in range(T):
                u = self.u[:, j % 2, self.off[t]:self.off[t] + (t + 1) * P]
                act.activation(u, u, ACT.Exp, bias=self.bias[:, j % 2, t:t + 1],
                               scale=self.root_c[:, j:j + 1]).then_inc(self.probs_ready, 1)

        def copy(j):
            for k in range(T):
                act.wait_ge(self.turned, T * j + 1 if k == 0 else T * (j + 1))
                if j >= 2 and k == 0:
                    act.wait_ge(self.pv_done, j - 1)
                bank, c0 = self.turned_place(k)
                act.activation(self.pT[:, j % 2, k, k * P:S], self.ps[:, bank, c0:c0 + S - k * P], ACT.Copy)\
                    .then_inc(self.pT_ready, 1)

        root(0)
        for j in range(GH):
            self.beside(side, 0)
            score(j)
            if j + 1 < GH:
                root(j + 1)
            self.beside(side, 1)
            probs(j)
            copy(j)
        act.wait_ge(self.pv_done, GH)
        act.activation(self.oT[:, :], self.ps[:, 3, :], ACT.Copy).then_inc(self.oT_copied, 1)


def mixed_attention(nc, w, x_src, x_dst, kscratch, qscratch, tscratch):
    with ExitStack() as ctx:
        st = Stage(nc, ctx, "s4")
        ps = st.psum()
        loads = []
        identf = constant(st, loads, "identf", w["identf"])
        identb = constant(st, loads, "identb", w["identb"], BF16)
        tri = constant(st, loads, "tri", w["tri"], BF16)
        triT = constant(st, loads, "triT", w["triT"], BF16)
        trif = constant(st, loads, "trif", w["trif"])
        blocks = constant(st, loads, "blocks", w["blocks"])
        cos = constant(st, loads, "cos", w["rot_cos"])
        sin = constant(st, loads, "sin", w["rot_sin"])
        wts = {n: weight(st, loads, n, w[f"mix_{n}"]) for n in ("wq", "wk", "wq_partner", "wk_partner", "wv")}
        wo = weight(st, loads, "wo", w["mix_wo"])
        bo = bias_row(st, loads, "bo", w["L1_attn_proj_b"])
        c_feature = st.sb("c_feature", [P, 1])
        loads.append((c_feature[:, :], w["curvature_feature"]))
        c_head = st.sb("c_head", [P, GH])
        loads.append((c_head[:, :], w["curvature"].rearrange("(o h) -> o h", o=1).to_broadcast([P, GH])))
        neg_c, inv_c = st.sb("neg_c", [P, 1]), st.sb("inv_c", [P, 1])
        root_c, eps_c = st.sb("root_c", [P, GH]), st.sb("eps_c", [P, GH])
        x = st.sb("x", [P, T, D])
        residual = st.sb("residual", [P, T, D])
        bank7 = SharedBank(7)
        norm = Norm(st, ps, x, identf, shared=bank7)
        split = Split(st, S, 4)
        rotary = Rotary(st, ps, split, bank7, cos, sin)
        att = Attention(st, ps, identf, identb, st.sb("otok", [P, T, D]), S, 3, causal=True, bank7=bank7,
                        own=2, side=1 + Norm.STEPS + 4 * 4 + 2 - GH * sum(Hyperbolic.SIDE), preloaded=2,
                        side_until=0.85, lead=7, nexts_from=2.3)
        hyp = Hyperbolic(st, ps, identf, trif, att, root_c, eps_c)
        proj = OutProjection(st, ps, identf, att.otok, st.sb("oF", [P, FT, S]), wo, residual, bias=bo)
        square = st.sb("square", [P, S])
        sums = st.sb("sums", [P, 2, S])
        t_full = st.sb("t_full", [P, S])
        t_level = st.sb("t_level", [P, 2, 3, S], BF16)
        rotated, squared, summed = st.sem("rotated"), st.sem("squared"), st.sem("summed")
        sums_ready, factor_ready = st.sem("sums_ready"), st.sem("factor_ready")
        t_levels_ready, t_in_dram = st.sem("t_levels_ready"), st.sem("t_in_dram")
        v_in_psum, kept, setup = st.sem("v_in_psum"), st.sem("kept"), st.sem("setup")
        dve_steps, act_steps, stored = st.sem("dve_steps"), st.sem("act_steps"), st.sem("stored")
        side_dve_steps, side_act_steps = st.sem("side_dve_steps"), st.sem("side_act_steps")
        load_constants(nc, st, loads, att)
        att.own_ready = (att.v_ready, 2)
        with nc.Block() as block:
            @block.vector
            def _(dve):
                dve.tensor_scalar(neg_c[:, :], c_feature[:, :], -1.0, None, ALU.mult)
                dve.reciprocal(inv_c[:, :], c_feature[:, :])
                dve.wait_ge(setup, 2)
                dve.tensor_scalar(eps_c[:, :], root_c[:, :], 1e-6, None, ALU.mult)

            @block.scalar
            def _(act):
                act.activation(root_c[:, :], c_head[:, :], ACT.Ln).then_inc(setup, 1)
                act.wait_ge(setup, 1)
                act.activation(root_c[:, :], root_c[:, :], ACT.Exp, scale=0.5).then_inc(setup, 1)

        hyp_rows = slice(64, P)
        cos_rows = (slice(96, P), slice(0, 64))

        def prologue_sync(sp, b, first):
            if not first:
                sp.wait_ge(kept, 1)
            load_x(sp, norm, x, x_src, b)
            yield from skip(1 + Norm.STEPS)
            for i, (f, is_q) in enumerate(ITEMS):
                yield from skip(3)
                split.sync(sp, i, S, (qscratch if is_q else kscratch)[b], (8 * f, 8 * f + 8),
                           Q_LAYOUT if is_q else K_LAYOUT)
                if f == 1:
                    n = 1 if is_q else 0
                    sp.wait_ge(t_levels_ready, n + 1)
                    for slot, count, lev, step in (K_LAYOUT, Q_LAYOUT)[n]:
                        if step:
                            src = t_level[64:P:HD, n, lev:lev + count, :]
                        else:
                            src = t_level[64:P:HD, n, lev, :].rearrange("p (o w) -> p o w", o=1)\
                                .to_broadcast([GH, count, S])
                        sp.dma_start(tscratch[b, n, :, slot:slot + count, :], src).then_inc(t_in_dram, 16)
                yield
                if i == 1:
                    split.wait_in_dram(sp, (0, 1))
                    att.preload(sp, 0, kscratch[b], qscratch[b], S, first)
                    yield
            for g in range(1, att.preloaded):
                att.preload(sp, g, kscratch[b], qscratch[b], S, first)
            yield
            split.wait_in_dram(sp, (2, 3))
            sp.wait_ge(t_in_dram, 2 * 16 * len(K_LAYOUT))
            sp.wait_ge(att.stack0_preloaded, 32)
            sp.wait_ge(att.stacks_preloaded, 32 * (att.preloaded - 1))

        def prologue_tensor(pe, b, first):
            xnT = norm.xnT[:, :, 1:]
            yield
            yield from norm.tensor(pe)
            pe.wait_ge(norm.xnT_ready, FT)
            for i, (f, is_q) in enumerate(ITEMS):
                for half, name in enumerate(("wq", "wq_partner") if is_q else ("wk", "wk_partner")):
                    bank7.take(pe)
                    for c in range(FT):
                        mm = pe.matmul(ps[:, 7, :], wts[name][:, c, f * P:(f + 1) * P], xnT[:, c, :],
                                       start=(c == 0), stop=(c == 1))
                    rotary.hand_over(mm, 2 * i + half)
                    yield
                bank7.take(pe)
                pe.wait_ge(squared, i + 1)
                pe.matmul(ps[:, 7, :], blocks[:, :], square[:, :], start=True, stop=True).then_inc(summed, 1)
                bank7.freed_by(sums_ready, i + 1)
                yield
                yield
                if i == 1:
                    yield
            yield

        def prologue_scalar(act, b, first):
            steps = Steps(act, side_act_steps)
            if first:
                act.preload_act_table_set(EXP_AND_LN)
            yield
            yield from norm.scalar(act, steps)
            for i, (f, is_q) in enumerate(ITEMS):
                yield
                act.wait_ge(rotated, i + 1)
                if i >= 1:
                    act.wait_ge(summed, i)
                act.activation(square[:, :], split.full[i % 2][:, :], ACT.Square).then_inc(squared, 1)
                yield
                act.wait_ge(sums_ready, i + 1)
                rows = cos_rows[f]
                steps.mark(act.activation(sums[rows, i % 2, :], sums[rows, i % 2, :], ACT.Ln, scale=2.0 ** 24))
                steps.settle()
                last = act.activation(sums[rows, i % 2, :], sums[rows, i % 2, :], ACT.Exp, scale=-0.5)
                if f == 1:
                    steps.mark(last)
                    steps.mark(act.activation(sums[hyp_rows, i % 2, :], sums[hyp_rows, i % 2, :], ACT.Ln,
                                              bias=inv_c[hyp_rows, :]))
                    steps.settle()
                    if is_q:
                        act.wait_ge(t_levels_ready, 1)
                    last = act.activation(t_full[hyp_rows, :], sums[hyp_rows, i % 2, :], ACT.Exp, scale=0.5)
                last.then_inc(factor_ready, 1)
                yield
                split.scalar(act, i, S)
                yield
                if i == 1:
                    yield
            yield

        def prologue_vector(dve, b, first):
            steps = Steps(dve, side_dve_steps)
            yield
            yield from norm.vector(dve, steps)
            for i, (f, is_q) in enumerate(ITEMS):
                full = split.full[i % 2][:, :]
                rotary.vector_a(dve, steps, i, 1.0)
                yield
                rotary.vector_b(dve, steps, i, 1.0)
                dve.sem_inc(rotated, 1)
                yield
                dve.wait_ge(summed, i + 1)
                dve.tensor_scalar(sums[:, i % 2, :], ps[:, 7, :], 1e-24, None, ALU.max).then_inc(sums_ready, 1)
                yield
                dve.wait_ge(factor_ready, i + 1)
                rows = cos_rows[f]
                scale = 4.0 if is_q else 1.0
                steps.mark(dve.scalar_tensor_tensor(out=full[rows, :], in0=full[rows, :], scalar=scale * 2.0 ** 12,
                                                    in1=sums[rows, i % 2, :], op0=ALU.mult, op1=ALU.mult))
                if is_q:
                    if f == 0:
                        steps.mark(dve.tensor_scalar(full[0:96, :], full[0:96, :], HD ** -0.5, None, ALU.mult))
                    else:
                        steps.mark(dve.tensor_scalar(full[hyp_rows, :], full[hyp_rows, :], neg_c[hyp_rows, :], None,
                                                     ALU.mult))
                        steps.mark(dve.tensor_scalar(t_full[hyp_rows, :], t_full[hyp_rows, :],
                                                     c_feature[hyp_rows, :], None, ALU.mult))
                steps.settle()
                dve.sem_inc(split.full_ready, 1)
                split.vector(dve, steps, i, S)
                if f == 1:
                    n = 1 if is_q else 0
                    tf, tl = t_full[hyp_rows, :], t_level[hyp_rows, n]
                    for lev in range(3):
                        steps.mark(dve.tensor_copy(tl[:, lev, :], tf))
                        steps.settle()
                        if lev < 2:
                            steps.mark(dve.tensor_tensor(tf, tf, tl[:, lev, :], ALU.subtract))
                            steps.settle()
                    dve.sem_inc(t_levels_ready, 1)
                yield
                if i == 1:
                    yield
            yield

        def v_tensor(pe):
            for t in range(T):
                for c in range(FT):
                    mm = pe.matmul(ps[:, t // 2, (t % 2) * D:(t % 2 + 1) * D],
                                   norm.xnT[:, c, 1 + t * P:1 + (t + 1) * P], wts["wv"][:, c, :],
                                   start=(c == 0), stop=(c == 1))
                if t % 2:
                    mm.then_inc(v_in_psum, 1)
                    yield

        def v_scalar(act):
            for n in range(2):
                act.wait_ge(v_in_psum, n + 1)
                act.activation(att.v[:, 2 * n:2 * n + 2, :, 0:HD], v_heads(ps[:, n, :]), ACT.Copy)\
                    .then_inc(att.v_ready, 1)
                yield

        def sync(sp, b, side):
            order = att.plan(kind(side))
            side = side()
            att.load_stacks(sp, 2, kscratch[b], qscratch[b], S)
            heads = slice(H - GH, H)
            for n, (dst, src) in enumerate(((hyp.kst, kscratch[b]), (hyp.qst, qscratch[b]))):
                sp.dma_start(dst[0:STACK, :, :], src[heads, :, :, 0:S].rearrange("h d s w -> (d s) h w"))\
                    .then_inc(hyp.loaded, 16)
                sp.dma_start(dst[STACK:STACK + NSLOT, :, :], tscratch[b, n].rearrange("h s w -> s h w"))\
                    .then_inc(hyp.loaded, 16)
            att.sync(sp, order, side=side)
            exhaust(side)
            store_x(sp, proj.x_done, 2, stored, residual, x_dst, b)

        def tensor(pe, b, side):
            order = att.plan(kind(side))
            side = side()
            att.tensor(pe, order, tri=tri, triT=triT, own=v_tensor(pe), side=side)
            pe.wait_ge(att.exped, 2 * T * 3)
            pe.wait_ge(att.max_taken, sum(item[0] == "max" for item in order))
            pe.wait_ge(att.oT_copied, 3)
            hyp.tensor(pe, side)
            proj.tensor(pe)

        def scalar(act, b, side):
            act.preload_act_table_set(EXP_AND_LN)
            order = att.plan(kind(side))
            side = side()
            att.scalar(act, order, own=v_scalar(act), side=side)
            hyp.scalar(act, Steps(act, act_steps), side)
            proj.scalar(act)

        def vector(dve, b, side):
            steps = Steps(dve, dve_steps)
            order = att.plan(kind(side))
            side = side()
            att.vector(dve, order, steps, side=side)
            hyp.vector(dve, steps, side)
            dve.wait_ge(att.o_divided, 3)
            dve.wait_ge(hyp.o_divided, 1)
            dve.sem_inc(proj.o_ready, 1)
            dve.wait_ge(kept, 1)
            proj.vector(dve, steps)

        def gpsimd(pool, b, side):
            keep_residual(nc, pool, residual, x, kept)

        pipelined_loop(nc, st,
                       {"sync": prologue_sync, "tensor": prologue_tensor, "scalar": prologue_scalar,
                        "vector": prologue_vector, "gpsimd": lambda pool, b, first: skip(0)},
                       {"sync": sync, "tensor": tensor, "scalar": scalar, "vector": vector, "gpsimd": gpsimd},
                       first_maxima(att, dve_steps, tri=tri))



NE = 7


def experts(nc, w, y_src, x_src, x_dst):
    with ExitStack() as ctx:
        st = Stage(nc, ctx, "s7")
        ps = st.psum()
        loads = []
        identf = constant(st, loads, "identf", w["identf"])
        number = st.sb("number", [P, NE + 1])
        loads.append((number[:, :], w["numbers"].rearrange("(o n) -> o n", o=1).to_broadcast([P, NE + 1])))
        w_ln = column(st, loads, "w_ln", w["L1_ffn_w_ln2"])
        wr = weight(st, loads, "wr", w["L1_ffn_W_router"])
        br = st.sb("br", [P, NE])
        loads.append((br[:, :], w["L1_ffn_routing_bias"].rearrange("(o n) -> o n", o=1).to_broadcast([P, NE])))
        wg, wu, wd = (st.sb(n, [P, NE + 1, FT, D]) for n in ("wg", "wu", "wd"))
        weights = []
        for tile, name in ((wg, "Wg"), (wu, "Wu"), (wd, "Wd")):
            weights.append((tile[:, 0, :, :], w[f"L1_ffn_{name}_s"].rearrange("(f p) n -> p f n", p=P)))
            for e in range(NE):
                weights.append((tile[:, 1 + e, :, :], w[f"L1_ffn_{name}_r"][e].rearrange("(f p) n -> p f n", p=P)))
        y, total = st.sb("y", [P, T, D]), st.sb("total", [P, T, D])
        residual = st.sb("residual", [P, T, D])
        bank7 = SharedBank(7)
        norm = Norm(st, ps, y, identf, rms=True, weight=w_ln, shared=bank7)
        xnT = st.sb("xnT_now", [P, FT, S])
        logit, odds = st.sb("logit", [P, T, NE]), st.sb("odds", [P, T, NE])
        prob = st.sb("prob", [P, T, NE + 1])
        top, where = st.sb("top", [P, T, 8]), st.sb("where", [P, T, 8], U32)
        wheref = st.sb("wheref", [P, T, 2])
        picked, both = st.sb("picked", [P, T, NE + 1]), st.sb("both", [P, T])
        share = st.sb("share", [P, T, NE + 1])
        share_next = st.sb("share_next", [P, T, NE + 1])
        gate, gated = st.sb("gate", [P, 2, S]), st.sb("gated", [P, 2, S])
        mid = st.sb("mid", [P, 2, FT, S])
        xnT_kept, total_kept, share_kept = st.sem("xnT_kept"), st.sem("total_kept"), st.sem("share_kept")
        logit_in_psum, logit_ready, odds_ready = st.sem("logit_in_psum"), st.sem("logit_ready"), st.sem("odds_ready")
        up_in_psum, gate_ready, gated_ready = st.sem("up_in_psum"), st.sem("gate_ready"), st.sem("gated_ready")
        mid_ready, down_in_psum, down_added = st.sem("mid_ready"), st.sem("down_in_psum"), st.sem("down_added")
        residual_loaded, weights_loaded = st.sem("residual_loaded"), st.sem("weights_loaded")
        side_dve_steps = st.sem("side_dve_steps")
        dve_steps, act_steps, stored = st.sem("dve_steps"), st.sem("act_steps"), st.sem("stored")
        load_constants(nc, st, loads)
        with nc.Block() as block:
            @block.vector
            def _(dve):
                dve.memset(prob[:, :, NE:NE + 1], -1.0)
        order = []
        for e in range(NE + 1):
            order += [("up", e, 0), ("up", e, 1)] + ([("down", e - 1)] if e else [])
        order.append(("down", NE))

        def down_bank(e, t):
            return 4 + (T * e + t) % 3

        SIDE = 1 + Norm.STEPS + 3
        side_at = {3 * n: n for n in range(SIDE - 1)}

        def prologue_sync(sp, b, first):
            if not first:
                sp.wait_ge(xnT_kept, 1)
                sp.wait_ge(total_kept, 1)
            load_x(sp, norm, y, y_src, b)
            sp.dma_start(residual[:, :, :], x_src[b].rearrange("(t p) d -> p t d", p=P))\
                .then_inc(residual_loaded, 16)
            if first:
                for tile, src in weights:
                    sp.dma_start(tile, src).then_inc(weights_loaded, 16)
            yield from skip(SIDE)
            if first:
                sp.wait_ge(weights_loaded, 16 * len(weights))

        def prologue_tensor(pe, b, first):
            if not first:
                pe.wait_ge(xnT_kept, 1)
            yield
            yield from norm.tensor(pe)
            pe.wait_ge(norm.xnT_ready, FT)
            bank7.take(pe)
            for t in range(T):
                for c in range(FT):
                    mm = pe.matmul(ps[:, 7, t * NE:(t + 1) * NE], norm.xnT[:, c, 1 + t * P:1 + (t + 1) * P],
                                   wr[:, c, :], start=(c == 0), stop=(c == 1))
            mm.then_inc(logit_in_psum, 1)
            bank7.freed_by(logit_ready, 1)
            yield from skip(3)

        def prologue_scalar(act, b, first):
            steps = Steps(act, act_steps)
            yield
            yield from norm.scalar(act, steps)
            act.wait_ge(logit_ready, 1)
            act.activation(odds[:, :, :], logit[:, :, :], ACT.Exp, scale=-1.0).then_inc(odds_ready, 1)
            yield from skip(3)

        def prologue_gpsimd(pool, b, first):
            yield from skip(SIDE)

        def prologue_vector(dve, b, first):
            steps = Steps(dve, side_dve_steps)

            def do(instruction):
                steps.mark(instruction)
                steps.settle()

            yield
            yield from norm.vector(dve, steps)
            dve.wait_ge(logit_in_psum, 1)
            dve.tensor_tensor(logit[:, :, :], ps[:, 7, 0:T * NE].rearrange("p (t n) -> p t n", t=T),
                              br[:, :].rearrange("p (o n) -> p o n", o=1).to_broadcast([P, T, NE]), ALU.add)\
                .then_inc(logit_ready, 1)
            dve.wait_ge(residual_loaded, 16)
            do(dve.tensor_tensor(residual[:, :, :], residual[:, :, :], y[:, :, :], ALU.add))
            yield
            dve.wait_ge(odds_ready, 1)
            do(dve.tensor_scalar(odds[:, :, :], odds[:, :, :], 1.0, None, ALU.add))
            do(dve.reciprocal(prob[:, :, 0:NE], odds[:, :, :]))
            for t in range(T):
                steps.mark(dve.max(top[:, t, :], prob[:, t, :]))
            steps.settle()
            for t in range(T):
                steps.mark(dve.max_index(where[:, t, :], top[:, t, :], prob[:, t, :]))
            do(dve.tensor_tensor(both[:, :], top[:, :, 0], top[:, :, 1], ALU.add))
            do(dve.reciprocal(both[:, :], both[:, :]))
            do(dve.tensor_copy(wheref[:, :, :], where[:, :, 0:2]))
            yield
            for t in range(T):
                steps.mark(dve.tensor_scalar(picked[:, t, :], number[:, :], wheref[:, t, 0:1], None, ALU.is_equal))
            steps.settle()
            for t in range(T):
                steps.mark(dve.scalar_tensor_tensor(out=picked[:, t, :], in0=number[:, :],
                                                    scalar=wheref[:, t, 1:2], in1=picked[:, t, :],
                                                    op0=ALU.is_equal, op1=ALU.add))
            steps.settle()
            for t in range(T):
                steps.mark(dve.scalar_tensor_tensor(out=share_next[:, t, :], in0=prob[:, t, :],
                                                    scalar=both[:, t:t + 1], in1=picked[:, t, :],
                                                    op0=ALU.mult, op1=ALU.mult))
            steps.settle()
            do(dve.tensor_scalar(share_next[:, :, :], share_next[:, :, :], 0.5, None, ALU.mult))
            yield

        def sync(sp, b, side):
            side = side()
            next(side, None)
            store_x(sp, down_added, T * (NE + 1), stored, total, x_dst, b)
            exhaust(side)

        def gpsimd(pool, b, side):
            pool.tensor_copy(share[:, :, :], share_next[:, :, :]).then_inc(share_kept, 1)
            pool.tensor_copy(total[:, :, :], residual[:, :, :]).then_inc(total_kept, 1)

        def tensor(pe, b, side):
            side = side()
            bank7.freed = None
            pe.wait_ge(xnT_kept, 1)
            downs = 0
            for place, item in enumerate(order):
                if place in side_at:
                    next(side, None)
                e = item[1]
                if item[0] == "up":
                    f = item[2]
                    i = 2 * e + f
                    if i >= 2:
                        pe.wait_ge(mid_ready, i - 1)
                    for bank, wt in ((2 * (i % 2), wg), (2 * (i % 2) + 1, wu)):
                        for c in range(FT):
                            mm = pe.matmul(ps[:, bank, :], wt[:, e, c, f * P:(f + 1) * P], xnT[:, c, :],
                                           start=(c == 0), stop=(c == 1))
                    mm.then_inc(up_in_psum, 1)
                    continue
                pe.wait_ge(mid_ready, 2 * e + 2)
                for t in range(T):
                    if downs >= 3:
                        pe.wait_ge(down_added, downs - 2)
                    for c in range(FT):
                        mm = pe.matmul(ps[:, down_bank(e, t), 0:D], mid[:, e % 2, c, t * P:(t + 1) * P],
                                       wd[:, e, c, :], start=(c == 0), stop=(c == 1))
                    mm.then_inc(down_in_psum, 1)
                    downs += 1
            exhaust(side)

        def scalar(act, b, side):
            side = side()
            act.activation(xnT[:, :, :], norm.xnT[:, :, 1:], ACT.Copy).then_inc(xnT_kept, 1)
            for place, item in enumerate(order):
                if place in side_at:
                    next(side, None)
                if item[0] == "up":
                    i = 2 * item[1] + item[2]
                    act.wait_ge(up_in_psum, i + 1)
                    if i >= 2:
                        act.wait_ge(gated_ready, i - 1)
                    act.activation(gate[:, i % 2, :], ps[:, 2 * (i % 2), :], ACT.Tanh, scale=0.5)\
                        .then_inc(gate_ready, 1)
            exhaust(side)

        def vector(dve, b, side):
            side = side()
            dve.wait_ge(share_kept, 1)
            dve.wait_ge(total_kept, 1)
            for place, item in enumerate(order):
                if place in side_at:
                    next(side, None)
                e = item[1]
                if item[0] == "up":
                    i = 2 * e + item[2]
                    g, u = 2 * (i % 2), 2 * (i % 2) + 1
                    dve.wait_ge(gate_ready, i + 1)
                    if i >= 2:
                        dve.wait_ge(mid_ready, i - 1)
                    dve.scalar_tensor_tensor(out=gated[:, i % 2, :], in0=gate[:, i % 2, :], scalar=1.0,
                                             in1=ps[:, g, :], op0=ALU.add, op1=ALU.mult).then_inc(gated_ready, 1)
                    dve.wait_ge(gated_ready, i + 1)
                    if e >= 2:
                        dve.wait_ge(down_in_psum, T * (e - 1))
                    dve.tensor_tensor(mid[:, e % 2, item[2], :], gated[:, i % 2, :], ps[:, u, :], ALU.mult)\
                        .then_inc(mid_ready, 1)
                    continue
                for t in range(T):
                    dve.wait_ge(down_in_psum, T * e + t + 1)
                    if e >= 1:
                        dve.wait_ge(down_added, T * (e - 1) + t + 1)
                    dve.scalar_tensor_tensor(out=total[:, t, :], in0=ps[:, down_bank(e, t), 0:D],
                                             scalar=share[:, t, e - 1:e] if e else 0.5, in1=total[:, t, :],
                                             op0=ALU.mult, op1=ALU.add).then_inc(down_added, 1)

            exhaust(side)

        pipelined_loop(nc, st,
                       {"sync": prologue_sync, "tensor": prologue_tensor, "scalar": prologue_scalar,
                        "vector": prologue_vector, "gpsimd": prologue_gpsimd},
                       {"sync": sync, "tensor": tensor, "scalar": scalar, "vector": vector, "gpsimd": gpsimd})



def decoder(nc, w, out):
    def scratch(name, shape, dt):
        return nc.dram_tensor(name, shape, dt, kind="Internal").ap()

    x = [w["x"]] + [scratch(f"x_after_{i}", (NB, S, D), F32) for i in range(1, 7)] + [out]
    kscratch = scratch("k_levels", (NB, H, HD, NSLOT, CTX), BF16)
    qscratch = scratch("q_levels", (NB, H, HD, NSLOT, S), BF16)
    tscratch = scratch("t_levels", (NB, 2, GH, NSLOT, S), BF16)
    latent_attention(nc, w, x[0], x[1], kscratch, qscratch)
    cross_attention(nc, w, x[1], x[2], kscratch, qscratch)
    channel_mix(nc, w, x[2], x[3])
    mixed_attention(nc, w, x[3], x[4], kscratch, qscratch, tscratch)
    linear_attention(nc, w, x[4], x[5])
    rotary_latent_attention(nc, w, x[5], x[6], kscratch, qscratch)
    experts(nc, w, x[6], x[5], x[7])


def kernel(**inputs):
    import ml_dtypes as _ml
    import numpy as _np
    import concourse.bacc as _bacc
    from concourse import mybir as _mybir
    from concourse.bass_utils import run_bass_kernel_spmd as _run

    f32 = _np.float32
    src = {name: _np.asarray(value) for name, value in inputs.items()}

    def columns(v):
        return v.reshape(FT, P).T

    a = {"x": src["x"], "mask": src["mask_BxSxS2_ff0"], "ctxT": src["ctx_1024"].transpose(0, 2, 1)}

    i = _np.arange(P)
    causal = _np.where(i[None, :] > i[:, None], NEG, 0.0)
    a["identf"], a["identb"] = _np.eye(P, dtype=f32), _np.eye(P).astype(_ml.bfloat16)
    a["tri"], a["triT"], a["trif"] = causal.astype(_ml.bfloat16), causal.T.astype(_ml.bfloat16), causal.astype(f32)
    a["blocks"] = _np.kron(_np.eye(P // HD), _np.ones((HD, HD))).astype(f32)
    a["numbers"] = _np.arange(NE + 1, dtype=f32)

    def rotary_tables(width):
        steps = f32(1.0) / _np.power(f32(10000.0), _np.arange(0, width, 2, dtype=f32) / f32(width))
        angles = _np.outer(_np.arange(S, dtype=f32), steps.astype(f32)).astype(f32)
        return _np.cos(angles).T, _np.sin(angles).T

    c, s = rotary_tables(HD)
    a["rot_cos"] = _np.tile(_np.concatenate([c, c]), (P // HD, 1))
    a["rot_sin"] = _np.tile(_np.concatenate([s, -s]), (P // HD, 1))
    c, s = rotary_tables(HD // 2)
    a["mla_cos"] = _np.tile(_np.concatenate([_np.ones((HD // 2, S), f32), c, c]), (P // HD, 1))
    a["mla_sin"] = _np.tile(_np.concatenate([_np.zeros((HD // 2, S), f32), -s, s]), (P // HD, 1))

    for name in ("L0_attn_W_DKV", "L0_attn_W_UK", "L0_attn_W_UV", "L0_attn_W_UQ", "L0_attn_W_O",
                 "L0_xattn_bv", "L0_xattn_bo", "L1_xattn_bk", "L1_xattn_bv", "L1_xattn_bo", "L1_attn_proj_b",
                 "L1_ffn_W_kvd", "L1_ffn_W_qd", "L1_ffn_W_vu", "L1_ffn_W_o", "L1_ffn_Wg_s", "L1_ffn_Wu_s",
                 "L1_ffn_Wd_s", "L1_ffn_Wg_r", "L1_ffn_Wu_r", "L1_ffn_Wd_r", "L1_ffn_W_router",
                 "L1_ffn_routing_bias"):
        a[name] = src[name]
    for name in ("L0_xattn_Wq", "L0_xattn_Wk", "L0_xattn_Wv", "L0_xattn_Wo", "L1_xattn_Wq", "L1_xattn_Wk",
                 "L1_xattn_Wv", "L1_xattn_Wo", "L0_ffn_W_r", "L0_ffn_W_k", "L0_ffn_W_v"):
        a[name] = src[name].T
    for name in ("L0_xattn_bq", "L0_xattn_bk", "L1_xattn_bq", "L0_ffn_mu_r", "L0_ffn_mu_k", "L1_ffn_w_ln1",
                 "L1_ffn_w_ln2"):
        a[name] = columns(src[name])

    order = [*range(6), *range(10, 16), *range(6, 10)]
    own = _np.concatenate([HD * h + _np.arange(HD) for h in order])
    partner = _np.concatenate([HD * h + (_np.arange(HD) + HD // 2) % HD for h in order])
    q, k, v = _np.split(src["L1_attn_qkv_w"], 3)
    a["mix_wq"], a["mix_wk"], a["mix_wv"] = q[own].T, k[own].T, v[own].T
    a["mix_wq_partner"], a["mix_wk_partner"] = q[partner].T, k[partner].T
    a["mix_wo"] = src["L1_attn_proj_w"].T[own]
    a["curvature"] = src["L1_attn_curvature"].reshape(GH)
    a["curvature_feature"] = _np.tile(_np.repeat(a["curvature"], HD), P // (GH * HD)).reshape(P, 1)

    def head_columns(plain, rotary, swapped=False):
        n, half = (plain if rotary is None else rotary).shape[0], HD // 2
        cols = _np.zeros((n, H, HD), f32)
        if plain is not None:
            cols[:, :, 0:half] = plain.reshape(n, H, half)
        if rotary is not None:
            order = (_np.arange(half) + half // 2) % half if swapped else _np.arange(half)
            cols[:, :, half:HD] = rotary.reshape(n, H, half)[:, :, order]
        return cols.reshape(n, D)

    a["mla_wku"] = head_columns(src["L1_ffn_W_ku"], None)
    a["mla_wkr"] = head_columns(None, src["L1_ffn_W_ropek"])
    a["mla_wkr_partner"] = head_columns(None, src["L1_ffn_W_ropek"], swapped=True)
    a["mla_wq"] = head_columns(src["L1_ffn_W_qu"], src["L1_ffn_W_ropeq"])
    a["mla_wq_partner"] = head_columns(None, src["L1_ffn_W_ropeq"], swapped=True)

    nc = _bacc.Bacc("TRN2", target_bir_lowering=False, num_devices=1)
    arrays, w = {}, {}
    for name, value in a.items():
        arrays[f"in_{name}"] = value = _np.ascontiguousarray(value)
        w[name] = nc.dram_tensor(f"in_{name}", value.shape, _mybir.dt.from_np(value.dtype),
                                 kind="ExternalInput").ap()
    out = nc.dram_tensor("out_x", (NB, S, D), F32, kind="ExternalOutput").ap()
    decoder(nc, w, out)
    r = _run(nc, [arrays], core_ids=[0])
    return r.results[0]["out_x"]
```
